# Optimizing a Trainium2 kernel written in Bass

```python
import numpy as np
import jax
import jax.numpy as jnp

def _softmax(x, axis=-1):
    return jax.nn.softmax(x, axis=axis)

def _gelu(x):
    return jax.nn.gelu(x, approximate=True)

def _silu(x):
    return jax.nn.silu(x)

def _sigmoid(x):
    return jax.nn.sigmoid(x)

def _layernorm(x, axis=-1, eps=1e-05):
    m = jnp.mean(x, axis=axis, keepdims=True)
    v = jnp.var(x, axis=axis, keepdims=True)
    return (x - m) / jnp.sqrt(v + eps)

def _scatter_add(tgt, idx, src, axis=0):
    return tgt.at[idx].add(src)

def _segment_sum(src, seg, n):
    return jax.ops.segment_sum(src, seg, n)
kernel_name = 'mk_flamingo_gated_d2_seqx_r4_a16469'

def setup_inputs(seed: int=0):
    np.random.seed(seed)
    _w = jnp.asarray

    def _rec_inputs():
        import jax
        import jax.numpy as jnp
        _rk = jax.random.key(seed)
        x = -0.0002928 + 1 * jax.random.normal(jax.random.fold_in(_rk, 1), (4, 1024, 256), jnp.float32)
        _lenS = 1024 - jax.random.randint(jax.random.fold_in(_rk, 7), (4,), 0, max(1, 1024 // 4) + 1, jnp.int32)
        _lenS2 = 64 - jax.random.randint(jax.random.fold_in(_rk, 8), (4,), 0, max(1, 64 // 4) + 1, jnp.int32)
        _ctx_1024P = jax.random.normal(jax.random.fold_in(_rk, 11), (4, 16, 256), jnp.float32)
        _ctx_1024c = jax.random.dirichlet(jax.random.fold_in(_rk, 511), 0.3 * jnp.ones((16,), jnp.float32), (4, 64))
        _ctx_1024t = jnp.einsum('bsk,bkd->bsd', _ctx_1024c, _ctx_1024P)
        _ctx_1024t = _ctx_1024t * jax.lax.rsqrt(jnp.mean(jnp.square(_ctx_1024t)) + 1e-12) * 0.953939
        ctx_1024 = -0.000292821 + 1.00034 * (_ctx_1024t + 0.3 * jax.random.normal(jax.random.fold_in(_rk, 611), (4, 64, 256), jnp.float32))
        _g = jax.random.normal(jax.random.fold_in(_rk, 9001), (2, 2), jnp.float32)
        _g = jnp.sign(_g) * jnp.maximum(jnp.abs(_g), 1.0) + (_g == 0) * 1.0
        g_xattn = _g[0]
        g_ffn = _g[1]
        return (x, ctx_1024, g_xattn, g_ffn)
    x, ctx_1024, g_xattn, g_ffn = _rec_inputs()

    def _L0_xattn_setup():
        import jax, jax.numpy as jnp
        import numpy as np
        HIDDEN = 256
        HEADS = 16
        HEAD_DIM = HIDDEN // HEADS
        SCALE = 1.0 / np.sqrt(HEAD_DIM).astype(np.float32)
        key = jax.random.key(seed)
        ks = jax.random.split(key, 8)
        b, t = (2, 512)
        x = jax.random.normal(ks[0], (b, t, HIDDEN), dtype=jnp.float32)
        context = x
        s = 0.02
        Wq = jax.random.normal(ks[1], (HIDDEN, HIDDEN), dtype=jnp.float32) * s
        Wk = jax.random.normal(ks[2], (HIDDEN, HIDDEN), dtype=jnp.float32) * s
        Wv = jax.random.normal(ks[3], (HIDDEN, HIDDEN), dtype=jnp.float32) * s
        Wo = jax.random.normal(ks[4], (HIDDEN, HIDDEN), dtype=jnp.float32) * s
        bo = jnp.zeros((HIDDEN,), dtype=jnp.float32)
        return {'x': x, 'context': context, 'Wq': Wq, 'Wk': Wk, 'Wv': Wv, 'Wo': Wo, 'bo': bo}
    _L0_xattn_all = _L0_xattn_setup()
    _L0_xattn_in = {k: v for k, v in _L0_xattn_all.items() if k in ('Wq', 'Wk', 'Wv', 'Wo', 'bo')}
    del _L0_xattn_all

    def _L0_ffn_setup():
        import jax, jax.numpy as jnp
        import numpy as np
        from functools import partial
        DIM = 256
        LIGHT_HID = 128
        HEAVY_HID = 1024
        NUM_HEAVY = 256
        N_ITERS = 50
        K_ROUTE = 8.0
        EPS = 0.1

        def rms_norm(x, gamma):
            norm = jnp.linalg.norm(x, axis=-1, keepdims=True)
            normed = x / jnp.maximum(norm, 1e-12)
            return normed * x.shape[-1] ** 0.5 * gamma

        def ffn(x, gamma, w1, b1, w2, b2):
            h = rms_norm(x, gamma)
            h = jax.nn.gelu(h @ w1 + b1, approximate=False)
            return h @ w2 + b2

        def coor_descent_route(x, routing_token, num_tokens):
            s = jnp.einsum('bnd,d->bn', x, routing_token)
            constant = EPS * jnp.log(jnp.asarray(K_ROUTE, dtype=s.dtype))
            b0 = -jax.nn.relu(s)
            a0 = jnp.zeros((s.shape[0], 1), dtype=s.dtype)

            def step(carry, _):
                a_prev, b = carry
                a = constant - EPS * jax.nn.logsumexp((s + b) / EPS, axis=-1, keepdims=True)
                b = -jax.nn.relu(s + a)
                return ((a, b), None)
            (a, b), _ = jax.lax.scan(step, (a0, b0), None, length=N_ITERS)
            scores = jnp.exp((s + a + b) / EPS)
            sel_scores, sel_idx = jax.lax.top_k(scores, num_tokens)
            sel_scores = sel_scores + jax.lax.stop_gradient(1.0 - sel_scores)
            return (sel_scores, sel_idx)
        key = jax.random.key(seed)
        ks = jax.random.split(key, 12)

        def lin(k, fan_in, fan_out):
            lim = 1.0 / np.sqrt(fan_in)
            kw, kb = jax.random.split(k)
            w = jax.random.uniform(kw, (fan_in, fan_out), jnp.float32, -lim, lim)
            b = jax.random.uniform(kb, (fan_out,), jnp.float32, -lim, lim)
            return (w, b)
        x = jax.random.normal(ks[0], (4, 2048, DIM), jnp.float32)
        routing_token = jax.random.normal(ks[1], (DIM,), jnp.float32)
        gamma_light = jnp.ones((DIM,), jnp.float32)
        w1_l, b1_l = lin(ks[2], DIM, LIGHT_HID)
        w2_l, b2_l = lin(ks[3], LIGHT_HID, DIM)
        gamma_heavy = jnp.ones((DIM,), jnp.float32)
        w1_h, b1_h = lin(ks[4], DIM, HEAVY_HID)
        w2_h, b2_h = lin(ks[5], HEAVY_HID, DIM)
        return dict(x=x, routing_token=routing_token, gamma_light=gamma_light, w1_light=w1_l, b1_light=b1_l, w2_light=w2_l, b2_light=b2_l, gamma_heavy=gamma_heavy, w1_heavy=w1_h, b1_heavy=b1_h, w2_heavy=w2_h, b2_heavy=b2_h)
    _L0_ffn_all = _L0_ffn_setup()
    _L0_ffn_in = {k: v for k, v in _L0_ffn_all.items() if k in ('routing_token', 'gamma_light', 'w1_light', 'b1_light', 'w2_light', 'b2_light', 'gamma_heavy', 'w1_heavy', 'b1_heavy', 'w2_heavy', 'b2_heavy')}
    del _L0_ffn_all

    def _L1_xattn_setup():
        import jax, jax.numpy as jnp
        import numpy as np
        D_MODEL = 256
        NUM_HEADS = 16
        D_K = D_MODEL // NUM_HEADS
        key = jax.random.key(seed)
        ks = jax.random.split(key, 11)
        B, L = (4, 512)
        s = 0.02
        return {'query': jax.random.normal(ks[0], (B, L, D_MODEL), jnp.float32), 'key': jax.random.normal(ks[1], (B, L, D_MODEL), jnp.float32), 'value': jax.random.normal(ks[2], (B, L, D_MODEL), jnp.float32), 'Wq': jax.random.normal(ks[3], (D_MODEL, D_MODEL), jnp.float32) * s, 'bq': jnp.zeros((D_MODEL,), jnp.float32), 'Wk': jax.random.normal(ks[4], (D_MODEL, D_MODEL), jnp.float32) * s, 'bk': jnp.zeros((D_MODEL,), jnp.float32), 'Wv': jax.random.normal(ks[5], (D_MODEL, D_MODEL), jnp.float32) * s, 'bv': jnp.zeros((D_MODEL,), jnp.float32), 'Wo': jax.random.normal(ks[6], (D_MODEL, D_MODEL), jnp.float32) * s, 'bo': jnp.zeros((D_MODEL,), jnp.float32)}
    _L1_xattn_all = _L1_xattn_setup()
    _L1_xattn_in = {k: v for k, v in _L1_xattn_all.items() if k in ('Wq', 'bq', 'Wk', 'bk', 'Wv', 'bv', 'Wo', 'bo')}
    del _L1_xattn_all

    def _L1_ffn_setup():
        import jax, jax.numpy as jnp
        import numpy as np
        B, L, C1, C2, K, K_IN = (4, 256, 256, 256, 32, 32)
        BN_EPS = 1e-05

        def _gated_bottleneck(x2d, conv_w, conv_b, gamma, beta, lin_w, lin_b):
            n = x2d.shape[0]
            g = conv_w.shape[0]
            xc = jnp.einsum('ngf,gf->ng', x2d.reshape(n, g, 4), conv_w) + conv_b
            mean = jnp.mean(xc, axis=0)
            var = jnp.mean((xc - mean) ** 2, axis=0)
            xn = (xc - mean) * jax.lax.rsqrt(var + BN_EPS) * gamma + beta
            xa = jax.nn.gelu(xn, approximate=False)
            return xa @ lin_w.T + lin_b
        key = jax.random.key(seed)
        ks = jax.random.split(key, 8)
        g = C1 // 4
        w_std = (2.0 / C2) ** 0.5
        lin_std = (1.0 / g) ** 0.5
        return {'x': jax.random.normal(ks[0], (B, L, C1), jnp.float32), 'weight': jax.random.normal(ks[1], (C1, C2), jnp.float32) * w_std, 'bias': jnp.zeros((C2,), jnp.float32), 'so_conv_w': jax.random.normal(ks[2], (g, 4), jnp.float32) * 0.5, 'so_conv_b': jnp.zeros((g,), jnp.float32), 'so_gamma': jnp.ones((g,), jnp.float32), 'so_beta': jnp.zeros((g,), jnp.float32), 'so_lin_w': jax.random.normal(ks[3], (C2, g), jnp.float32) * lin_std, 'so_lin_b': jnp.zeros((C2,), jnp.float32), 'si_conv_w': jax.random.normal(ks[4], (g, 4), jnp.float32) * 0.5, 'si_conv_b': jnp.zeros((g,), jnp.float32), 'si_gamma': jnp.ones((g,), jnp.float32), 'si_beta': jnp.zeros((g,), jnp.float32), 'si_lin_w': jax.random.normal(ks[5], (C1, g), jnp.float32) * lin_std, 'si_lin_b': jnp.zeros((C1,), jnp.float32)}
    _L1_ffn_all = _L1_ffn_setup()
    _L1_ffn_in = {k: v for k, v in _L1_ffn_all.items() if k in ('weight', 'bias', 'so_conv_w', 'so_conv_b', 'so_gamma', 'so_beta', 'so_lin_w', 'so_lin_b', 'si_conv_w', 'si_conv_b', 'si_gamma', 'si_beta', 'si_lin_w', 'si_lin_b')}
    del _L1_ffn_all
    return {'x': x, 'ctx_1024': ctx_1024, 'g_xattn': g_xattn, 'g_ffn': g_ffn, 'L0_xattn_Wq': _L0_xattn_in['Wq'], 'L0_xattn_Wk': _L0_xattn_in['Wk'], 'L0_xattn_Wv': _L0_xattn_in['Wv'], 'L0_xattn_Wo': _L0_xattn_in['Wo'], 'L0_xattn_bo': _L0_xattn_in['bo'], 'L0_ffn_routing_token': _L0_ffn_in['routing_token'], 'L0_ffn_gamma_light': _L0_ffn_in['gamma_light'], 'L0_ffn_w1_light': _L0_ffn_in['w1_light'], 'L0_ffn_b1_light': _L0_ffn_in['b1_light'], 'L0_ffn_w2_light': _L0_ffn_in['w2_light'], 'L0_ffn_b2_light': _L0_ffn_in['b2_light'], 'L0_ffn_gamma_heavy': _L0_ffn_in['gamma_heavy'], 'L0_ffn_w1_heavy': _L0_ffn_in['w1_heavy'], 'L0_ffn_b1_heavy': _L0_ffn_in['b1_heavy'], 'L0_ffn_w2_heavy': _L0_ffn_in['w2_heavy'], 'L0_ffn_b2_heavy': _L0_ffn_in['b2_heavy'], 'L1_xattn_Wq': _L1_xattn_in['Wq'], 'L1_xattn_bq': _L1_xattn_in['bq'], 'L1_xattn_Wk': _L1_xattn_in['Wk'], 'L1_xattn_bk': _L1_xattn_in['bk'], 'L1_xattn_Wv': _L1_xattn_in['Wv'], 'L1_xattn_bv': _L1_xattn_in['bv'], 'L1_xattn_Wo': _L1_xattn_in['Wo'], 'L1_xattn_bo': _L1_xattn_in['bo'], 'L1_ffn_weight': _L1_ffn_in['weight'], 'L1_ffn_bias': _L1_ffn_in['bias'], 'L1_ffn_so_conv_w': _L1_ffn_in['so_conv_w'], 'L1_ffn_so_conv_b': _L1_ffn_in['so_conv_b'], 'L1_ffn_so_gamma': _L1_ffn_in['so_gamma'], 'L1_ffn_so_beta': _L1_ffn_in['so_beta'], 'L1_ffn_so_lin_w': _L1_ffn_in['so_lin_w'], 'L1_ffn_so_lin_b': _L1_ffn_in['so_lin_b'], 'L1_ffn_si_conv_w': _L1_ffn_in['si_conv_w'], 'L1_ffn_si_conv_b': _L1_ffn_in['si_conv_b'], 'L1_ffn_si_gamma': _L1_ffn_in['si_gamma'], 'L1_ffn_si_beta': _L1_ffn_in['si_beta'], 'L1_ffn_si_lin_w': _L1_ffn_in['si_lin_w'], 'L1_ffn_si_lin_b': _L1_ffn_in['si_lin_b']}

def reference(x, ctx_1024, g_xattn, g_ffn, L0_xattn_Wq, L0_xattn_Wk, L0_xattn_Wv, L0_xattn_Wo, L0_xattn_bo, L0_ffn_routing_token, L0_ffn_gamma_light, L0_ffn_w1_light, L0_ffn_b1_light, L0_ffn_w2_light, L0_ffn_b2_light, L0_ffn_gamma_heavy, L0_ffn_w1_heavy, L0_ffn_b1_heavy, L0_ffn_w2_heavy, L0_ffn_b2_heavy, L1_xattn_Wq, L1_xattn_bq, L1_xattn_Wk, L1_xattn_bk, L1_xattn_Wv, L1_xattn_bv, L1_xattn_Wo, L1_xattn_bo, L1_ffn_weight, L1_ffn_bias, L1_ffn_so_conv_w, L1_ffn_so_conv_b, L1_ffn_so_gamma, L1_ffn_so_beta, L1_ffn_so_lin_w, L1_ffn_so_lin_b, L1_ffn_si_conv_w, L1_ffn_si_conv_b, L1_ffn_si_gamma, L1_ffn_si_beta, L1_ffn_si_lin_w, L1_ffn_si_lin_b):
    import jax
    import jax.numpy as jnp

    def _L0_xattn_ref(x, context, Wq, Wk, Wv, Wo, bo):
        import jax, jax.numpy as jnp
        import numpy as np
        HIDDEN = 256
        HEADS = 16
        HEAD_DIM = HIDDEN // HEADS
        SCALE = 1.0 / np.sqrt(HEAD_DIM).astype(np.float32)
        b, t, c = x.shape
        kv_t = context.shape[1]
        q = x @ Wq.T
        k = context @ Wk.T
        v = context @ Wv.T
        q = q.reshape(b, t, HEADS, HEAD_DIM).transpose(0, 2, 1, 3)
        k = k.reshape(b, kv_t, HEADS, HEAD_DIM).transpose(0, 2, 1, 3)
        v = v.reshape(b, kv_t, HEADS, HEAD_DIM).transpose(0, 2, 1, 3)
        scores = jnp.einsum('bhqd,bhkd->bhqk', q, k) * SCALE
        causal = jnp.tril(jnp.ones((t, kv_t), dtype=bool))
        scores = jnp.where(causal[None, None, :, :], scores, -jnp.inf)
        probs = jax.nn.softmax(scores, axis=-1)
        y = jnp.einsum('bhqk,bhkd->bhqd', probs, v)
        y = y.transpose(0, 2, 1, 3).reshape(b, t, c)
        return y @ Wo.T + bo

    def _L0_ffn_ref(x, routing_token, gamma_light, w1_light, b1_light, w2_light, b2_light, gamma_heavy, w1_heavy, b1_heavy, w2_heavy, b2_heavy):
        import jax, jax.numpy as jnp
        import numpy as np
        from functools import partial
        DIM = 256
        LIGHT_HID = 128
        HEAVY_HID = 1024
        NUM_HEAVY = 256
        N_ITERS = 50
        K_ROUTE = 8.0
        EPS = 0.1

        def rms_norm(x, gamma):
            norm = jnp.linalg.norm(x, axis=-1, keepdims=True)
            normed = x / jnp.maximum(norm, 1e-12)
            return normed * x.shape[-1] ** 0.5 * gamma

        def ffn(x, gamma, w1, b1, w2, b2):
            h = rms_norm(x, gamma)
            h = jax.nn.gelu(h @ w1 + b1, approximate=False)
            return h @ w2 + b2

        def coor_descent_route(x, routing_token, num_tokens):
            s = jnp.einsum('bnd,d->bn', x, routing_token)
            constant = EPS * jnp.log(jnp.asarray(K_ROUTE, dtype=s.dtype))
            b0 = -jax.nn.relu(s)
            a0 = jnp.zeros((s.shape[0], 1), dtype=s.dtype)

            def step(carry, _):
                a_prev, b = carry
                a = constant - EPS * jax.nn.logsumexp((s + b) / EPS, axis=-1, keepdims=True)
                b = -jax.nn.relu(s + a)
                return ((a, b), None)
            (a, b), _ = jax.lax.scan(step, (a0, b0), None, length=N_ITERS)
            scores = jnp.exp((s + a + b) / EPS)
            sel_scores, sel_idx = jax.lax.top_k(scores, num_tokens)
            sel_scores = sel_scores + jax.lax.stop_gradient(1.0 - sel_scores)
            return (sel_scores, sel_idx)
        bsz = x.shape[0]
        light_out = ffn(x, gamma_light, w1_light, b1_light, w2_light, b2_light)
        sel_scores, sel_idx = coor_descent_route(x, routing_token, NUM_HEAVY)
        batch_range = jnp.arange(bsz)[:, None]
        routed = x[batch_range, sel_idx]
        routed_out = ffn(routed, gamma_heavy, w1_heavy, b1_heavy, w2_heavy, b2_heavy)
        routed_out = routed_out * sel_scores[..., None]
        heavy_out = jnp.zeros_like(x).at[batch_range, sel_idx].set(routed_out)
        return light_out + heavy_out

    def _L1_xattn_ref(query, key, value, Wq, bq, Wk, bk, Wv, bv, Wo, bo):
        import jax, jax.numpy as jnp
        import numpy as np
        D_MODEL = 256
        NUM_HEADS = 16
        D_K = D_MODEL // NUM_HEADS
        B, Lq, _ = query.shape
        Lk = key.shape[1]
        q = (query @ Wq.T + bq).reshape(B, Lq, NUM_HEADS, D_K).transpose(0, 2, 1, 3)
        k = (key @ Wk.T + bk).reshape(B, Lk, NUM_HEADS, D_K).transpose(0, 2, 1, 3)
        v = (value @ Wv.T + bv).reshape(B, Lk, NUM_HEADS, D_K).transpose(0, 2, 1, 3)
        scores = jnp.einsum('bhqd,bhkd->bhqk', q, k) / jnp.sqrt(jnp.float32(D_K))
        attn = jax.nn.softmax(scores, axis=-1)
        out = jnp.einsum('bhqk,bhkd->bhqd', attn, v)
        out = out.transpose(0, 2, 1, 3).reshape(B, Lq, D_MODEL)
        return out @ Wo.T + bo

    def _L1_ffn_ref(x, weight, bias, so_conv_w, so_conv_b, so_gamma, so_beta, so_lin_w, so_lin_b, si_conv_w, si_conv_b, si_gamma, si_beta, si_lin_w, si_lin_b):
        import jax, jax.numpy as jnp
        import numpy as np
        B, L, C1, C2, K, K_IN = (4, 256, 256, 256, 32, 32)
        BN_EPS = 1e-05

        def _gated_bottleneck(x2d, conv_w, conv_b, gamma, beta, lin_w, lin_b):
            n = x2d.shape[0]
            g = conv_w.shape[0]
            xc = jnp.einsum('ngf,gf->ng', x2d.reshape(n, g, 4), conv_w) + conv_b
            mean = jnp.mean(xc, axis=0)
            var = jnp.mean((xc - mean) ** 2, axis=0)
            xn = (xc - mean) * jax.lax.rsqrt(var + BN_EPS) * gamma + beta
            xa = jax.nn.gelu(xn, approximate=False)
            return xa @ lin_w.T + lin_b
        b, l, c1 = x.shape
        c2 = weight.shape[1]
        x2d = x.reshape(b * l, c1)
        bi = jnp.arange(b)[:, None, None]
        li = jnp.arange(l)[None, :, None]
        score_out = jax.nn.softmax(_gated_bottleneck(x2d, so_conv_w, so_conv_b, so_gamma, so_beta, so_lin_w, so_lin_b).reshape(b, l, c2), axis=-1)
        s_v_out, s_i_out = jax.lax.top_k(score_out, K)
        full = jnp.einsum('blc,co->blo', x, weight)
        out_k = jnp.take_along_axis(full, s_i_out, axis=-1) * s_v_out
        out_branch = jnp.zeros((b, l, c2), x.dtype).at[bi, li, s_i_out].add(out_k)
        score_in = jax.nn.softmax(_gated_bottleneck(x2d, si_conv_w, si_conv_b, si_gamma, si_beta, si_lin_w, si_lin_b).reshape(b, l, c1), axis=-1)
        s_v_in, s_i_in = jax.lax.top_k(score_in, K_IN)
        x_gated = jnp.take_along_axis(x, s_i_in, axis=-1) * s_v_in
        x_sparse = jnp.zeros((b, l, c1), x.dtype).at[bi, li, s_i_in].add(x_gated)
        in_branch = jnp.einsum('blc,co->blo', x_sparse, weight)
        return out_branch + in_branch + bias
    x = x + jnp.tanh(g_xattn[0]) * _L0_xattn_ref(_layernorm(x, axis=-1), ctx_1024, L0_xattn_Wq, L0_xattn_Wk, L0_xattn_Wv, L0_xattn_Wo, L0_xattn_bo)
    x = x + jnp.tanh(g_ffn[0]) * _L0_ffn_ref(_layernorm(x, axis=-1), L0_ffn_routing_token, L0_ffn_gamma_light, L0_ffn_w1_light, L0_ffn_b1_light, L0_ffn_w2_light, L0_ffn_b2_light, L0_ffn_gamma_heavy, L0_ffn_w1_heavy, L0_ffn_b1_heavy, L0_ffn_w2_heavy, L0_ffn_b2_heavy)
    x = x + jnp.tanh(g_xattn[1]) * _L1_xattn_ref(_layernorm(x, axis=-1), ctx_1024, ctx_1024, L1_xattn_Wq, L1_xattn_bq, L1_xattn_Wk, L1_xattn_bk, L1_xattn_Wv, L1_xattn_bv, L1_xattn_Wo, L1_xattn_bo)
    x = x + jnp.tanh(g_ffn[1]) * _L1_ffn_ref(_layernorm(x, axis=-1), L1_ffn_weight, L1_ffn_bias, L1_ffn_so_conv_w, L1_ffn_so_conv_b, L1_ffn_so_gamma, L1_ffn_so_beta, L1_ffn_so_lin_w, L1_ffn_so_lin_b, L1_ffn_si_conv_w, L1_ffn_si_conv_b, L1_ffn_si_gamma, L1_ffn_si_beta, L1_ffn_si_lin_w, L1_ffn_si_lin_b)
    return x

_drawn_inputs = setup_inputs


def setup_inputs(seed=0):
    import zlib

    import numpy as np

    out = dict(_drawn_inputs(seed))
    spreads = {'g_ffn': (-1.0, 0.6),
     'L0_xattn_bo': (0.0, 0.1),
     'L0_ffn_gamma_light': (1.0, 0.2),
     'L0_ffn_gamma_heavy': (1.0, 0.6),
     'L1_xattn_bq': (0.0, 0.8),
     'L1_xattn_bk': (0.0, 0.8),
     'L1_xattn_bv': (0.0, 0.282),
     'L1_xattn_bo': (0.0, 0.1),
     'L1_ffn_bias': (0.0, 0.1),
     'L1_ffn_so_conv_b': (0.0, 0.8),
     'L1_ffn_so_gamma': (1.0, 0.6),
     'L1_ffn_so_beta': (0.0, 0.8),
     'L1_ffn_so_lin_b': (0.0, 0.8),
     'L1_ffn_si_conv_b': (0.0, 0.8),
     'L1_ffn_si_gamma': (1.0, 0.6),
     'L1_ffn_si_beta': (0.0, 0.8),
     'L1_ffn_si_lin_b': (0.0, 0.8)}
    factors = {'L0_xattn_Wq': 8.0,
     'L0_xattn_Wk': 8.0,
     'L0_ffn_b1_light': 6.083,
     'L0_ffn_b1_heavy': 8.0,
     'L0_ffn_b2_heavy': 8.0,
     'L1_xattn_Wq': 8.0,
     'L1_xattn_Wk': 8.0,
     'L1_ffn_weight': 8.0,
     'L1_ffn_so_conv_w': 8.0,
     'L1_ffn_so_lin_w': 8.0,
     'L1_ffn_si_conv_w': 8.0,
     'L1_ffn_si_lin_w': 8.0}
    for name, (base, spread) in spreads.items():
        noise = np.random.default_rng([zlib.crc32(name.encode()), seed]).standard_normal(out[name].shape)
        drawn = base * np.exp(spread * noise) if base else spread * noise
        out[name] = jnp.asarray(drawn.astype(out[name].dtype))
    for name, factor in factors.items():
        out[name] = (out[name] * factor).astype(out[name].dtype)
    return out
```

```python
import math
from contextlib import ExitStack

import concourse.bass as bass
from concourse import mybir

F32 = mybir.dt.float32
BF16 = mybir.dt.bfloat16
U32 = mybir.dt.uint32
ALU = mybir.AluOpType
ACT = mybir.ActivationFunctionType
AX_X = mybir.AxisListType.X
ds = bass.ds

P = 128
BATCH, TOKENS, DIM = 4, 1024, 256
KEYS, HEADS, HEAD_DIM = 64, 16, 16
KH = DIM // P
TILES = BATCH * TOKENS // P
CHUNK_TILES = 4
CHUNK = CHUNK_TILES * P
CHUNKS = TILES // CHUNK_TILES
PAIRS = HEADS // 2
SCALE = HEAD_DIM ** -0.5
LN_EPS = 1e-5

LIGHT, HEAVY = 128, 1024
ROUTED = 256
ROUTE_ITERS, ROUTE_K, ROUTE_EPS = 50, 8.0, 0.1
TOPK = 32
FOUND = -1e30
LOG_TINY = -87.33654
LOG_SHIFT = 40
GROUPS = DIM // 4
BN_EPS = 1e-5
FIRST = 1


class Chain:

    def __init__(self, eng, sem):
        self.eng, self.sem, self.base, self.k, self.i, self.per = eng, sem, 0, 0, None, 0

    def did(self, ins):
        ins.then_inc(self.sem, 1)
        self.k += 1
        return ins

    def at(self):
        return self.base + self.k if self.i is None else self.i * self.per + (self.base + self.k)

    def settle(self):
        self.eng.wait_ge(self.sem, self.at())

    def enter(self, i, per):
        self.base, self.k, self.i, self.per = self.base + self.k, 0, i, per

    def leave(self, trips):
        assert self.k == self.per, (self.k, self.per)
        self.base, self.k, self.i = self.base + trips * self.per, 0, None


def build(nc, A):
    with ExitStack() as ctx:
        def sb(name, shape, dt=F32):
            return ctx.enter_context(nc.sbuf_tensor(name, shape, dt))

        def sem(name):
            return ctx.enter_context(nc.semaphore(name))

        x = sb("x", [P, TILES, DIM])
        ident = sb("ident", [P, P])
        ident16 = sb("ident16", [P, P], BF16)
        ones16 = sb("ones16", [P, P], BF16)
        head_mask = sb("head_mask", [P, 8, KEYS])
        pair_mask = sb("pair_mask", [P, HEADS, HEAD_DIM])
        neg_sel16 = sb("neg_sel16", [P, PAIRS, P], BF16)
        causal_rows16 = sb("causal_rows16", [P, 512], BF16)
        causal_keys16 = sb("causal_keys16", [P, KEYS], BF16)
        gates = sb("gates", [P, 4])
        ctxT = sb("ctxT", [P, KH, BATCH, 2, KEYS])
        Wq = [sb(f"Wq{l}", [P, KH, DIM]) for l in range(2)]
        Wk = [sb(f"Wk{l}", [P, KH, DIM]) for l in range(2)]
        Wv = [sb(f"Wv{l}", [P, KH, DIM]) for l in range(2)]
        Wo = [sb(f"Wo{l}", [P, KH, DIM]) for l in range(2)]
        qkv_bias = sb("qkv_bias", [P, 4])
        v_bias = sb("v_bias", [P, DIM])
        BO0, BO1, B2_LIGHT, BIAS1, B2_HEAVY, SO_B, SI_B = range(7)
        bias_rows = sb("bias_rows", [7, DIM])
        bias_gates = sb("bias_gates", [4, 1])
        bias_piece = [sb(f"bias_piece{k}", [7, DIM], BF16) for k in range(3)]
        bias3 = sb("bias3", [P, 7, DIM], BF16)
        arena = sb("arena", [P, 14592])

        def at(first, words, pattern=None, **sizes):
            flat = arena[:, first:first + words]
            return flat.rearrange(pattern, **sizes) if pattern else flat

        Q, DEN, PROBS, YT, H, HT, K16, KT, VALL, KD, Q16, VD = 0, 2048, 4096, 6144, 7168, 8192, 9216, 11264, 11776, 12800, 13824, 14336
        qT = [at(Q + i * 1024, 1024, "p (m n) -> p m n", m=KH) for i in range(2)]
        log_den = at(DEN, 1024, "p (m n) -> p m n", m=KH)
        inv_den = at(DEN + 1024, 1024, "p (m n) -> p m n", m=KH)
        probs = at(PROBS, 2048, "p (a n) -> p a n", a=4)
        yT = at(YT, 1024, "p (m n) -> p m n", m=KH)
        h = at(H, 1024, "p (t d) -> p t d", t=CHUNK_TILES)
        hT = at(HT, 1024, "p (m n) -> p m n", m=KH)
        k16 = at(K16, 2048).bitcast(BF16).rearrange("p (b m h k) -> p b m h k", b=BATCH, m=KH, h=8)
        kT = at(KT, 512, "p (m b k) -> p m b k", m=KH, b=BATCH)
        v_all = at(VALL, 1024, "p (b d) -> p b d", b=BATCH)
        k_diag = at(KD, 1024, "p (m h k) -> p m h k", m=KH, h=8)
        q16 = at(Q16, 512).bitcast(BF16).rearrange("p (m n) -> p m n", m=KH)
        v_diag = at(VD, 256, "p (h d) -> p h d", h=HEADS)
        logit_rows = at(Q, 4096, "p (b n) -> p b n", b=BATCH)
        heavy_gT = at(PROBS, 2048, "p (m n) -> p m n", m=HEAVY // P)
        light_gT = at(YT, 512)
        compare_out = at(KD, 1024)
        picked = [at(K16 + i * 514, 514, "p (j d) -> p j d", j=2) for i in range(2)]
        heavy_y = [at(VALL + i * 512, 512, "p (j d) -> p j d", j=2) for i in range(2)]
        pickedT = at(Q16, 512, "p (k n) -> p k n", k=KH)
        row_stats = sb("row_stats", [P, CHUNK_TILES, 6])
        mean_var = sb("mean_var", [P, CHUNK_TILES, 2])
        var_eps = sb("var_eps", [P, CHUNK_TILES])
        minus_half = sb("minus_half", [P, CHUNK_TILES])
        rstd = sb("rstd", [P, CHUNK_TILES])
        max16 = sb("max16", [P, CHUNK_TILES, HEADS], BF16)
        maxT16 = sb("maxT16", [P, CHUNK], BF16)
        w1l, w2l = sb("w1l", [P, KH, LIGHT]), sb("w2l", [P, DIM])
        w1h, w2h = sb("w1h", [P, KH, HEAVY]), sb("w2h", [P, HEAVY // P, DIM])
        ffn0_cols = sb("ffn0_cols", [P, 13])
        token_row = sb("token_row", [P, DIM])
        ROW = DIM + 1
        normed = sb("normed", [P, TILES, ROW])
        big = sb("big", [P, BATCH * TOKENS])
        heavy_rows = [big[:, i * 8 * DIM:(i + 1) * 8 * DIM].rearrange("p (t d) -> p t d", t=8) for i in range(2)]
        route_stats = sb("route_stats", [P, CHUNK_TILES, 6])
        route_mv = sb("route_mv", [P, CHUNK_TILES, 2])
        route_var = sb("route_var", [P, 6, CHUNK_TILES])
        row_scale = sb("row_scale", [P, CHUNK_TILES])
        row_norm = sb("row_norm", [P, TILES])
        raw_dot = sb("raw_dot", [P, CHUNK_TILES])
        dot_out = sb("dot_out", [P, DIM])
        logit = sb("logit", [P, TILES])
        above = sb("above", [P, TILES])
        level = sb("level", [P, BATCH])
        top_logit = sb("top_logit", [P, BATCH])
        minus_a = sb("minus_a", [P, BATCH])
        log_sum = sb("log_sum", [P, BATCH])
        args = sb("args", [P, TILES + BATCH])
        exps = sb("exps", [P, TILES + BATCH])
        capped = sb("capped", [P, TILES])
        part_sum = sb("part_sum", [P, BATCH])
        eighth = sb("eighth", [P, P])
        before16 = sb("before16", [P, P], BF16)
        diag4 = sb("diag4", [4, BATCH])
        col4 = sb("col4", [4, 1])
        ones4 = sb("ones4", [4, P])
        score_of = sb("score_of", [P, TILES])
        pick = sb("pick", [P, 4, TILES])
        flag16 = sb("flag16", [P, TILES], BF16)
        count16 = sb("count16", [P, BATCH], BF16)
        slot_base = sb("slot_base", [P, 2, TILES])
        slot = sb("slot", [P, TILES], U32)
        pick_gate = sb("pick_gate", [P, 2])
        rows_in = [nc.dram_tensor(f"rows_in{b}", (ROUTED, ROW), F32, kind="Internal").ap() for b in range(BATCH)]
        rows_out = [nc.dram_tensor(f"rows_out{b}", (ROUTED, DIM), F32, kind="Internal").ap() for b in range(BATCH)]

        conv_bd = sb("conv_bd", [P, KH, P])
        lin_bd = sb("lin_bd", [P, 2 * DIM])
        gate_w = sb("gate_w", [P, KH, DIM])
        bn_cols = sb("bn_cols", [P, 3])
        groups = big[:, :]
        bn_parts = sb("bn_parts", [P, CHUNKS * 6])
        bn_mv = sb("bn_mv", [P, 2])
        bn_tmp = sb("bn_tmp", [P, 5])
        hs = [at(i * 256, 256) for i in range(2)]
        hsT = [at(512 + i * 256, 256, "p (k n) -> p k n", k=KH) for i in range(2)]
        acts = [at(1024 + i * 128, 128) for i in range(2)]
        work = [at(1280 + i * 512, 512) for i in range(2)]
        expw = at(2304, 512)
        taken = at(2816, 512)
        out_part = at(3328, 256)
        sparse = at(3584, 256)
        sparseT = at(3840, 256, "p (k n) -> p k n", k=KH)
        top8 = sb("top8", [P, 4, 2, 8])
        zeros2 = sb("zeros2", [P, 2])
        minus_top = sb("minus_top", [P, 2])
        exp_sum = sb("exp_sum", [P, 2])
        inv_sum = sb("inv_sum", [P, 2])
        bank = [ctx.enter_context(nc.psum_tensor(f"bank{i}", [P, 512], F32)) for i in range(8)]
        F0, F1, M0, M1, S0, S1, YB, DB = bank
        front = [F0, F1]
        mid = [M0, M1]
        score = [S0, S1]
        out_banks = [YB, DB]
        heavy_banks = [M0, M1, S0, S1]
        CHUNK_ITERS = 6
        ROUTE_BLOCKS = [12, 12, 12, 14]
        assert sum(ROUTE_BLOCKS) == ROUTE_ITERS and len(ROUTE_BLOCKS) == BATCH
        sums_before = [sum(ROUTE_BLOCKS[:n]) + n for n in range(BATCH + 1)]
        maxT_ps = S0[0:HEADS, 0:CHUNK // 2].bitcast(BF16)

        x_in = [sem(f"x_in{i}") for i in range(3)]
        ctx_in, gates_in, consts_in, masks_in = sem("ctx_in"), sem("gates_in"), sem("consts_in"), sem("masks_in")
        attn_w_in = [sem(f"attn_w_in{l}") for l in range(2)]
        bias_in = sem("bias_in")
        gates_ready, set_ready, wo_ready = sem("gates_ready"), sem("set_ready"), sem("wo_ready")
        pieces_ready, bias_ready = sem("pieces_ready"), sem("bias_ready")
        dve_step, pool_step, act_step = sem("dve_step"), sem("pool_step"), sem("act_step")
        top_step = sem("top_step")
        out_done, waits_taken = sem("out_done"), sem("waits_taken")
        names = ("k_ps k_sb k16_ready v_ps v_sb stats rstd_ready h_ready hT_ps hT_sb q_ps q_sb q16_ready "
                 "max_ps max_done maxT_ps maxT_sb s_ps s_exp pv inv_ready y_ready o_ps x_new kv_diag").split()
        ffn0_in, route_in = sem("ffn0_in"), sem("route_in")
        ffn0_ready = sem("ffn0_ready")
        route_stats_ready, scale_ready, logit_ready = sem("route_stats_ready"), sem("scale_ready"), sem("logit_ready")
        rows_ps, rows_sb = sem("rows_ps"), sem("rows_sb")
        cross_in, cross_ps, cross_col, cross_diag, cross_out = (sem(n) for n in ("cross_in", "cross_ps", "cross_col", "cross_diag", "cross_out"))
        part_ready, sum_ready, log_ready, args_ready, exps_ready = (sem(n) for n in ("part_ready", "sum_ready", "log_ready", "args_ready", "exps_ready"))
        score_arg, score_ready = sem("score_arg"), sem("score_ready")
        flags_ready, prefix_ready, slot_ready = sem("flags_ready"), sem("prefix_ready"), sem("slot_ready")
        copied, light_T, light_Tsb, light_h, light_g, light_o, light_added = (
            sem(n) for n in ("copied", "light_T", "light_Tsb", "light_h", "light_g", "light_o", "light_added"))
        scattered = [sem(f"scattered{b}") for b in range(BATCH)]
        picked_in, stored = sem("picked_in"), sem("stored")
        gathered = [sem(f"gathered{b}") for b in range(BATCH)]
        heavy_room = sem("heavy_room")
        heavy_T, heavy_Tsb, heavy_h, heavy_g, heavy_o, heavy_done, mixed = (
            sem(n) for n in ("heavy_T", "heavy_Tsb", "heavy_h", "heavy_g", "heavy_o", "heavy_done", "mixed"))
        S = [{n: sem(f"{n}_{l}") for n in names} for l in range(2)]
        gate_in, gate_ready = sem("gate_in"), sem("gate_ready")
        G = {n: sem(f"g_{n}") for n in (
            "stats rstd_ready h_ready h_saved hT_ps hT_sb sums_ps sums_sb bn_done bn_ready hs_ready acts_ready hsT_ps hsT_sb "
            "logit_ps full_ps work_ready top_done minus_ready exp_ready taken_ready part_ready sparse_ready sparseT_ps "
            "sparseT_sb in_ps part_added x_new").split()}

        start_at_first = (
            [s[n] for s in S for n in ("o_ps", "s_exp", "x_new", "y_ready")] +
            [G[n] for n in ("exp_ready", "hT_sb", "in_ps", "part_ready", "sparseT_ps", "sparseT_sb", "sums_ps",
             "sums_sb", "taken_ready", "x_new")] +
            [heavy_Tsb, heavy_done, heavy_h, heavy_o, light_T, light_Tsb, light_added, light_g, light_o,
             scale_ready])

        block = ctx.enter_context(nc.Block())

        x_dram = A["x"].rearrange("(n p) d -> p n d", p=P)
        out_dram = A["out"].rearrange("(n p) d -> p n d", p=P)

        def halves(w):
            return w.rearrange("(k p) n -> p k n", p=P)

        def plain(eng):
            eng.sem_inc(waits_taken, 1)

        @block.sync
        def _(sp):
            sp.dma_start(x[:, 0:4, :], x_dram[:, 0:4, :]).then_inc(x_in[0], 16)
            for i in range(2):
                for k in range(KH):
                    sp.dma_start(ctxT[:, k, :, i, :], A["ctxT"][k * P:(k + 1) * P, :].rearrange("p (b n) -> p b n", n=KEYS))\
                      .then_inc(ctx_in, 16)
            for w, name in ((Wk[0], "Wk0"), (Wv[0], "Wv0"), (Wq[0], "Wq0"), (Wo[0], "Wo0")):
                sp.dma_start(w[:, :, :], halves(A[name])).then_inc(attn_w_in[0], 16)
            sp.dma_start(x[:, 4:8, :], x_dram[:, 4:8, :]).then_inc(x_in[1], 16)
            sp.dma_start(x[:, 8:TILES, :], x_dram[:, 8:TILES, :]).then_inc(x_in[2], 16)
            for w, name in ((Wk[1], "Wk1"), (Wv[1], "Wv1"), (Wq[1], "Wq1"), (Wo[1], "Wo1")):
                sp.dma_start(w[:, :, :], halves(A[name])).then_inc(attn_w_in[1], 16)
            for w, name in ((conv_bd[:, :, :], halves(A["conv_bd"])), (gate_w[:, :, :], halves(A["gate_w"])),
                            (lin_bd[:, :], A["lin_bd"]), (bn_cols[:, :], A["bn_cols"])):
                sp.dma_start(w, name).then_inc(gate_in, 16)
            sp.wait_ge(pieces_ready, 1)
            for k in range(3):
                sp.dma_start(bias3[k:k + 1, :, :].rearrange("p j d -> p (j d)"), bias_piece[k][:, :]).then_inc(bias_ready, 16)

            def load_picked(b):
                sp.wait_ge(scattered[b], 16 * 8)
                if b >= 2:
                    sp.wait_ge(heavy_T, b - 1)
                    sp.wait_ge(heavy_done, b - 1 + FIRST)
                sp.dma_start(picked[b % 2][:, :, :], rows_in[b].rearrange("(j p) d -> p j d", p=P))\
                  .then_inc(picked_in, 16)
                sp.wait_ge(picked_in, 16 * (b + 1))

            def store_heavy(b):
                sp.wait_ge(heavy_done, b + 1 + FIRST)
                sp.dma_start(rows_out[b].rearrange("(j p) d -> p j d", p=P), heavy_y[b % 2][:, :, :])\
                  .then_inc(stored, 16)
                sp.wait_ge(stored, 16 * (b + 1))
                sp.sem_inc(heavy_room, 1)

            sp.sem_inc(heavy_room, 2)
            load_picked(0)
            load_picked(1)
            for b in range(BATCH):
                store_heavy(b)
                if b + 2 < BATCH:
                    load_picked(b + 2)
            for b in range(BATCH):
                sp.wait_ge(G["x_new"], 8 * (b + 1) + FIRST)
                sp.dma_start(out_dram[:, 8 * b:8 * b + 8, :], x[:, 8 * b:8 * b + 8, :]).then_inc(out_done, 16)
            sp.wait_ge(out_done, 16 * BATCH)

        @block.gpsimd
        def _(pool):
            for first in start_at_first:
                pool.sem_inc(first, FIRST)
            step = Chain(pool, pool_step)
            pool.memset(minus_half[:, :], -0.5).then_inc(set_ready, 1)
            pool.memset(ones16[:, :], 1.0).then_inc(set_ready, 1)
            pool.memset(maxT16[:, :], 0.0).then_inc(set_ready, 1)

            pool.memset(eighth[:, :], 1.0 / ROUTE_K).then_inc(set_ready, 1)
            pool.memset(ones4[:, :], 1.0).then_inc(set_ready, 1)
            pool.memset(zeros2[:, :], 0.0).then_inc(set_ready, 1)

            def row_rstd(s, n):
                pool.wait_ge(s["stats"], n)
                plain(pool)
                step.did(pool.tensor_scalar(var_eps[:, :], mean_var[:, :, 1], LN_EPS, None, ALU.add))
                step.settle()
                pool.tensor_tensor(rstd[:, :], var_eps[:, :], minus_half[:, :], ALU.pow).then_inc(s["rstd_ready"], 1)

            def keys16(s, l):
                for b in range(BATCH):
                    for m in range(KH):
                        pool.wait_ge(s["k_sb"], m + 1)
                        pool.tensor_tensor(k16[:, b, m, :, :], kT[:, m, b, :].unsqueeze(1).to_broadcast([P, 8, KEYS]),
                                           head_mask[:, :, :], ALU.mult).then_inc(s["k16_ready"], 1)

            def row_scales(c):
                pool.wait_ge(route_stats_ready, c + 1)
                plain(pool)
                v = [route_var[:, i, :] for i in range(6)]
                step.did(pool.tensor_scalar(v[0], route_mv[:, :, 1], LN_EPS, None, ALU.add))
                step.settle()
                step.did(pool.tensor_tensor(v[1], v[0], minus_half[:, :], ALU.pow))
                step.settle()
                step.did(pool.tensor_tensor(v[2], v[1], v[1], ALU.mult))
                step.settle()
                step.did(pool.tensor_tensor(v[3], v[2], route_mv[:, :, 1], ALU.mult))
                step.settle()
                plain(pool)
                step.did(pool.tensor_scalar(v[4], v[3], (1e-12 / 16.0) ** 2, None, ALU.max))
                step.settle()
                step.did(pool.tensor_tensor(v[5], v[4], minus_half[:, :], ALU.pow))
                step.settle()
                pool.tensor_tensor(row_scale[:, :], v[5], v[1], ALU.mult).then_inc(scale_ready, 1)
                pool.tensor_tensor(row_norm[:, ds(c * 4, 4)], v[5], v[4], ALU.mult).then_inc(scale_ready, 1)

            def route_rows():
                pool.wait_ge(slot_ready, 1)
                def clear(i):
                    step.did(pool.memset(heavy_rows[i][:, :, :], 0.0))
                for b in range(BATCH):
                    for t in range(8 * b, 8 * b + 8):
                        pool.indirect_dma_start(rows_in[b], bass.IndirectOffsetOnAxis(ap=slot[:, t:t + 1], axis=0),
                                                normed[:, t, :], None, bounds_check=ROUTED - 1,
                                                oob_is_err=False).then_inc(scattered[b], 16)
                for i in range(2):
                    clear(i)
                step.settle()

                def gather(b):
                    pool.wait_ge(stored, 16 * (b + 1))
                    for t in range(8 * b, 8 * b + 8):
                        pool.indirect_dma_start(heavy_rows[b % 2][:, t - 8 * b, :], None, rows_out[b],
                                                bass.IndirectOffsetOnAxis(ap=slot[:, t:t + 1], axis=0),
                                                bounds_check=ROUTED - 1, oob_is_err=False).then_inc(gathered[b], 16)

                def add_heavy(b):
                    pool.wait_ge(gathered[b], 16 * 8)
                    pool.tensor_tensor(x[:, 8 * b:8 * b + 8, :], x[:, 8 * b:8 * b + 8, :], heavy_rows[b % 2][:, :, :],
                                       ALU.add).then_inc(mixed, 1)

                gather(0)
                for b in range(BATCH):
                    if b + 1 < BATCH:
                        if b:
                            pool.wait_ge(mixed, b)
                            clear((b + 1) % 2)
                            step.settle()
                        gather(b + 1)
                    if b == 0:
                        pool.wait_ge(light_added, 2 * CHUNKS + FIRST)
                    add_heavy(b)

            def gate_norm():
                pool.wait_ge(G["bn_done"], 1)
                c = [bn_tmp[:, i:i + 1] for i in range(5)]
                step.did(pool.tensor_scalar(c[0], bn_mv[:, 1:2], BN_EPS, None, ALU.add))
                step.settle()
                step.did(pool.tensor_tensor(c[1], c[0], minus_half[:, 0:1], ALU.pow))
                step.settle()
                step.did(pool.tensor_tensor(c[2], c[1], bn_cols[:, 1:2], ALU.mult))
                step.settle()
                step.did(pool.tensor_tensor(c[3], c[2], bn_mv[:, 0:1], ALU.mult))
                step.settle()
                pool.tensor_tensor(c[4], bn_cols[:, 2:3], c[3], ALU.subtract).then_inc(G["bn_ready"], 1)

            def gate_tile(t):
                pool.wait_ge(G["top_done"], t + 1)
                pool.tensor_tensor(minus_top[:, :], zeros2[:, :], top8[:, 0, :, 0], ALU.subtract).then_inc(G["minus_ready"], 1)
                pool.wait_ge(G["taken_ready"], t + 1 + FIRST)
                pool.wait_ge(G["sparseT_ps"], t + FIRST)
                step.did(pool.tensor_tensor(sparse, taken[:, DIM:], inv_sum[:, 1:2].to_broadcast([P, DIM]), ALU.mult))
                step.settle()
                pool.tensor_tensor(sparse, sparse, normed[:, ds(t, 1), 0:DIM].rearrange("p a d -> p (a d)"),
                                   ALU.mult).then_inc(G["sparse_ready"], 1)
                pool.wait_ge(G["part_ready"], t + 1 + FIRST)
                rows = x[:, ds(t, 1), :].rearrange("p a d -> p (a d)")
                pool.tensor_tensor(rows, rows, out_part, ALU.add).then_inc(G["part_added"], 1)

            pool.wait_ge(set_ready, 1)
            pool.wait_ge(masks_in, 32)
            for l in range(2):
                s = S[l]
                if l == 1:
                    pool.wait_ge(S[0]["max_ps"], 8 * CHUNKS)
                    keys16(s, l)
                row_rstd(s, 1)
                if l == 0:
                    keys16(s, l)
                row_rstd(s, 2)
                with pool.Fori(0, BATCH - 1) as b:
                    step.enter(b, 2 + (12 if l == 0 else 0))
                    for e in range(2):
                        row_rstd(s, b * 2 + (e + 3))
                        if l == 0:
                            row_scales(b * 2 + e)
                    step.leave(BATCH - 1)
                if l == 0:
                    for e in range(2):
                        row_scales(CHUNKS - 2 + e)
                    route_rows()
            pool.wait_ge(gate_in, 64)
            row_rstd(G, 1)
            with pool.Fori(1, CHUNKS) as c:
                step.enter(c - 1, 1)
                row_rstd(G, c + 1)
                step.leave(CHUNKS - 1)
            gate_norm()
            with pool.Fori(0, TILES) as t:
                step.enter(t, 1)
                gate_tile(t)
                step.leave(TILES)

        @block.scalar
        def _(act):
            act.dma_start(gates[:, :], A["gates"].partition_broadcast(P)).then_inc(gates_in, 16)
            act.dma_start(bias_gates[:, :], A["bias_gates"]).then_inc(gates_in, 16)
            act.dma_start(ident[:, :], A["ident"]).then_inc(consts_in, 16)
            act.dma_start(head_mask[:, :, :], A["head_mask"].rearrange("p (h k) -> p h k", h=8)).then_inc(masks_in, 16)
            act.dma_start(pair_mask[:, :, :], A["pair_mask"].rearrange("p (h d) -> p h d", h=HEADS)).then_inc(masks_in, 16)
            act.dma_start(qkv_bias[:, :], A["qk_bias"]).then_inc(bias_in, 16)
            act.dma_start(v_bias[:, :], A["bv1"].partition_broadcast(P)).then_inc(bias_in, 16)
            act.dma_start(bias_rows[:, :], A["bias_rows"]).then_inc(bias_in, 16)
            act.dma_start(ident16[:, :], A["ident16"].bitcast(BF16)).then_inc(consts_in, 16)
            act.dma_start(neg_sel16[:, :, :], A["neg_sel16"].bitcast(BF16).rearrange("p (a n) -> p a n", a=PAIRS)).then_inc(consts_in, 16)
            act.dma_start(causal_rows16[:, :], A["causal_rows16"].bitcast(BF16)).then_inc(consts_in, 16)
            act.dma_start(causal_keys16[:, :], A["causal_keys16"].bitcast(BF16)).then_inc(consts_in, 16)
            act.dma_start(token_row[:, :], A["token"].partition_broadcast(P)).then_inc(route_in, 16)
            act.dma_start(slot_base[:, :, :], A["slot_base"].rearrange("p (a n) -> p a n", a=2)).then_inc(route_in, 16)
            act.dma_start(before16[:, :], A["before16"].bitcast(BF16)).then_inc(route_in, 16)
            act.dma_start(ffn0_cols[:, :], A["ffn0_cols"]).then_inc(ffn0_in, 16)
            act.dma_start(w1l[:, :, :], halves(A["w1l"])).then_inc(ffn0_in, 16)
            act.dma_start(w2l[:, :], A["w2l"]).then_inc(ffn0_in, 16)
            act.dma_start(w1h[:, :, :], halves(A["w1h"])).then_inc(ffn0_in, 16)
            act.dma_start(w2h[:, :, :], A["w2h"].rearrange("(m p) n -> p m n", p=P)).then_inc(ffn0_in, 16)
            act.wait_ge(gates_in, 32)
            act.activation(gates[:, :], gates[:, :], ACT.Tanh).then_inc(gates_ready, 1)
            act.activation(bias_gates[:, :], bias_gates[:, :], ACT.Tanh).then_inc(gates_ready, 1)

            def keys(s, l):
                for m in range(KH):
                    act.wait_ge(s["k_ps"], m + 1)
                    src = front[m][:, 0:BATCH * KEYS].rearrange("p (b n) -> p b n", b=BATCH)
                    if l == 0:
                        act.activation(kT[:, m, :, :], src, ACT.Copy).then_inc(s["k_sb"], 1)
                    else:
                        act.activation(kT[:, m, :, :], src, ACT.Identity, bias=qkv_bias[:, 2 + m:3 + m]).then_inc(s["k_sb"], 1)

            def evac_hT(s, a):
                act.wait_ge(s["hT_ps"], a + 1)
                if not (isinstance(a, int) and a == 0):
                    act.wait_ge(s["q_ps"], a * 2)
                for k in range(KH):
                    act.activation(hT[:, k, :], front[k][:, :], ACT.Copy).then_inc(s["hT_sb"], 1)

            def evac_q(s, l, a, e, m):
                act.wait_ge(s["q_ps"], a * 2 + (m + 1))
                if not isinstance(a, int) or a >= 2:
                    act.wait_ge(s["s_ps"], a * 8 - 8)
                if l == 0:
                    act.activation(qT[e][:, m, :], front[m][:, :], ACT.Copy).then_inc(s["q_sb"], 1)
                else:
                    act.activation(qT[e][:, m, :], front[m][:, :], ACT.Identity,
                                   bias=qkv_bias[:, m:m + 1]).then_inc(s["q_sb"], 1)

            def evac_maxT(s, n):
                act.wait_ge(s["maxT_ps"], n + 1)
                if not (isinstance(n, int) and n == 0):
                    act.wait_ge(s["s_ps"], n * 8)
                act.activation(maxT16[0:HEADS, :], maxT_ps, ACT.Copy).then_inc(s["maxT_sb"], 1)

            def exp(s, c, p):
                act.wait_ge(s["s_ps"], c * 8 + (p + 1))
                act.wait_ge(s["pv"], c * 8 + (p + 1))
                act.activation(probs[:, p % 4, :], score[p % 2][:, :], ACT.Exp, scale=SCALE).then_inc(s["s_exp"], 1)

            def inverse(s, step, c, m):
                act.wait_ge(s["pv"], c * 8 + (4 * m + 4 + 4))
                act.wait_ge(s["y_ready"], c * 2 + m + FIRST)
                step.did(act.activation(log_den[:, m, :], DB[:, :], ACT.Ln))
                step.settle()
                act.activation(inv_den[:, m, :], log_den[:, m, :], ACT.Exp, scale=-1.0).then_inc(s["inv_ready"], 1)

            def chunk_step(s, l, step, c, e, ahead, nxt):
                for p in range(PAIRS):
                    exp(s, c, p)
                    if p == 3 and ahead:
                        evac_hT(s, c + 2)
                    if p == 5:
                        inverse(s, step, c, 0)
                    if p == 6 and ahead:
                        evac_q(s, l, c + 2, e, 0)
                inverse(s, step, c, 1)
                if nxt:
                    evac_maxT(s, c + 1)
                if ahead:
                    evac_q(s, l, c + 2, e, 1)

            def ffn0():
                for b in range(BATCH):
                    for i in range(2):
                        act.wait_ge(rows_ps, 2 * b + i + 1)
                        act.activation(logit_rows[:, b, i * 512:(i + 1) * 512], score[i][:, :], ACT.Copy).then_inc(rows_sb, 1)
                act.wait_ge(args_ready, 1)
                act.activation(exps[:, :], args[:, :], ACT.Exp).then_inc(exps_ready, 1)

                def light_chunk(n):
                    act.wait_ge(light_T, n + FIRST)
                    act.activation(h[:, :, :], normed[:, ds(n * 4, 4), 0:DIM], ACT.Copy).then_inc(copied, 1)
                    act.wait_ge(light_T, n + 1 + FIRST)
                    for k in range(KH):
                        act.activation(hT[:, k, :], front[k][:, :], ACT.Copy).then_inc(light_Tsb, 1)
                    act.wait_ge(light_h, n + 1)
                    act.wait_ge(light_o, n * 2 + FIRST)
                    act.activation(light_gT, mid[0][:, :], ACT.Gelu, bias=ffn0_cols[:, 4:5]).then_inc(light_g, 1)

                def relevel(n):
                    act.wait_ge(sum_ready, n)
                    act.activation(log_sum[:, :], DB[:, 0:BATCH], ACT.Ln, scale=2.0 ** -LOG_SHIFT).then_inc(log_ready, 1)

                for n in range(len(ROUTE_BLOCKS)):
                    with act.Fori(0, 2) as i:
                        light_chunk(i + 2 * n)
                    relevel(sums_before[n + 1])
                    if n + 1 < len(ROUTE_BLOCKS):
                        act.wait_ge(args_ready, n + 2)
                        act.activation(exps[:, :], args[:, :], ACT.Exp).then_inc(exps_ready, 1)
                act.wait_ge(score_arg, 1)
                act.activation(score_of[:, :], args[:, 0:TILES], ACT.Exp).then_inc(score_ready, 1)
                with act.Fori(0, BATCH) as b:
                    for m in range(HEAVY // P):
                        act.wait_ge(heavy_h, b * 8 + (m + 1) + FIRST)
                        if m == 0:
                            act.wait_ge(heavy_o, b + FIRST)
                        act.activation(heavy_gT[:, m, :], heavy_banks[m % 4][:, 0:ROUTED], ACT.Gelu,
                                       bias=ffn0_cols[:, 5 + m:6 + m]).then_inc(heavy_g, 1)

            step = Chain(act, act_step)
            for l in range(2):
                s = S[l]
                if l == 1:
                    ffn0()
                act.sem_inc(s["pv"], 4)
                act.preload_act_table_set("natural_log_exp_and_others")
                if l == 1:
                    act.wait_ge(bias_in, 48)
                keys(s, l)
                for a in range(2):
                    evac_hT(s, a)
                    for m in range(KH):
                        evac_q(s, l, a, a, m)
                evac_maxT(s, 0)
                with act.Fori(0, BATCH - 1) as b:
                    step.enter(b, 4)
                    for e in range(2):
                        chunk_step(s, l, step, b * 2 + e, e, True, True)
                    step.leave(BATCH - 1)
                for e in range(2):
                    chunk_step(s, l, step, CHUNKS - 2 + e, e, False, e == 0)
            act.wait_ge(gate_in, 64)
            with act.Fori(0, CHUNKS) as c:
                act.wait_ge(G["h_ready"], c + 1)
                act.activation(normed[:, ds(c * 4, 4), 0:DIM], h[:, :, :], ACT.Copy).then_inc(G["h_saved"], 1)
                act.wait_ge(G["hT_ps"], c + 1)
                act.wait_ge(G["sums_ps"], c + FIRST)
                for k in range(KH):
                    act.activation(hT[:, k, :], front[k][:, :], ACT.Copy).then_inc(G["hT_sb"], 1)
                act.wait_ge(G["sums_ps"], c + 1 + FIRST)
                act.activation(groups[:, ds(c * CHUNK, CHUNK)], M0[:, :], ACT.Identity,
                               bias=bn_cols[:, 0:1]).then_inc(G["sums_sb"], 1)
            act.wait_ge(G["bn_ready"], 1)
            with act.Fori(0, CHUNKS) as c:
                step.enter(c, 1)
                step.did(act.activation(groups[:, ds(c * CHUNK, CHUNK)], groups[:, ds(c * CHUNK, CHUNK)], ACT.Gelu,
                                        bias=bn_tmp[:, 4:5], scale=bn_tmp[:, 2:3]))
                step.leave(CHUNKS)
            step.settle()

            def prepare(t, e):
                act.wait_ge(G["hsT_ps"], t)
                act.activation(hs[e], normed[:, ds(t, 1), 0:DIM].rearrange("p a d -> p (a d)"), ACT.Copy).then_inc(G["hs_ready"], 1)
                act.wait_ge(G["logit_ps"], t)
                act.activation(acts[e], groups[:, ds(t * P, P)], ACT.Copy).then_inc(G["acts_ready"], 1)
                act.wait_ge(G["hsT_ps"], t + 1)
                act.wait_ge(G["full_ps"], t)
                act.activation(hsT[e], F0[:, 0:2 * P].rearrange("p (k n) -> p k n", k=KH), ACT.Copy).then_inc(G["hsT_sb"], 1)
                act.wait_ge(G["logit_ps"], t + 1)
                if not (isinstance(t, int) and t == 0):
                    act.wait_ge(G["taken_ready"], t - 1 + FIRST)
                act.activation(work[e], mid[e][:, :], ACT.Copy).then_inc(G["work_ready"], 1)

            def gate_tile(t, e, ahead):
                act.wait_ge(G["minus_ready"], t + 1)
                act.wait_ge(G["taken_ready"], t + FIRST)
                for br in range(2):
                    act.activation(expw[:, br * DIM:(br + 1) * DIM], mid[e][:, br * DIM:(br + 1) * DIM], ACT.Exp,
                                   bias=minus_top[:, br:br + 1], accum_out=exp_sum[:, br:br + 1]).then_inc(G["exp_ready"], 1)
                if ahead:
                    prepare(t + 1, 1 - e)
                act.wait_ge(G["sparseT_ps"], t + 1 + FIRST)
                act.wait_ge(G["in_ps"], t + FIRST)
                act.activation(sparseT, F1[:, 0:2 * P].rearrange("p (k n) -> p k n", k=KH), ACT.Copy).then_inc(G["sparseT_sb"], 1)

            prepare(0, 0)
            with act.Fori(0, TILES // 2 - 1) as i:
                for e in range(2):
                    gate_tile(i * 2 + e, e, True)
            for e in range(2):
                gate_tile(TILES - 2 + e, e, e == 0)

        @block.vector
        def _(dve):
            step = Chain(dve, dve_step)

            def split_biases():
                step.did(dve.memset(bias3[:, :, :], 0.0))
                step.did(dve.tensor_scalar(bias_rows[0:4, :], bias_rows[0:4, :], bias_gates[:, 0:1], None, ALU.mult))
                step.settle()
                for k in range(3):
                    step.did(dve.tensor_copy(bias_piece[k][:, :], bias_rows[:, :]))
                    step.settle()
                    if k < 2:
                        step.did(dve.tensor_tensor(bias_rows[:, :], bias_rows[:, :], bias_piece[k][:, :], ALU.subtract))
                        step.settle()
                dve.sem_inc(pieces_ready, 1)

            def row_stats_of(s, tile0, n, step):
                if not (isinstance(n, int) and n == 0):
                    dve.wait_ge(s["rstd_ready"], n)
                    plain(dve)
                for t in range(CHUNK_TILES):
                    step.did(dve.bn_stats(row_stats[:, t, :], x[:, ds(tile0 + t, 1), :].rearrange("p a d -> p (a d)")))
                step.settle()
                plain(dve)
                for t in range(CHUNK_TILES):
                    ins = dve.bn_aggr(mean_var[:, t, :], row_stats[:, t, :])
                ins.then_inc(s["stats"], 1)

            def normalize(s, tile0, a):
                dve.wait_ge(s["rstd_ready"], a + 1)
                if not (isinstance(a, int) and a == 0):
                    dve.wait_ge(s["hT_ps"], a)
                for t in range(CHUNK_TILES):
                    ins = dve.tensor_scalar(h[:, t, :], x[:, ds(tile0 + t, 1), :].rearrange("p a d -> p (a d)"),
                                            mean_var[:, t, 0:1], rstd[:, t:t + 1], ALU.subtract, ALU.mult)
                ins.then_inc(s["h_ready"], 1)

            def q_to_16(s, a, e, m):
                dve.wait_ge(s["q_sb"], a * 2 + (m + 1))
                if not (isinstance(a, int) and a == 0):
                    dve.wait_ge(s["max_ps"], a * 8)
                dve.tensor_copy(q16[:, m, :], qT[e][:, m, :]).then_inc(s["q16_ready"], 1)

            def row_max(s, n, j):
                t, m = j // 2, j % 2
                dve.wait_ge(s["max_ps"], n * 8 + (j + 1))
                if j == 0 and not (isinstance(n, int) and n == 0):
                    dve.wait_ge(s["maxT_ps"], n)
                dve.tensor_reduce(max16[:, t, 8 * m:8 * m + 8], mid[j % 2][:, :].rearrange("p (h k) -> p h k", h=8),
                                  AX_X, ALU.max).then_inc(s["max_done"], 1)

            def divide(s, c, m):
                dve.wait_ge(s["inv_ready"], c * 2 + (m + 1))
                if not (isinstance(c, int) and c == 0):
                    dve.wait_ge(s["o_ps"], c * 2 + FIRST)
                dve.tensor_tensor(yT[:, m, :], YB[:, :], inv_den[:, m, :], ALU.mult).then_inc(s["y_ready"], 1)

            def add_to_x(s, c, g):
                dve.wait_ge(s["o_ps"], c * 2 + (g + 1) + FIRST)
                rows = x[:, ds(c * 4 + 2 * g, 2), :].rearrange("p a d -> p (a d)")
                dve.tensor_tensor(rows, rows, mid[g][:, :], ALU.add).then_inc(s["x_new"], 1)

            def key_value_diagonals(s, b, first):
                if not first:
                    dve.wait_ge(s["s_ps"], b * 16)
                for m in range(KH):
                    dve.tensor_tensor(k_diag[:, m, :, :], kT[:, m, ds(b, 1), :].to_broadcast([P, 8, KEYS]),
                                      head_mask[:, :, :], ALU.mult).then_inc(s["kv_diag"], 1)
                if not first:
                    dve.wait_ge(s["pv"], b * 16 + 4)
                dve.tensor_tensor(v_diag[:, :, :], v_all[:, ds(b, 1), :].rearrange("p a (h d) -> p (a h) d", h=HEADS),
                                  pair_mask[:, :, :], ALU.mult).then_inc(s["kv_diag"], 1)

            def chunk_step(s, c, e, b, ahead, nxt):
                if ahead:
                    row_stats_of(s, c * 4 + 8, c + 2, step)
                for p in range(PAIRS):
                    if p == 2 and ahead:
                        normalize(s, c * 4 + 8, c + 2)
                    if nxt:
                        row_max(s, c + 1, p)
                    if p == 5:
                        divide(s, c, 0)
                divide(s, c, 1)
                if ahead:
                    for m in range(KH):
                        q_to_16(s, c + 2, e, m)
                for g in range(2):
                    add_to_x(s, c, g)
                if e == 1 and nxt:
                    key_value_diagonals(s, b + 1, False)

            def route_stats_of(c):
                dve.wait_ge(s0["x_new"], c * 2 + 2 + FIRST)
                dve.wait_ge(scale_ready, c * 2 + FIRST)
                plain(dve)
                for t in range(CHUNK_TILES):
                    step.did(dve.bn_stats(route_stats[:, t, :], x[:, ds(c * 4 + t, 1), :].rearrange("p a d -> p (a d)")))
                step.settle()
                plain(dve)
                for t in range(CHUNK_TILES):
                    ins = dve.bn_aggr(route_mv[:, t, :], route_stats[:, t, :])
                ins.then_inc(route_stats_ready, 1)

            def route_logits_of(c):
                dve.wait_ge(scale_ready, c * 2 + 2 + FIRST)
                for t in range(CHUNK_TILES):
                    step.did(dve.tensor_scalar(normed[:, ds(c * 4 + t, 1), 0:DIM].rearrange("p a d -> p (a d)"),
                                               x[:, ds(c * 4 + t, 1), :].rearrange("p a d -> p (a d)"),
                                               route_mv[:, t, 0:1], row_scale[:, t:t + 1], ALU.subtract, ALU.mult))
                for t in range(CHUNK_TILES):
                    step.did(dve.scalar_tensor_tensor(
                        out=dot_out[:, :], in0=x[:, ds(c * 4 + t, 1), :].rearrange("p a d -> p (a d)"),
                        scalar=route_mv[:, t, 0:1], in1=token_row[:, :], op0=ALU.subtract, op1=ALU.mult,
                        accum_out=raw_dot[:, t:t + 1]))
                    step.settle()
                step.did(dve.tensor_tensor(raw_dot[:, :], raw_dot[:, :], row_scale[:, :], ALU.mult))
                step.settle()
                dve.tensor_tensor(logit[:, ds(c * 4, 4)], raw_dot[:, :], row_norm[:, ds(c * 4, 4)], ALU.mult).then_inc(logit_ready, 1)

            by_batch = lambda ap: ap.rearrange("p (b c) -> p b c", b=BATCH)
            spread = lambda ap: ap.unsqueeze(2).to_broadcast([P, BATCH, TILES // BATCH])

            def cross_max(n):
                dve.wait_ge(cross_ps, n + 1)
                dve.tensor_reduce(col4[:, :], YB[0:BATCH, 0:P], AX_X, ALU.max).then_inc(cross_col, 1)
                dve.wait_ge(cross_col, n + 1)
                dve.tensor_scalar(diag4[:, :], ident[0:BATCH, 0:BATCH], col4[:, 0:1], None, ALU.mult).then_inc(cross_diag, 1)
                dve.wait_ge(cross_out, n + 1)

            def exp_args():
                step.did(dve.tensor_tensor(level[:, :], minus_a[:, :], top_logit[:, :], ALU.min))
                step.settle()
                step.did(dve.tensor_tensor(by_batch(args[:, 0:TILES]), by_batch(logit[:, :]), spread(level[:, :]), ALU.subtract))
                step.did(dve.tensor_tensor(args[:, TILES:], minus_a[:, :], level[:, :], ALU.subtract))
                step.settle()
                dve.tensor_scalar(args[:, :], args[:, :], 1.0 / ROUTE_EPS, 80.0, ALU.mult, ALU.min).then_inc(args_ready, 1)

            def route_iteration(sums):
                dve.wait_ge(sum_ready, sums)
                step.did(dve.tensor_tensor(by_batch(capped[:, :]), by_batch(exps[:, 0:TILES]), spread(DB[:, 0:BATCH]), ALU.min))
                step.settle()
                dve.tensor_reduce(part_sum[:, :], by_batch(capped[:, :]), AX_X, ALU.add).then_inc(part_ready, 1)

            def count_above(b, t):
                step.did(dve.tensor_scalar(compare_out[:, :], logit_rows[:, b, :], logit[:, ds(t, 1)], 0.0,
                                           ALU.is_gt, ALU.add, accum_out=above[:, ds(t, 1)]))

            def light_to_x(n, g):
                dve.wait_ge(light_o, n * 2 + (g + 1) + FIRST)
                rows = x[:, ds(n * 4 + 2 * g, 2), :].rearrange("p a d -> p (a d)")
                dve.tensor_tensor(rows, rows, score[g][:, :], ALU.add).then_inc(light_added, 1)

            def route():
                dve.wait_ge(logit_ready, CHUNKS)
                dve.wait_ge(s0["x_new"], 2 * CHUNKS + FIRST)
                dve.tensor_reduce(part_sum[:, :], by_batch(logit[:, :]), AX_X, ALU.max).then_inc(cross_in, 1)
                step.did(dve.memset(minus_a[:, :], 0.0))
                cross_max(0)
                step.did(dve.tensor_copy(top_logit[:, :], YB[:, P:P + BATCH]))
                step.settle()
                exp_args()
                for n, iters in enumerate(ROUTE_BLOCKS):
                    dve.wait_ge(exps_ready, n + 1)
                    dve.tensor_scalar(part_sum[:, :], exps[:, TILES:], ROUTE_K / P, None, ALU.mult).then_inc(part_ready, 1)
                    dve.wait_ge(rows_sb, 2 * n + 2)
                    with dve.Fori(0, 2) as i:
                        step.enter(i, CHUNK_ITERS + CHUNK_TILES)
                        for j in range(CHUNK_ITERS):
                            route_iteration(i * CHUNK_ITERS + (sums_before[n] + 1 + j))
                            if j < CHUNK_TILES:
                                count_above(n, i * 4 + (8 * n + j))
                            else:
                                light_to_x(i + 2 * n, j - CHUNK_TILES)
                        step.leave(2)
                    for j in range(2 * CHUNK_ITERS, iters):
                        route_iteration(sums_before[n] + 1 + j)
                    dve.wait_ge(log_ready, n + 1)
                    step.did(dve.tensor_scalar(log_sum[:, :], log_sum[:, :], LOG_SHIFT * math.log(2.0), None, ALU.add))
                    step.settle()
                    step.did(dve.scalar_tensor_tensor(out=minus_a[:, :], in0=log_sum[:, :], scalar=ROUTE_EPS, in1=level[:, :],
                                                      op0=ALU.mult, op1=ALU.add))
                    step.settle()
                    if n + 1 < len(ROUTE_BLOCKS):
                        exp_args()
                step.did(dve.tensor_tensor(by_batch(args[:, 0:TILES]), by_batch(logit[:, :]), spread(minus_a[:, :]), ALU.subtract))
                step.settle()
                step.did(dve.tensor_scalar(args[:, 0:TILES], args[:, 0:TILES], 0.0, 1.0 / ROUTE_EPS, ALU.min, ALU.mult))
                step.settle()
                dve.sem_inc(score_arg, 1)
                key, larger, equal, take = (pick[:, i, :] for i in range(4))
                step.did(dve.tensor_scalar(key, args[:, 0:TILES], LOG_TINY, None, ALU.max))
                step.did(dve.tensor_scalar(take, above[:, :], ROUTED - 0.5, 1.0, ALU.is_gt, ALU.mult))
                step.settle()
                step.did(dve.scalar_tensor_tensor(out=larger, in0=take, scalar=1e4, in1=key, op0=ALU.mult, op1=ALU.add))
                step.settle()
                dve.tensor_reduce(part_sum[:, :], by_batch(larger), AX_X, ALU.min, negate=True).then_inc(cross_in, 1)
                cross_max(1)
                step.did(dve.tensor_scalar(level[:, :], YB[:, P:P + BATCH], -1.0, None, ALU.mult))
                step.settle()
                step.did(dve.tensor_tensor(by_batch(larger), by_batch(key), spread(level[:, :]), ALU.is_gt))
                step.did(dve.tensor_tensor(by_batch(equal), by_batch(key), spread(level[:, :]), ALU.is_equal))
                step.settle()
                step.did(dve.tensor_copy(flag16[:, :], equal))
                step.did(dve.tensor_reduce(part_sum[:, :], by_batch(larger), AX_X, ALU.add))
                step.settle()
                dve.tensor_copy(count16[:, :], part_sum[:, :]).then_inc(flags_ready, 1)
                dve.wait_ge(prefix_ready, 1)
                step.did(dve.tensor_scalar(minus_a[:, :], M1[:, 0:BATCH], -1.0, float(ROUTED), ALU.mult, ALU.add))
                step.settle()
                step.did(dve.tensor_tensor(by_batch(take), by_batch(M0[:, 0:TILES]), spread(minus_a[:, :]), ALU.is_lt))
                step.settle()
                step.did(dve.tensor_tensor(take, take, equal, ALU.mult))
                step.settle()
                step.did(dve.tensor_tensor(take, take, larger, ALU.add))
                step.settle()
                dve.tensor_copy(flag16[:, :], take).then_inc(flags_ready, 1)
                dve.wait_ge(prefix_ready, 2)
                step.did(dve.scalar_tensor_tensor(out=take, in0=M0[:, 0:TILES], scalar=float(ROUTED), in1=take,
                                                  op0=ALU.is_lt, op1=ALU.mult))
                step.did(dve.tensor_tensor(key, M0[:, 0:TILES], slot_base[:, 0, :], ALU.add))
                step.settle()
                step.did(dve.tensor_tensor(key, key, take, ALU.mult))
                step.settle()
                step.did(dve.tensor_tensor(key, key, slot_base[:, 1, :], ALU.add))
                step.settle()
                dve.wait_ge(score_ready, 1)
                step.did(dve.tensor_copy(normed[:, :, DIM], score_of[:, :]))
                step.did(dve.tensor_copy(slot[:, :], key))
                step.settle()
                dve.sem_inc(slot_ready, 1)

            def heavy():
                with dve.Fori(0, BATCH // 2) as i:
                    step.enter(i, 2 * 3)
                    for e in range(2):
                        b = i * 2 + e
                        dve.wait_ge(heavy_T, b + 1)
                        dve.wait_ge(heavy_h, b * 8 + FIRST)
                        dve.tensor_copy(pickedT[:, :, :], F0[:, :].rearrange("p (k n) -> p k n", k=KH)).then_inc(heavy_Tsb, 1)
                        dve.wait_ge(picked_in, b * 16 + 16)
                        dve.wait_ge(heavy_done, b + FIRST)
                        step.did(dve.tensor_scalar(pick_gate[:, :], picked[e][:, :, DIM], -1.0, 1.0, ALU.mult, ALU.add))
                        step.settle()
                        step.did(dve.tensor_tensor(pick_gate[:, :], pick_gate[:, :], picked[e][:, :, DIM], ALU.add))
                        step.settle()
                        step.did(dve.tensor_scalar(pick_gate[:, :], pick_gate[:, :], gates[:, 1:2], None, ALU.mult))
                        step.settle()
                        dve.wait_ge(heavy_o, b + 1 + FIRST)
                        dve.wait_ge(heavy_room, b + 1)
                        for j in range(2):
                            ins = dve.tensor_scalar(heavy_y[e][:, j, :], YB[:, j * DIM:(j + 1) * DIM], pick_gate[:, j:j + 1], None,
                                                    ALU.mult)
                        ins.then_inc(heavy_done, 1)
                    step.leave(BATCH // 2)

            def gate_ffn0():
                dve.wait_ge(ffn0_in, 16 * 5)
                for k in range(KH):
                    dve.tensor_scalar(w1l[:, k, :], w1l[:, k, :], ffn0_cols[:, k:k + 1], None, ALU.mult).then_inc(ffn0_ready, 1)
                    dve.tensor_scalar(w1h[:, k, :], w1h[:, k, :], ffn0_cols[:, 2 + k:3 + k], None, ALU.mult).then_inc(ffn0_ready, 1)
                dve.tensor_scalar(w2l[:, :], w2l[:, :], gates[:, 1:2], None, ALU.mult).then_inc(ffn0_ready, 1)

            def gate_rows(c):
                dve.wait_ge(G["rstd_ready"], c + 1)
                dve.wait_ge(G["hT_ps"], c)
                dve.wait_ge(G["h_saved"], c)
                for t in range(CHUNK_TILES):
                    ins = step.did(dve.tensor_scalar(h[:, t, :], x[:, ds(c * 4 + t, 1), :].rearrange("p a d -> p (a d)"),
                                                     mean_var[:, t, 0:1], rstd[:, t:t + 1], ALU.subtract, ALU.mult))
                step.settle()
                dve.sem_inc(G["h_ready"], 1)

            def group_stats(c):
                dve.wait_ge(G["sums_sb"], c + 1 + FIRST)
                plain(dve)
                step.did(dve.bn_stats(bn_parts[:, ds(c * 6, 6)], groups[:, ds(c * CHUNK, CHUNK)]))

            def gate_tile(t, e, first=False):
                dve.wait_ge(G["work_ready"], t + 1)
                dve.wait_ge(G["minus_ready"], t)
                for r in range(4):
                    for br in range(2):
                        cols = work[e][:, br * DIM:(br + 1) * DIM]
                        if r:
                            dve.wait_ge(top_step, t * 16 + (4 * r + br - 1))
                        plain(dve)
                        dve.max(top8[:, r, br, :], cols).then_inc(top_step, 1)
                    if r == 0:
                        dve.wait_ge(top_step, t * 16 + 2)
                        dve.sem_inc(G["top_done"], 1)
                    for br in range(2):
                        cols = work[e][:, br * DIM:(br + 1) * DIM]
                        dve.wait_ge(top_step, t * 16 + (4 * r + br + 1))
                        plain(dve)
                        dve.match_replace(cols, top8[:, r, br, :], cols, FOUND).then_inc(top_step, 1)
                    if r == 1 and not first:
                        add_in(t - 1, 1 - e)
                dve.wait_ge(G["exp_ready"], t * 2 + 2 + FIRST)
                dve.wait_ge(G["sparse_ready"], t)
                plain(dve)
                step.did(dve.reciprocal(inv_sum[:, :], exp_sum[:, :]))
                dve.wait_ge(top_step, t * 16 + 16)
                step.did(dve.scalar_tensor_tensor(out=taken, in0=work[e], scalar=FOUND / 2, in1=expw, op0=ALU.is_lt, op1=ALU.mult))
                step.settle()
                dve.sem_inc(G["taken_ready"], 1)
                dve.wait_ge(G["full_ps"], t + 1)
                dve.wait_ge(G["part_added"], t)
                dve.scalar_tensor_tensor(out=out_part, in0=score[e][:, 0:DIM], scalar=inv_sum[:, 0:1], in1=taken[:, 0:DIM],
                                         op0=ALU.mult, op1=ALU.mult).then_inc(G["part_ready"], 1)

            def add_in(t, e):
                dve.wait_ge(G["in_ps"], t + 1 + FIRST)
                dve.wait_ge(G["part_added"], t + 1)
                rows = x[:, ds(t, 1), :].rearrange("p a d -> p (a d)")
                dve.tensor_tensor(rows, rows, out_banks[e][:, 0:DIM], ALU.add).then_inc(G["x_new"], 1)

            def gate_layer():
                dve.wait_ge(gate_in, 64)
                dve.tensor_scalar(gate_w[:, :, :], gate_w[:, :, :], gates[:, 3:4], None, ALU.mult).then_inc(gate_ready, 1)
                row_stats_of(G, 0, 0, step)
                gate_rows(0)
                row_stats_of(G, 4, 1, step)
                with dve.Fori(1, CHUNKS - 1) as c:
                    step.enter(c - 1, 9)
                    gate_rows(c)
                    row_stats_of(G, c * 4 + 4, c + 1, step)
                    group_stats(c - 1)
                    step.leave(CHUNKS - 2)
                gate_rows(CHUNKS - 1)
                group_stats(CHUNKS - 2)
                group_stats(CHUNKS - 1)
                step.settle()
                dve.bn_aggr(bn_mv[:, :], bn_parts[:, :]).then_inc(G["bn_done"], 1)
                gate_tile(0, 0, first=True)
                step.base, step.k = step.base + step.k, 0
                gate_tile(1, 1)
                with dve.Fori(1, TILES // 2) as i:
                    step.enter(i - 1, 4)
                    for e in range(2):
                        gate_tile(i * 2 + e, e)
                    step.leave(TILES // 2 - 1)
                add_in(TILES - 1, 1)

            s0 = S[0]
            dve.wait_ge(bias_in, 48)
            dve.wait_ge(gates_ready, 2)
            split_biases()
            dve.wait_ge(x_in[0], 16)
            for l in range(2):
                s = S[l]
                if l == 1:
                    route()
                    heavy()
                    dve.wait_ge(mixed, BATCH)
                row_stats_of(s, 0, 0, step)
                normalize(s, 0, 0)
                if l == 0:
                    dve.wait_ge(x_in[1], 16)
                    dve.wait_ge(masks_in, 32)
                for b in range(BATCH):
                    dve.wait_ge(s["v_ps"], b + 1)
                    if l == 0:
                        dve.tensor_copy(v_all[:, b, :], mid[b % 2][:, 0:DIM]).then_inc(s["v_sb"], 1)
                    else:
                        dve.tensor_tensor(v_all[:, b, :], mid[b % 2][:, 0:DIM], v_bias[:, :], ALU.add).then_inc(s["v_sb"], 1)
                row_stats_of(s, 4, 1, step)
                normalize(s, 4, 1)
                dve.wait_ge(attn_w_in[l], 64)
                dve.tensor_scalar(Wo[l][:, :, :], Wo[l][:, :, :], gates[:, 2 * l:2 * l + 1], None, ALU.mult).then_inc(wo_ready, 1)
                dve.wait_ge(s["v_sb"], BATCH)
                dve.wait_ge(s["k_sb"], KH)
                key_value_diagonals(s, 0, True)
                for a in range(2):
                    for m in range(KH):
                        q_to_16(s, a, a, m)
                    if a == 0:
                        for j in range(8):
                            row_max(s, 0, j)
                if l == 0:
                    dve.wait_ge(x_in[2], 16)
                if l == 0:
                    gate_ffn0()
                    dve.wait_ge(route_in, 48)
                with dve.Fori(0, BATCH - 1) as b:
                    step.enter(b, 8 + (26 if l == 0 else 0))
                    for e in range(2):
                        chunk_step(s, b * 2 + e, e, b, True, True)
                        if l == 0:
                            route_stats_of(b * 2 + e)
                            route_logits_of(b * 2 + e)
                    step.leave(BATCH - 1)
                for e in range(2):
                    chunk_step(s, CHUNKS - 2 + e, e, BATCH - 1, False, e == 0)
                    if l == 0:
                        route_stats_of(CHUNKS - 2 + e)
                        route_logits_of(CHUNKS - 2 + e)
            gate_layer()

        @block.tensor
        def _(pe):
            def keys_values(s, l):
                for m in range(KH):
                    for k in range(KH):
                        mm = pe.matmul(front[m][:, 0:BATCH * KEYS], Wk[l][:, k, m * P:(m + 1) * P],
                                       ctxT[:, k, :, 0, :], start=(k == 0), stop=(k == KH - 1))
                    mm.then_inc(s["k_ps"], 1)
                for b in range(BATCH):
                    if b >= 2:
                        pe.wait_ge(s["v_sb"], b - 1)
                    for k in range(KH):
                        mm = pe.matmul(mid[b % 2][:, 0:DIM], ctxT[:, k, b, :, :].rearrange("p r n -> p (r n)"), Wv[l][:, k, :],
                                       start=(k == 0), stop=(k == KH - 1))
                    mm.then_inc(s["v_ps"], 1)

            def transpose_h(s, a):
                pe.wait_ge(s["h_ready"], a + 1)
                if not (isinstance(a, int) and a == 0):
                    pe.wait_ge(s["q_sb"], a * 2)
                for k in range(KH):
                    for t in range(CHUNK_TILES):
                        mm = pe.transpose(front[k][:, t * P:(t + 1) * P], h[:, t, k * P:(k + 1) * P], ident[:, :])
                mm.then_inc(s["hT_ps"], 1)

            def project_q(s, l, a, m):
                pe.wait_ge(s["hT_sb"], a * 2 + 2)
                for k in range(KH):
                    mm = pe.matmul(front[m][:, :], Wq[l][:, k, m * P:(m + 1) * P], hT[:, k, :],
                                   start=(k == 0), stop=(k == KH - 1))
                mm.then_inc(s["q_ps"], 1)

            def max_scores(s, l, n, first, b, j):
                t, m = j // 2, j % 2
                pe.wait_ge(s["q16_ready"], n * 2 + (m + 1))
                if j >= 2:
                    pe.wait_ge(s["max_done"], n * 8 + (j - 1))
                masked = l == 0 and first and t == 0
                mm = pe.matmul(mid[j % 2][:, :], q16[:, m, t * P:(t + 1) * P],
                               k16[:, ds(b, 1), m, :, :].rearrange("p a h k -> p (a h k)"), start=True, stop=not masked)
                if masked:
                    mm = pe.matmul(mid[j % 2][:, :], ident16[:, :], causal_rows16[:, :], start=False, stop=True)
                mm.then_inc(s["max_ps"], 1)

            def transpose_max(s, n):
                pe.wait_ge(s["max_done"], n * 8 + 8)
                if not (isinstance(n, int) and n == 0):
                    pe.wait_ge(s["s_exp"], n * 8 + FIRST)
                for t in range(CHUNK_TILES):
                    mm = pe.transpose(maxT_ps[:, t * P:(t + 1) * P], max16[:, t, :], ident16[:, :])
                mm.then_inc(s["maxT_ps"], 1)

            def scores(s, l, c, e, p):
                m = p // 4
                if p == 0:
                    pe.wait_ge(s["maxT_sb"], c + 1)
                if p % 4 == 0:
                    pe.wait_ge(s["q_sb"], c * 2 + (m + 1))
                if not (isinstance(c, int) and c == 0 and p < 2):
                    pe.wait_ge(s["s_exp"], (c * 8 + (p - 1) if p else c * 8) + FIRST)
                out = score[p % 2][:, :]
                pe.matmul(out, k_diag[:, m, 2 * (p % 4):2 * (p % 4) + 2, :].rearrange("p h k -> p (h k)"), qT[e][:, m, :],
                          start=True, stop=False)
                masked = l == 0 and e == 0
                if masked:
                    pe.matmul(score[p % 2][:, 0:KEYS], ident16[:, :], causal_keys16[:, :], start=False, stop=False)
                pe.matmul(out, neg_sel16[:, p, :], maxT16[:, :], start=False, stop=True).then_inc(s["s_ps"], 1)

            def weigh_values(s, c, p):
                m, r = p // 4, 32 * (p % 4)
                pe.wait_ge(s["s_exp"], c * 8 + (p + 1) + FIRST)
                if p % 4 == 0:
                    pe.wait_ge(s["y_ready"], c * 2 + m + FIRST)
                pe.matmul(YB[r:r + 32, :], v_diag[:, 2 * p:2 * p + 2, :].rearrange("p h d -> p (h d)"), probs[:, p % 4, :],
                          start=True, stop=True)
                pe.matmul(DB[r:r + 32, :], pair_mask[:, 0:2, :].rearrange("p h d -> p (h d)"), probs[:, p % 4, :],
                          start=True, stop=True).then_inc(s["pv"], 1)

            def project_out(s, l, c):
                pe.wait_ge(s["y_ready"], c * 2 + 2 + FIRST)
                for g in range(2):
                    for i in range(2):
                        t = 2 * g + i
                        out = mid[g][:, i * DIM:(i + 1) * DIM]
                        for m in range(KH):
                            pe.matmul(out, yT[:, m, t * P:(t + 1) * P], Wo[l][:, m, :], start=(i == 0 and m == 0), stop=False,
                                      skip_group_check=True)
                        mm = pe.matmul(out, ones16[:, :], bias3[:, l, :], start=False, stop=(i == 1),
                                       skip_group_check=True)
                    mm.then_inc(s["o_ps"], 1)

            def chunk_step(s, l, c, e, b, ahead, nxt):
                for p in range(PAIRS):
                    if p == 0 and e == 0:
                        pe.wait_ge(s["kv_diag"], b * 3 + 3)
                    scores(s, l, c, e, p)
                    if nxt:
                        if p < 2 and not (isinstance(c, int) and c == 0):
                            pe.wait_ge(s["x_new"], c * 2 + FIRST)
                        max_scores(s, l, c + 1, e == 1, b + 1 if e == 1 else b, p)
                    if p >= 2:
                        weigh_values(s, c, p - 2)
                    if p == 2 and ahead:
                        transpose_h(s, c + 2)
                    if p == 5 and ahead:
                        project_q(s, l, c + 2, 0)
                for p in range(PAIRS - 2, PAIRS):
                    weigh_values(s, c, p)
                if nxt:
                    transpose_max(s, c + 1)
                if ahead:
                    project_q(s, l, c + 2, 1)
                if nxt:
                    pe.wait_ge(s["max_done"], c * 8 + 16)
                elif not (isinstance(c, int) and c == 0):
                    pe.wait_ge(s["x_new"], c * 2 + FIRST)
                project_out(s, l, c)

            def cross_max(n):
                pe.wait_ge(cross_in, n + 1)
                pe.transpose(YB[0:BATCH, 0:P], part_sum[:, :], ident[:, :]).then_inc(cross_ps, 1)
                pe.wait_ge(cross_diag, n + 1)
                pe.matmul(YB[:, P:P + BATCH], ones4[:, :], diag4[:, :], start=True, stop=True).then_inc(cross_out, 1)

            def sum_parts(n):
                pe.wait_ge(part_ready, n)
                pe.matmul(DB[:, 0:BATCH], eighth[:, :], part_sum[:, :], start=True, stop=True).then_inc(sum_ready, 1)

            def light_piece(n, j):
                if j == 0:
                    pe.wait_ge(copied, n + 1)
                    pe.wait_ge(light_Tsb, n * 2 + FIRST)
                    for k in range(KH):
                        for t in range(CHUNK_TILES):
                            mm = pe.transpose(front[k][:, t * P:(t + 1) * P], h[:, t, k * P:(k + 1) * P], ident[:, :])
                    mm.then_inc(light_T, 1)
                elif j == 1:
                    pe.wait_ge(light_Tsb, n * 2 + 2 + FIRST)
                    pe.wait_ge(light_g, n + FIRST)
                    for k in range(KH):
                        mm = pe.matmul(mid[0][:, :], w1l[:, k, :], hT[:, k, :], start=(k == 0), stop=(k == KH - 1))
                    mm.then_inc(light_h, 1)
                else:
                    t = j - 2
                    if t == 0:
                        pe.wait_ge(light_g, n + 1 + FIRST)
                    if t % 2 == 0:
                        pe.wait_ge(light_added, (n * 2 + (t // 2 - 1) if t else n * 2) + FIRST)
                    out = score[t // 2][:, (t % 2) * DIM:(t % 2 + 1) * DIM]
                    pe.matmul(out, light_gT[:, t * P:(t + 1) * P], w2l[:, :], start=(t % 2 == 0), stop=False, skip_group_check=True)
                    mm = pe.matmul(out, ones16[:, :], bias3[:, B2_LIGHT, :], start=False, stop=(t % 2 == 1),
                                   skip_group_check=True)
                    if t % 2 == 1:
                        mm.then_inc(light_o, 1)

            def prefix(n):
                pe.wait_ge(flags_ready, n + 1)
                out, flags = M0[:, 0:TILES].rearrange("p (b c) -> p b c", b=BATCH), flag16[:, :].rearrange("p (b c) -> p b c", b=BATCH)
                mm = pe.matmul(out, before16[:, :], flags, start=True, stop=False, skip_group_check=True)
                for d in range(1, 8):
                    mm = pe.matmul(out[:, :, d:8], ones16[:, :], flags[:, :, 0:8 - d], start=False, stop=(d == 7),
                                   skip_group_check=True)
                if n == 0:
                    mm = pe.matmul(M1[:, 0:BATCH], ones16[:, :], count16[:, :], start=True, stop=True)
                mm.then_inc(prefix_ready, 1)

            def ffn0():
                cross_max(0)
                pe.wait_ge(logit_ready, CHUNKS)
                for b in range(BATCH):
                    for i in range(2):
                        if b:
                            pe.wait_ge(rows_sb, 2 * b + i - 1)
                        for t in range(4):
                            mm = pe.matmul(score[i][:, t * P:(t + 1) * P],
                                           logit[:, 8 * b + 4 * i + t:8 * b + 4 * i + t + 1].to_broadcast([P, P]),
                                           ident[:, :], start=True, stop=True)
                        mm.then_inc(rows_ps, 1)
                pe.wait_ge(rows_sb, 2 * BATCH)
                pe.wait_ge(ffn0_ready, 5)
                pe.wait_ge(bias_ready, 48)
                for n, iters in enumerate(ROUTE_BLOCKS):
                    sum_parts(sums_before[n] + 1)
                    with pe.Fori(0, 2) as i:
                        for j in range(CHUNK_ITERS):
                            sum_parts(i * CHUNK_ITERS + (sums_before[n] + 2 + j))
                            light_piece(i + 2 * n, j)
                    for j in range(2 * CHUNK_ITERS, iters):
                        sum_parts(sums_before[n] + 2 + j)
                cross_max(1)
                prefix(0)
                prefix(1)
                with pe.Fori(0, BATCH // 2) as i:
                    for e in range(2):
                        b = i * 2 + e
                        pe.wait_ge(picked_in, b * 16 + 16)
                        pe.wait_ge(heavy_Tsb, b + FIRST)
                        for k in range(KH):
                            for j in range(2):
                                mm = pe.transpose(F0[:, (2 * k + j) * P:(2 * k + j + 1) * P],
                                                  picked[e][:, j, k * P:(k + 1) * P], ident[:, :])
                        mm.then_inc(heavy_T, 1)
                        pe.wait_ge(heavy_Tsb, b + 1 + FIRST)
                        for m in range(HEAVY // P):
                            if m >= 4:
                                pe.wait_ge(heavy_g, b * 8 + (m - 3))
                            for k in range(KH):
                                mm = pe.matmul(heavy_banks[m % 4][:, 0:ROUTED], w1h[:, k, m * P:(m + 1) * P], pickedT[:, k, :],
                                               start=(k == 0), stop=(k == KH - 1))
                            mm.then_inc(heavy_h, 1)
                        pe.wait_ge(heavy_g, b * 8 + 8)
                        pe.wait_ge(heavy_done, b + FIRST)
                        for j in range(2):
                            out = YB[:, j * DIM:(j + 1) * DIM]
                            for m in range(HEAVY // P):
                                pe.matmul(out, heavy_gT[:, m, j * P:(j + 1) * P], w2h[:, m, :], start=(j == 0 and m == 0),
                                          stop=False, skip_group_check=True)
                            mm = pe.matmul(out, ones16[:, :], bias3[:, B2_HEAVY, :], start=False, stop=(j == 1),
                                           skip_group_check=True)
                        mm.then_inc(heavy_o, 1)

            pe.wait_ge(ctx_in, 64)
            pe.wait_ge(consts_in, 80)
            pe.wait_ge(set_ready, 6)
            for l in range(2):
                s = S[l]
                if l == 1:
                    ffn0()
                pe.wait_ge(attn_w_in[l], 64)
                keys_values(s, l)
                pe.wait_ge(s["k_sb"], KH)
                for a in range(2):
                    transpose_h(s, a)
                    for m in range(KH):
                        project_q(s, l, a, m)
                    if a == 0:
                        pe.wait_ge(s["k16_ready"], BATCH * KH)
                        pe.wait_ge(s["v_sb"], BATCH)
                        for j in range(8):
                            max_scores(s, l, 0, True, 0, j)
                        transpose_max(s, 0)
                pe.wait_ge(wo_ready, l + 1)
                pe.wait_ge(bias_ready, 48)
                with pe.Fori(0, BATCH - 1) as b:
                    for e in range(2):
                        chunk_step(s, l, b * 2 + e, e, b, True, True)
                for e in range(2):
                    chunk_step(s, l, CHUNKS - 2 + e, e, BATCH - 1, False, e == 0)
            pe.wait_ge(gate_in, 64)
            with pe.Fori(0, CHUNKS) as c:
                pe.wait_ge(G["h_ready"], c + 1)
                pe.wait_ge(G["hT_sb"], c * 2 + FIRST)
                for k in range(KH):
                    for t in range(CHUNK_TILES):
                        mm = pe.transpose(front[k][:, t * P:(t + 1) * P], h[:, t, k * P:(k + 1) * P], ident[:, :])
                mm.then_inc(G["hT_ps"], 1)
                pe.wait_ge(G["hT_sb"], c * 2 + 2 + FIRST)
                pe.wait_ge(G["sums_sb"], c + FIRST)
                for k in range(KH):
                    mm = pe.matmul(M0[:, :], conv_bd[:, k, :], hT[:, k, :], start=(k == 0), stop=(k == KH - 1))
                mm.then_inc(G["sums_ps"], 1)
            pe.wait_ge(gate_ready, 1)

            def prepare(t, e):
                pe.wait_ge(G["hs_ready"], t + 1)
                pe.wait_ge(G["hsT_sb"], t)
                for k in range(KH):
                    mm = pe.transpose(F0[:, k * P:(k + 1) * P], hs[e][:, k * P:(k + 1) * P], ident[:, :])
                mm.then_inc(G["hsT_ps"], 1)
                pe.wait_ge(G["acts_ready"], t + 1)
                if not (isinstance(t, int) and t == 0):
                    pe.wait_ge(G["exp_ready"], t * 2 - 2 + FIRST)
                pe.matmul(mid[e][:, :], acts[e], lin_bd[:, :], start=True, stop=False)
                pe.matmul(mid[e][:, :], ones16[:, :], bias3[:, SO_B:SO_B + 2, :].rearrange("p a d -> p (a d)"),
                          start=False, stop=True).then_inc(G["logit_ps"], 1)
                pe.wait_ge(G["hsT_sb"], t + 1)
                if not (isinstance(t, int) and t == 0):
                    pe.wait_ge(G["part_ready"], t - 1 + FIRST)
                for k in range(KH):
                    mm = pe.matmul(score[e][:, 0:DIM], hsT[e][:, k, :], gate_w[:, k, :], start=(k == 0), stop=(k == KH - 1))
                mm.then_inc(G["full_ps"], 1)

            def gate_tile(t, e, ahead):
                if ahead:
                    prepare(t + 1, 1 - e)
                pe.wait_ge(G["sparse_ready"], t + 1)
                pe.wait_ge(G["sparseT_sb"], t + FIRST)
                for k in range(KH):
                    mm = pe.transpose(F1[:, k * P:(k + 1) * P], sparse[:, k * P:(k + 1) * P], ident[:, :])
                mm.then_inc(G["sparseT_ps"], 1)
                pe.wait_ge(G["sparseT_sb"], t + 1 + FIRST)
                pe.wait_ge(G["x_new"], t + FIRST)
                for k in range(KH):
                    pe.matmul(out_banks[e][:, 0:DIM], sparseT[:, k, :], gate_w[:, k, :], start=(k == 0), stop=False)
                pe.matmul(out_banks[e][:, 0:DIM], ones16[:, :], bias3[:, BIAS1, :], start=False, stop=True).then_inc(G["in_ps"], 1)

            prepare(0, 0)
            with pe.Fori(0, TILES // 2 - 1) as i:
                for e in range(2):
                    gate_tile(i * 2 + e, e, True)
            for e in range(2):
                gate_tile(TILES - 2 + e, e, e == 0)


def host_arrays(inp):
    import numpy as np
    f = lambda a: np.ascontiguousarray(np.asarray(a))
    bf16_bits = lambda a: (np.ascontiguousarray(a, np.float32).view(np.uint32) >> 16).astype(np.uint16)
    r = np.arange(P)
    col = np.arange(512)
    d = {"x": f(inp["x"]).reshape(BATCH * TOKENS, DIM), "ctxT": f(np.asarray(inp["ctx_1024"]).reshape(-1, DIM).T)}
    for l in range(2):
        for w in "qkvo":
            d[f"W{w}{l}"] = f(np.asarray(inp[f"L{l}_xattn_W{w}"]).T)
    d["gates"] = np.stack([np.asarray(inp["g_xattn"])[0], np.asarray(inp["g_ffn"])[0],
                           np.asarray(inp["g_xattn"])[1], np.asarray(inp["g_ffn"])[1]])
    d["qk_bias"] = f(np.concatenate([np.asarray(inp["L1_xattn_bq"]).reshape(KH, P),
                                     np.asarray(inp["L1_xattn_bk"]).reshape(KH, P)]).T)
    d["bv1"] = f(inp["L1_xattn_bv"])
    d["bias_rows"] = np.stack([np.asarray(inp[n]) for n in (
        "L0_xattn_bo", "L1_xattn_bo", "L0_ffn_b2_light", "L1_ffn_bias", "L0_ffn_b2_heavy", "L1_ffn_so_lin_b", "L1_ffn_si_lin_b")])
    d["bias_gates"] = d["gates"][[0, 2, 1, 3]].reshape(4, 1)
    d["ident"] = np.eye(P, dtype=np.float32)
    d["ident16"] = bf16_bits(np.eye(P))
    d["head_mask"] = (r[:, None] // HEAD_DIM == col[None, :] // KEYS).astype(np.float32)
    d["pair_mask"] = (r[:, None] // KEYS == (np.arange(DIM)[None, :] // HEAD_DIM) % 2).astype(np.float32)
    pair = np.arange(PAIRS)[None, :, None]
    d["neg_sel16"] = bf16_bits(-1.0 * (r[:, None, None] == 2 * pair + r[None, None, :] // KEYS)).reshape(P, -1)
    d["causal_rows16"] = bf16_bits(np.where(col[None, :] % KEYS > r[:, None], -1e30, 0.0))
    d["causal_keys16"] = bf16_bits(np.where(r[:, None] % KEYS > np.arange(KEYS)[None, :], -1e30, 0.0))
    tile = np.arange(TILES)[None, :]
    outside = BATCH * TOKENS + tile * P + r[:, None]
    d["slot_base"] = np.concatenate([-outside, outside], 1).astype(np.float32)
    d["before16"] = bf16_bits(r[:, None] < r[None, :])
    d["token"] = f(inp["L0_ffn_routing_token"])
    cols = lambda a: np.asarray(a).reshape(-1, P).T
    d["ffn0_cols"] = f(np.concatenate([cols(inp["L0_ffn_gamma_light"]), cols(inp["L0_ffn_gamma_heavy"]),
                                       cols(inp["L0_ffn_b1_light"]), cols(inp["L0_ffn_b1_heavy"])], 1))
    for a, b in (("w1l", "w1_light"), ("w2l", "w2_light"), ("w1h", "w1_heavy"), ("w2h", "w2_heavy")):
        d[a] = f(inp["L0_ffn_" + b])
    conv, lin = np.zeros((DIM, P), np.float32), np.zeros((P, 2 * DIM), np.float32)
    feature = np.arange(DIM)
    for i, br in enumerate(("so", "si")):
        conv[feature, i * GROUPS + feature // 4] = np.asarray(inp[f"L1_ffn_{br}_conv_w"]).reshape(-1)
        lin[i * GROUPS:(i + 1) * GROUPS, i * DIM:(i + 1) * DIM] = np.asarray(inp[f"L1_ffn_{br}_lin_w"]).T
    d["conv_bd"], d["lin_bd"], d["gate_w"] = conv, lin, f(inp["L1_ffn_weight"])
    d["bn_cols"] = f(np.stack([np.concatenate([np.asarray(inp[f"L1_ffn_{br}_{n}"]) for br in ("so", "si")])
                               for n in ("conv_b", "gamma", "beta")], 1))
    return d


def kernel(**inputs):
    import concourse.bacc as bacc
    from concourse.bass_utils import run_bass_kernel_spmd

    nc = bacc.Bacc("TRN2", target_bir_lowering=False, num_devices=1)
    arrays = host_arrays(inputs)
    A = {n: nc.dram_tensor(f"in_{n}", a.shape, mybir.dt.from_np(a.dtype), kind="ExternalInput").ap()
         for n, a in arrays.items()}
    A["out"] = nc.dram_tensor("out", (BATCH * TOKENS, DIM), F32, kind="ExternalOutput").ap()
    build(nc, A)
    r = run_bass_kernel_spmd(nc, [{f"in_{n}": a for n, a in arrays.items()}], core_ids=[0])
    return r.results[0]["out"].reshape(BATCH, TOKENS, DIM)
```

```python
import math
from contextlib import ExitStack

import concourse.bass as bass
from concourse import mybir

F32 = mybir.dt.float32
BF16 = mybir.dt.bfloat16
U32 = mybir.dt.uint32
ALU = mybir.AluOpType
ACT = mybir.ActivationFunctionType
AX_X = mybir.AxisListType.X
ds = bass.ds

P = 128
BATCH, TOKENS, DIM = 4, 1024, 256
KEYS, HEADS, HEAD_DIM = 64, 16, 16
KH = DIM // P
TILES = BATCH * TOKENS // P
CHUNK_TILES = 4
CHUNK = CHUNK_TILES * P
CHUNKS = TILES // CHUNK_TILES
PAIRS = HEADS // 2
SCALE = HEAD_DIM ** -0.5
LN_EPS = 1e-5

LIGHT, HEAVY = 128, 1024
ROUTED = 256
ROUTE_ITERS, ROUTE_K, ROUTE_EPS = 50, 8.0, 0.1
TOPK = 32
FOUND = -1e30
LOG_TINY = -87.33654
LOG_SHIFT = 40
GROUPS = DIM // 4
BN_EPS = 1e-5
FIRST = 1


class Chain:

    def __init__(self, eng, sem):
        self.eng, self.sem, self.base, self.k, self.i, self.per = eng, sem, 0, 0, None, 0

    def did(self, ins):
        ins.then_inc(self.sem, 1)
        self.k += 1
        return ins

    def at(self):
        return self.base + self.k if self.i is None else self.i * self.per + (self.base + self.k)

    def settle(self):
        self.eng.wait_ge(self.sem, self.at())

    def enter(self, i, per):
        self.base, self.k, self.i, self.per = self.base + self.k, 0, i, per

    def leave(self, trips):
        assert self.k == self.per, (self.k, self.per)
        self.base, self.k, self.i = self.base + trips * self.per, 0, None


def build(nc, A):
    with ExitStack() as ctx:
        def sb(name, shape, dt=F32):
            return ctx.enter_context(nc.sbuf_tensor(name, shape, dt))

        def sem(name):
            return ctx.enter_context(nc.semaphore(name))

        x = sb("x", [P, TILES, DIM])
        def parts(name, widths, dt=F32):
            whole, at0, views = sb(name, [P, sum(widths)], dt), 0, []
            for w in widths:
                views.append(whole[:, at0:at0 + w])
                at0 += w
            return whole, views

        consts, (ident, head_mask, pair_mask, slot_base, qkv_bias, ffn0_cols, bn_cols) = parts(
            "consts", [P, 8 * KEYS, DIM, 2 * TILES, 4, 13, 3])
        head_mask = head_mask.rearrange("p (h k) -> p h k", h=8)
        pair_mask = pair_mask.rearrange("p (h d) -> p h d", h=HEADS)
        slot_base = slot_base.rearrange("p (a n) -> p a n", a=2)
        consts16, (ident16, neg_sel16, causal_rows16, causal_keys16, before16) = parts(
            "consts16", [P, PAIRS * P, 512, KEYS, P], BF16)
        neg_sel16 = neg_sel16.rearrange("p (a n) -> p a n", a=PAIRS)
        ctx_all, (ctxT,) = parts("ctx_all", [KH * BATCH * 2 * KEYS])
        ctxT = ctxT.rearrange("p (k b r n) -> p k b r n", k=KH, b=BATCH, r=2)
        kvqo, Wk, Wv, Wq, Wo = [], [], [], [], []
        for l in range(2):
            whole, views = parts(f"kvqo{l}", [KH * DIM] * 4)
            kvqo.append(whole)
            for w, v in zip((Wk, Wv, Wq, Wo), views):
                w.append(v.rearrange("p (k n) -> p k n", k=KH))
        light_w, (w1l, w2l) = parts("light_w", [KH * LIGHT, DIM])
        w1l = w1l.rearrange("p (k n) -> p k n", k=KH)
        heavy_w, (w1h, w2h) = parts("heavy_w", [KH * HEAVY, HEAVY // P * DIM])
        w1h, w2h = w1h.rearrange("p (k n) -> p k n", k=KH), w2h.rearrange("p (m n) -> p m n", m=HEAVY // P)
        gate_all, (conv_bd, gate_w, lin_bd) = parts("gate_all", [KH * P, KH * DIM, 2 * DIM])
        conv_bd, gate_w = (w.rearrange("p (k n) -> p k n", k=KH) for w in (conv_bd, gate_w))
        ones16 = sb("ones16", [P, P], BF16)
        gates = sb("gates", [P, 4])
        v_bias, bias1 = sb("v_bias", [P, DIM]), sb("bias1", [P, DIM])
        BO0, BO1, B2_LIGHT, B2_HEAVY, SO_B, SI_B = range(6)
        bias_rows = sb("bias_rows", [6, DIM])
        bias_gates = sb("bias_gates", [3, 1])
        bias_piece = [sb(f"bias_piece{k}", [6, DIM], BF16) for k in range(3)]
        bias3 = sb("bias3", [P, 6, DIM], BF16)
        arena = sb("arena", [P, 14592])

        def at(first, words, pattern=None, **sizes):
            flat = arena[:, first:first + words]
            return flat.rearrange(pattern, **sizes) if pattern else flat

        Q, DEN, PROBS, YT, H, HT, K16, KT, VALL, KD, Q16, VD = 0, 2048, 4096, 6144, 7168, 8192, 9216, 11264, 11776, 12800, 13824, 14336
        qT = [at(Q + i * 1024, 1024, "p (m n) -> p m n", m=KH) for i in range(2)]
        log_den = at(DEN, 1024, "p (m n) -> p m n", m=KH)
        inv_den = at(DEN + 1024, 1024, "p (m n) -> p m n", m=KH)
        probs = at(PROBS, 2048, "p (a n) -> p a n", a=4)
        yT = at(YT, 1024, "p (m n) -> p m n", m=KH)
        h = at(H, 1024, "p (t d) -> p t d", t=CHUNK_TILES)
        hT = at(HT, 1024, "p (m n) -> p m n", m=KH)
        k16 = at(K16, 2048).bitcast(BF16).rearrange("p (b m h k) -> p b m h k", b=BATCH, m=KH, h=8)
        kT = at(KT, 512, "p (m b k) -> p m b k", m=KH, b=BATCH)
        v_all = at(VALL, 1024, "p (b d) -> p b d", b=BATCH)
        k_diag = at(KD, 1024, "p (m h k) -> p m h k", m=KH, h=8)
        q16 = at(Q16, 512).bitcast(BF16).rearrange("p (m n) -> p m n", m=KH)
        v_diag = at(VD, 256, "p (h d) -> p h d", h=HEADS)
        logit_rows = at(Q, 4096, "p (b n) -> p b n", b=BATCH)
        heavy_gT = at(PROBS, 2048, "p (m n) -> p m n", m=HEAVY // P)
        light_gT = at(YT, 512)
        larger16 = [at(first + i * 512, 512).bitcast(BF16) for first in (KD, PROBS) for i in range(2)]
        picked = [at(Q + i * 514, 514, "p (j d) -> p j d", j=2) for i in range(2)]
        pickedT = at(Q + 1028, 512, "p (k n) -> p k n", k=KH)
        heavy_y = [at(DEN + i * 512, 512, "p (j d) -> p j d", j=2) for i in range(2)]
        row_stats = sb("row_stats", [P, CHUNK_TILES, 6])
        mean_var = sb("mean_var", [P, CHUNK_TILES, 2])
        var_eps = sb("var_eps", [P, CHUNK_TILES])
        minus_half = sb("minus_half", [P, CHUNK_TILES])
        rstd = sb("rstd", [P, CHUNK_TILES])
        max16 = sb("max16", [P, CHUNK_TILES, HEADS], BF16)
        maxT16 = sb("maxT16", [P, CHUNK], BF16)
        token_row = sb("token_row", [P, DIM])
        ROW = DIM + 1
        normed = sb("normed", [P, TILES, ROW])
        big = sb("big", [P, BATCH * TOKENS])
        heavy_rows = [big[:, i * 8 * DIM:(i + 1) * 8 * DIM].rearrange("p (t d) -> p t d", t=8) for i in range(2)]
        route_stats = sb("route_stats", [P, CHUNK_TILES, 6])
        route_mv = sb("route_mv", [P, CHUNK_TILES, 2])
        route_var = sb("route_var", [P, 6, CHUNK_TILES])
        row_scale = sb("row_scale", [P, CHUNK_TILES])
        row_norm = sb("row_norm", [P, TILES])
        raw_dot = sb("raw_dot", [P, CHUNK_TILES])
        dot_out = sb("dot_out", [P, DIM])
        logit = sb("logit", [P, TILES])
        level = sb("level", [P, BATCH])
        top_logit = sb("top_logit", [P, BATCH])
        minus_a = sb("minus_a", [P, BATCH])
        log_sum = sb("log_sum", [P, BATCH])
        args = sb("args", [P, TILES + BATCH])
        exps = sb("exps", [P, TILES + BATCH])
        capped = sb("capped", [P, TILES])
        part_sum = sb("part_sum", [P, BATCH])
        eighth = sb("eighth", [P, P])
        diag4 = sb("diag4", [4, BATCH])
        col4 = sb("col4", [4, 1])
        ones4 = sb("ones4", [4, P])
        score_of = sb("score_of", [P, TILES])
        pick = sb("pick", [P, 4, TILES])
        flag16 = sb("flag16", [P, TILES], BF16)
        count16 = sb("count16", [P, BATCH], BF16)
        slot = sb("slot", [P, TILES], U32)
        pick_gate = sb("pick_gate", [P, 2])
        rows_in = [nc.dram_tensor(f"rows_in{b}", (ROUTED, ROW), F32, kind="Internal").ap() for b in range(BATCH)]
        rows_out = [nc.dram_tensor(f"rows_out{b}", (ROUTED, DIM), F32, kind="Internal").ap() for b in range(BATCH)]

        groups = big[:, :]
        bn_parts = sb("bn_parts", [P, CHUNKS * 6])
        bn_mv = sb("bn_mv", [P, 2])
        bn_tmp = sb("bn_tmp", [P, 5])
        rows2 = [at(first, 1024, "p (t d) -> p t d", t=CHUNK_TILES) for first in (H, PROBS)]
        rowsT2 = [at(first, 1024, "p (m n) -> p m n", m=KH) for first in (HT, DEN)]
        hs = [at(i * 256, 256) for i in range(2)]
        hsT = [at(512 + i * 256, 256, "p (k n) -> p k n", k=KH) for i in range(2)]
        acts = [at(1024 + i * 128, 128) for i in range(2)]
        work = [at(1280 + i * 512, 512) for i in range(2)]
        expw = [at(first, 512) for first in (2304, 4096)]
        taken = at(2816, 512)
        out_part = at(3328, 256)
        sparse = at(3584, 256)
        sparseT = at(3840, 256, "p (k n) -> p k n", k=KH)
        top8 = sb("top8", [P, 4, 2, 8])
        zeros16 = sb("zeros16", [P, TILES], BF16)
        minus_top = sb("minus_top", [P, 2])
        exp_sum = sb("exp_sum", [P, 2])
        inv_sum = [sb(f"inv_sum{i}", [P, 2]) for i in range(2)]
        bank = [ctx.enter_context(nc.psum_tensor(f"bank{i}", [P, 512], F32)) for i in range(8)]
        F0, F1, M0, M1, S0, S1, YB, DB = bank
        front = [F0, F1]
        mid = [M0, M1]
        score = [S0, S1]
        out_banks = [YB, DB]
        rowsT_banks = [front, score]
        heavy_banks = [M0, M1, S0, S1]
        CHUNK_ITERS = 6
        COUNT_SLOTS = [1, 2, 3, 5]
        ROUTE_BLOCKS = [12, 12, 12, 14]
        assert sum(ROUTE_BLOCKS) == ROUTE_ITERS and len(ROUTE_BLOCKS) == BATCH
        sums_before = [sum(ROUTE_BLOCKS[:n]) + n for n in range(BATCH + 1)]
        counts_ps = M1[:, 0:TILES]
        maxT_ps = S0[0:HEADS, 0:CHUNK // 2].bitcast(BF16)

        x_in = [sem(f"x_in{i}") for i in range(3)]
        ctx_in, gates_in, consts_in, consts16_in, kv_in = (sem(n) for n in ("ctx_in", "gates_in", "consts_in", "consts16_in", "kv_in"))
        attn_w_in = [sem(f"attn_w_in{l}") for l in range(2)]
        bias_in = sem("bias_in")
        gates_ready, set_ready, wo_ready = sem("gates_ready"), sem("set_ready"), sem("wo_ready")
        pieces_ready, bias_ready = sem("pieces_ready"), sem("bias_ready")
        dve_step, pool_step, act_step = sem("dve_step"), sem("pool_step"), sem("act_step")
        top_step = sem("top_step")
        out_done, waits_taken = sem("out_done"), sem("waits_taken")
        names = ("k_ps k_sb k16_ready v_ps v_sb stats rstd_ready h_ready hT_ps hT_sb q_ps q_sb q16_ready "
                 "max_ps max_done maxT_ps maxT_sb s_ps s_exp pv inv_ready y_ready o_ps x_new kv_diag").split()
        ffn0_in, route_in = sem("ffn0_in"), sem("route_in")
        ffn0_ready = sem("ffn0_ready")
        route_stats_ready, scale_ready, logit_ready = sem("route_stats_ready"), sem("scale_ready"), sem("logit_ready")
        rows_ps, rows_sb = sem("rows_ps"), sem("rows_sb")
        compared, counted = [sem("compared_pool"), sem("compared_dve")], sem("counted")
        cross_in, cross_ps, cross_col, cross_diag, cross_out = (sem(n) for n in ("cross_in", "cross_ps", "cross_col", "cross_diag", "cross_out"))
        part_ready, sum_ready, log_ready, args_ready, exps_ready = (sem(n) for n in ("part_ready", "sum_ready", "log_ready", "args_ready", "exps_ready"))
        score_arg, score_ready = sem("score_arg"), sem("score_ready")
        flags_ready, prefix_ready, slot_ready = sem("flags_ready"), sem("prefix_ready"), sem("slot_ready")
        copied, light_T, light_Tsb, light_h, light_g, light_o, light_added = (
            sem(n) for n in ("copied", "light_T", "light_Tsb", "light_h", "light_g", "light_o", "light_added"))
        scattered = [sem(f"scattered{b}") for b in range(BATCH)]
        picked_in, stored = sem("picked_in"), sem("stored")
        gathered = [sem(f"gathered{b}") for b in range(BATCH)]
        heavy_room = sem("heavy_room")
        heavy_T, heavy_Tsb, heavy_h, heavy_g, heavy_o, heavy_done, mixed = (
            sem(n) for n in ("heavy_T", "heavy_Tsb", "heavy_h", "heavy_g", "heavy_o", "heavy_done", "mixed"))
        S = [{n: sem(f"{n}_{l}") for n in names} for l in range(2)]
        gate_in, gate_ready = sem("gate_in"), sem("gate_ready")
        G = {n: sem(f"g_{n}") for n in (
            "stats rstd_ready h_ready copied bias_added hT_ps hT_sb sums_ps sums_sb bn_done bn_ready hs_ready acts_ready hsT_ps hsT_sb "
            "logit_ps full_ps work_ready top_done minus_ready exp_ready top_ready taken_ready part_ready sparse_ready sparseT_ps "
            "sparseT_sb in_ps part_added x_new").split()}

        start_at_first = (
            [s[n] for s in S for n in ("s_exp", "x_new", "y_ready")] +
            [G[n] for n in ("part_ready", "sparseT_ps", "sums_sb", "x_new")] +
            [heavy_Tsb, heavy_done, heavy_h, heavy_o, light_o])

        block = ctx.enter_context(nc.Block())

        x_dram = A["x"].rearrange("(n p) d -> p n d", p=P)
        out_dram = A["out"].rearrange("(n p) d -> p n d", p=P)

        def halves(w):
            return w.rearrange("(k p) n -> p k n", p=P)

        def plain(eng):
            eng.sem_inc(waits_taken, 1)

        @block.sync
        def _(sp):
            sp.dma_start(x[:, 0:4, :], x_dram[:, 0:4, :]).then_inc(x_in[0], 16)
            sp.dma_start(ctx_all[:, :], A["ctxT"]).then_inc(ctx_in, 16)
            HALF = 2 * KH * DIM
            sp.dma_start(kvqo[0][:, 0:HALF], A["kvqo0"][:, 0:HALF]).then_inc(kv_in, 16)
            sp.dma_start(kvqo[0][:, HALF:], A["kvqo0"][:, HALF:]).then_inc(attn_w_in[0], 16)
            sp.dma_start(x[:, 4:8, :], x_dram[:, 4:8, :]).then_inc(x_in[1], 16)
            sp.dma_start(x[:, 8:TILES, :], x_dram[:, 8:TILES, :]).then_inc(x_in[2], 16)
            sp.dma_start(light_w[:, :], A["light_w"]).then_inc(ffn0_in, 16)
            sp.dma_start(heavy_w[:, :], A["heavy_w"]).then_inc(ffn0_in, 16)
            sp.dma_start(kvqo[1][:, :], A["kvqo1"]).then_inc(attn_w_in[1], 16)
            sp.dma_start(gate_all[:, :], A["gate_all"]).then_inc(gate_in, 16)
            sp.wait_ge(pieces_ready, 1)
            for k in range(3):
                sp.dma_start(bias3[k:k + 1, :, :].rearrange("p j d -> p (j d)"), bias_piece[k][:, :]).then_inc(bias_ready, 16)

            def load_picked(b):
                sp.wait_ge(scattered[b], 16 * 8)
                if b >= 2:
                    sp.wait_ge(heavy_T, b - 1)
                    sp.wait_ge(heavy_done, b - 1 + FIRST)
                sp.dma_start(picked[b % 2][:, :, :], rows_in[b].rearrange("(j p) d -> p j d", p=P))\
                  .then_inc(picked_in, 16)
                sp.wait_ge(picked_in, 16 * (b + 1))

            def store_heavy(b):
                sp.wait_ge(heavy_done, b + 1 + FIRST)
                sp.dma_start(rows_out[b].rearrange("(j p) d -> p j d", p=P), heavy_y[b % 2][:, :, :])\
                  .then_inc(stored, 16)
                sp.wait_ge(stored, 16 * (b + 1))
                sp.sem_inc(heavy_room, 1)

            sp.sem_inc(heavy_room, 2)
            load_picked(0)
            load_picked(1)
            for b in range(BATCH):
                store_heavy(b)
                if b + 2 < BATCH:
                    load_picked(b + 2)
            for b in range(BATCH):
                sp.wait_ge(G["x_new"], 8 * (b + 1) + FIRST)
                sp.dma_start(out_dram[:, 8 * b:8 * b + 8, :], x[:, 8 * b:8 * b + 8, :]).then_inc(out_done, 16)
            sp.wait_ge(out_done, 16 * BATCH)

        @block.gpsimd
        def _(pool):
            for first in start_at_first:
                pool.sem_inc(first, FIRST)
            step = Chain(pool, pool_step)
            pool.memset(minus_half[:, :], -0.5).then_inc(set_ready, 1)
            pool.memset(ones16[:, :], 1.0).then_inc(set_ready, 1)
            pool.memset(maxT16[:, :], 0.0).then_inc(set_ready, 1)

            pool.memset(eighth[:, :], 1.0 / ROUTE_K).then_inc(set_ready, 1)
            pool.memset(ones4[:, :], 1.0).then_inc(set_ready, 1)
            pool.memset(zeros16[:, :], 0.0).then_inc(set_ready, 1)

            def row_rstd(s, n):
                pool.wait_ge(s["stats"], n)
                plain(pool)
                step.did(pool.tensor_scalar(var_eps[:, :], mean_var[:, :, 1], LN_EPS, None, ALU.add))
                step.settle()
                pool.tensor_tensor(rstd[:, :], var_eps[:, :], minus_half[:, :], ALU.pow).then_inc(s["rstd_ready"], 1)

            def keys16(s, batches):
                for b in batches:
                    for m in range(KH):
                        pool.wait_ge(s["k_sb"], m + 1)
                        pool.tensor_tensor(k16[:, b, m, :, :], kT[:, m, b, :].unsqueeze(1).to_broadcast([P, 8, KEYS]),
                                           head_mask[:, :, :], ALU.mult).then_inc(s["k16_ready"], 1)

            def row_scales(c):
                pool.wait_ge(route_stats_ready, c + 1)
                plain(pool)
                v = [route_var[:, i, :] for i in range(6)]
                step.did(pool.tensor_scalar(v[0], route_mv[:, :, 1], LN_EPS, None, ALU.add))
                step.settle()
                step.did(pool.tensor_tensor(v[1], v[0], minus_half[:, :], ALU.pow))
                step.settle()
                step.did(pool.tensor_tensor(v[2], v[1], v[1], ALU.mult))
                step.settle()
                step.did(pool.tensor_tensor(v[3], v[2], route_mv[:, :, 1], ALU.mult))
                step.settle()
                plain(pool)
                step.did(pool.tensor_scalar(v[4], v[3], (1e-12 / 16.0) ** 2, None, ALU.max))
                step.settle()
                step.did(pool.tensor_tensor(v[5], v[4], minus_half[:, :], ALU.pow))
                step.settle()
                pool.tensor_tensor(row_scale[:, :], v[5], v[1], ALU.mult).then_inc(scale_ready, 1)
                pool.tensor_tensor(row_norm[:, ds(c * 4, 4)], v[5], v[4], ALU.mult).then_inc(scale_ready, 1)

            def route_rows():
                for k in range(0, TILES, 2):
                    if k % 8 == 0:
                        pool.wait_ge(rows_sb, 2 * (k // 8) + 2)
                    if k >= 4:
                        pool.wait_ge(counted, k - 3)
                    pool.tensor_scalar(larger16[k % 4], logit_rows[:, k // 8, :], logit[:, k:k + 1], None,
                                       ALU.is_lt).then_inc(compared[0], 1)

                def clear(i):
                    step.did(pool.memset(heavy_rows[i][:, :, :], 0.0))
                for i in range(2):
                    clear(i)
                step.settle()
                keys16(S[1], range(BATCH))
                pool.wait_ge(slot_ready, 1)
                for b in range(BATCH):
                    for t in range(8 * b, 8 * b + 8):
                        pool.indirect_dma_start(rows_in[b], bass.IndirectOffsetOnAxis(ap=slot[:, t:t + 1], axis=0),
                                                normed[:, t, :], None, bounds_check=ROUTED - 1,
                                                oob_is_err=False).then_inc(scattered[b], 16)

                def gather(b):
                    pool.wait_ge(stored, 16 * (b + 1))
                    for t in range(8 * b, 8 * b + 8):
                        pool.indirect_dma_start(heavy_rows[b % 2][:, t - 8 * b, :], None, rows_out[b],
                                                bass.IndirectOffsetOnAxis(ap=slot[:, t:t + 1], axis=0),
                                                bounds_check=ROUTED - 1, oob_is_err=False).then_inc(gathered[b], 16)

                def add_heavy(b):
                    pool.wait_ge(gathered[b], 16 * 8)
                    pool.tensor_tensor(x[:, 8 * b:8 * b + 8, :], x[:, 8 * b:8 * b + 8, :], heavy_rows[b % 2][:, :, :],
                                       ALU.add).then_inc(mixed, 1)

                pool.wait_ge(light_added, 2 * CHUNKS)
                for b in range(BATCH - 1):
                    gather(b)
                    add_heavy(b)
                    if b < 2:
                        pool.wait_ge(mixed, b + 1)
                        clear(b)
                        step.settle()
                row_rstd(S[1], 1)
                row_rstd(S[1], 2)
                gather(BATCH - 1)
                add_heavy(BATCH - 1)

            def gate_norm():
                pool.wait_ge(G["bn_done"], 1)
                pool.wait_ge(G["bias_added"], CHUNKS)
                c = [bn_tmp[:, i:i + 1] for i in range(5)]
                step.did(pool.tensor_scalar(c[0], bn_mv[:, 1:2], BN_EPS, None, ALU.add))
                step.settle()
                step.did(pool.tensor_tensor(c[1], c[0], minus_half[:, 0:1], ALU.pow))
                step.settle()
                step.did(pool.tensor_tensor(c[2], c[1], bn_cols[:, 1:2], ALU.mult))
                step.settle()
                step.did(pool.tensor_tensor(c[3], c[2], bn_mv[:, 0:1], ALU.mult))
                step.settle()
                pool.tensor_tensor(c[4], bn_cols[:, 2:3], c[3], ALU.subtract).then_inc(G["bn_ready"], 1)

            def gate_tile(t, e):
                pool.wait_ge(G["top_ready"], t + 1)
                pool.wait_ge(G["sparseT_ps"], t + FIRST)
                pool.wait_ge(G["part_ready"], t + FIRST)
                plain(pool)
                step.did(pool.tensor_scalar(taken, work[e], FOUND / 2, None, ALU.is_lt))
                step.settle()
                pool.tensor_tensor(taken, taken, expw[e], ALU.mult).then_inc(G["taken_ready"], 1)
                pool.wait_ge(G["taken_ready"], t + 1)
                pool.tensor_tensor(sparse, taken[:, DIM:], normed[:, ds(t, 1), 0:DIM].rearrange("p a d -> p (a d)"), ALU.mult).then_inc(G["sparse_ready"], 1)
                pool.wait_ge(G["part_ready"], t + 1 + FIRST)
                rows = x[:, ds(t, 1), :].rearrange("p a d -> p (a d)")
                pool.tensor_tensor(rows, rows, out_part, ALU.add).then_inc(G["part_added"], 1)

            def gate_scales(c):
                pool.wait_ge(G["stats"], c + 1)
                plain(pool)
                step.did(pool.tensor_scalar(route_var[:, 0, :], route_mv[:, :, 1], LN_EPS, None, ALU.add))
                step.settle()
                pool.tensor_tensor(row_scale[:, :], route_var[:, 0, :], minus_half[:, :], ALU.pow).then_inc(G["rstd_ready"], 1)
                pool.wait_ge(G["h_ready"], c + 1)
                pool.wait_ge(gate_ready, 2)
                rows = x[:, ds(c * 4, 4), :]
                pool.tensor_tensor(rows, rows, bias1[:, :].unsqueeze(1).to_broadcast([P, CHUNK_TILES, DIM]),
                                   ALU.add).then_inc(G["bias_added"], 1)

            pool.wait_ge(set_ready, 1)
            pool.wait_ge(consts_in, 16)
            for l in range(2):
                s = S[l]
                if l == 0:
                    row_rstd(s, 1)
                    keys16(s, range(1))
                    row_rstd(s, 2)
                    keys16(s, range(1, BATCH))
                row_rstd(s, 3)
                with pool.Fori(1, CHUNKS - 2) as c:
                    step.enter(c - 1, 1 + (6 if l == 0 else 1))
                    row_rstd(s, c + 3)
                    scales = row_scales if l == 0 else gate_scales
                    scales(c - 1)
                    step.leave(CHUNKS - 3)
                for c in range(CHUNKS - 3, CHUNKS):
                    scales(c)
                if l == 0:
                    route_rows()
            gate_norm()
            with pool.Fori(0, TILES // 2) as i:
                step.enter(i, 2)
                for e in range(2):
                    gate_tile(i * 2 + e, e)
                step.leave(TILES // 2)

        @block.scalar
        def _(act):
            act.dma_start(consts[:, :], A["consts"]).then_inc(consts_in, 16)
            act.dma_start(consts16[:, :], A["consts16"].bitcast(BF16)).then_inc(consts16_in, 16)
            act.dma_start(gates[:, :], A["gates"].partition_broadcast(P)).then_inc(gates_in, 16)
            act.dma_start(bias_gates[:, :], A["bias_gates"]).then_inc(gates_in, 16)
            act.dma_start(bias_rows[:, :], A["bias_rows"]).then_inc(bias_in, 16)
            act.dma_start(token_row[:, :], A["token"].partition_broadcast(P)).then_inc(route_in, 16)
            act.dma_start(v_bias[:, :], A["bv1"].partition_broadcast(P)).then_inc(route_in, 16)
            act.dma_start(bias1[:, :], A["bias1"].partition_broadcast(P)).then_inc(route_in, 16)
            act.wait_ge(gates_in, 32)
            act.activation(gates[:, :], gates[:, :], ACT.Tanh).then_inc(gates_ready, 1)
            act.activation(bias_gates[:, :], bias_gates[:, :], ACT.Tanh).then_inc(gates_ready, 1)

            def keys(s, l):
                for m in range(KH):
                    act.wait_ge(s["k_ps"], m + 1)
                    src = front[m][:, 0:BATCH * KEYS].rearrange("p (b n) -> p b n", b=BATCH)
                    if l == 0:
                        act.activation(kT[:, m, :, :], src, ACT.Copy).then_inc(s["k_sb"], 1)
                    else:
                        act.activation(kT[:, m, :, :], src, ACT.Identity, bias=qkv_bias[:, 2 + m:3 + m]).then_inc(s["k_sb"], 1)

            def evac_hT(s, a):
                act.wait_ge(s["hT_ps"], a + 1)
                if not (isinstance(a, int) and a == 0):
                    act.wait_ge(s["q_ps"], a * 2)
                for k in range(KH):
                    act.activation(hT[:, k, :], front[k][:, :], ACT.Copy).then_inc(s["hT_sb"], 1)

            def evac_q(s, l, a, e, m):
                act.wait_ge(s["q_ps"], a * 2 + (m + 1))
                if not isinstance(a, int) or a >= 2:
                    act.wait_ge(s["s_ps"], a * 8 - 8)
                if not (isinstance(a, int) and a == 0):
                    act.wait_ge(s["max_ps"], a * 8)
                for q, ready in ((q16, "q16_ready"), (qT[e], "q_sb")):
                    if l == 0:
                        act.activation(q[:, m, :], front[m][:, :], ACT.Copy).then_inc(s[ready], 1)
                    else:
                        act.activation(q[:, m, :], front[m][:, :], ACT.Identity, bias=qkv_bias[:, m:m + 1]).then_inc(s[ready], 1)

            def evac_maxT(s, n):
                act.wait_ge(s["maxT_ps"], n + 1)
                if not (isinstance(n, int) and n == 0):
                    act.wait_ge(s["s_ps"], n * 8)
                act.activation(maxT16[0:HEADS, :], maxT_ps, ACT.Copy).then_inc(s["maxT_sb"], 1)

            def exp(s, c, p):
                act.wait_ge(s["s_ps"], c * 8 + (p + 1))
                act.wait_ge(s["pv"], c * 8 + (p + 1))
                act.activation(probs[:, p % 4, :], score[p % 2][:, :], ACT.Exp, scale=SCALE).then_inc(s["s_exp"], 1)

            def inverse(s, step, c, m):
                act.wait_ge(s["pv"], c * 8 + (4 * m + 4 + 4))
                act.wait_ge(s["y_ready"], c * 2 + m + FIRST)
                step.did(act.activation(log_den[:, m, :], DB[:, :], ACT.Ln))
                step.settle()
                act.activation(inv_den[:, m, :], log_den[:, m, :], ACT.Exp, scale=-1.0).then_inc(s["inv_ready"], 1)

            def chunk_step(s, l, step, c, e, ahead, nxt):
                for p in range(PAIRS):
                    exp(s, c, p)
                    if p == 6 and ahead:
                        evac_hT(s, c + 2)
                    if p == 5:
                        inverse(s, step, c, 0)
                inverse(s, step, c, 1)
                if ahead:
                    evac_q(s, l, c + 2, e, 0)
                if nxt:
                    evac_maxT(s, c + 1)
                if ahead:
                    evac_q(s, l, c + 2, e, 1)

            def ffn0():
                keys(S[1], 1)
                for b in range(BATCH):
                    for i in range(2):
                        act.wait_ge(rows_ps, 2 * b + i + 1)
                        act.activation(logit_rows[:, b, i * 512:(i + 1) * 512], score[i][:, :], ACT.Copy).then_inc(rows_sb, 1)
                act.wait_ge(args_ready, 1)
                act.activation(exps[:, :], args[:, :], ACT.Exp).then_inc(exps_ready, 1)

                def copy_rows(n):
                    act.activation(h[:, :, :], normed[:, ds(n * 4, 4), 0:DIM], ACT.Copy).then_inc(copied, 1)

                def light_chunk(n, more):
                    act.wait_ge(light_T, n + 1)
                    for k in range(KH):
                        act.activation(hT[:, k, :], front[k][:, :], ACT.Copy).then_inc(light_Tsb, 1)
                    if more:
                        copy_rows(n + 1)
                    act.wait_ge(light_h, n + 1)
                    act.wait_ge(light_o, n * 2 + FIRST)
                    act.activation(light_gT, mid[0][:, :], ACT.Gelu, bias=ffn0_cols[:, 4:5]).then_inc(light_g, 1)

                def relevel(n):
                    act.wait_ge(sum_ready, n)
                    act.activation(log_sum[:, :], DB[:, 0:BATCH], ACT.Ln, scale=2.0 ** -LOG_SHIFT).then_inc(log_ready, 1)

                copy_rows(0)
                for n in range(len(ROUTE_BLOCKS)):
                    act.preload_act_table_set("gelu_and_others")
                    if n + 1 < len(ROUTE_BLOCKS):
                        with act.Fori(0, 2) as i:
                            light_chunk(i + 2 * n, True)
                    else:
                        light_chunk(CHUNKS - 2, True)
                        light_chunk(CHUNKS - 1, False)
                    act.preload_act_table_set("natural_log_exp_and_others")
                    relevel(sums_before[n + 1])
                    if n + 1 < len(ROUTE_BLOCKS):
                        act.wait_ge(args_ready, n + 2)
                        act.activation(exps[:, :], args[:, :], ACT.Exp).then_inc(exps_ready, 1)
                act.wait_ge(score_arg, 1)
                act.activation(score_of[:, :], args[:, 0:TILES], ACT.Exp).then_inc(score_ready, 1)
                with act.Fori(0, BATCH) as b:
                    for m in range(HEAVY // P):
                        act.wait_ge(heavy_h, b * 8 + (m + 1) + FIRST)
                        if m == 0:
                            act.wait_ge(heavy_o, b + FIRST)
                        act.activation(heavy_gT[:, m, :], heavy_banks[m % 4][:, 0:ROUTED], ACT.Gelu,
                                       bias=ffn0_cols[:, 5 + m:6 + m]).then_inc(heavy_g, 1)

            step = Chain(act, act_step)
            for l in range(2):
                s = S[l]
                if l == 1:
                    ffn0()
                act.sem_inc(s["pv"], 4)
                act.preload_act_table_set("natural_log_exp_and_others")
                if l == 0:
                    keys(s, l)
                for a in range(2):
                    evac_hT(s, a)
                    for m in range(KH):
                        evac_q(s, l, a, a, m)
                evac_maxT(s, 0)
                with act.Fori(0, BATCH - 1) as b:
                    step.enter(b, 4)
                    for e in range(2):
                        chunk_step(s, l, step, b * 2 + e, e, True, True)
                    step.leave(BATCH - 1)
                for e in range(2):
                    chunk_step(s, l, step, CHUNKS - 2 + e, e, False, e == 0)
            def evac_rowsT(c, e):
                act.wait_ge(G["hT_ps"], c + 1)
                if not isinstance(c, int) or c >= 2:
                    act.wait_ge(G["sums_ps"], c - 1)
                for k in range(KH):
                    act.activation(rowsT2[e][:, k, :], rowsT_banks[e][k][:, :], ACT.Copy).then_inc(G["hT_sb"], 1)

            def save_sums(c, e):
                act.wait_ge(G["sums_ps"], c + 1)
                act.activation(groups[:, ds(c * CHUNK, CHUNK)], mid[e][:, :], ACT.Identity,
                               bias=bn_cols[:, 0:1]).then_inc(G["sums_sb"], 1)

            def activate(c):
                return act.activation(groups[:, ds(c * CHUNK, CHUNK)], groups[:, ds(c * CHUNK, CHUNK)], ACT.Gelu,
                                      bias=bn_tmp[:, 4:5], scale=bn_tmp[:, 2:3])

            def prepare_rows(t, e):
                act.wait_ge(G["hsT_ps"], t)
                act.activation(hs[e], normed[:, ds(t, 1), 0:DIM].rearrange("p a d -> p (a d)"), ACT.Copy).then_inc(G["hs_ready"], 1)

            def prepare_acts(t, e):
                act.wait_ge(G["logit_ps"], t)
                act.activation(acts[e], groups[:, ds(t * P, P)], ACT.Copy).then_inc(G["acts_ready"], 1)

            def evac_hs(t, e):
                act.wait_ge(G["hsT_ps"], t + 1)
                act.wait_ge(G["full_ps"], t)
                act.activation(hsT[e], F0[:, 0:2 * P].rearrange("p (k n) -> p k n", k=KH), ACT.Copy).then_inc(G["hsT_sb"], 1)

            def save_logits(t, e):
                act.wait_ge(G["logit_ps"], t + 1)
                if not (isinstance(t, int) and t == 0):
                    act.wait_ge(G["taken_ready"], t - 1)
                act.activation(work[e], mid[e][:, :], ACT.Copy).then_inc(G["work_ready"], 1)

            def exponentials(t, e):
                act.wait_ge(G["minus_ready"], t + 1)
                for br in range(2):
                    act.activation(expw[e][:, br * DIM:(br + 1) * DIM], mid[e][:, br * DIM:(br + 1) * DIM], ACT.Exp,
                                   bias=minus_top[:, br:br + 1], accum_out=exp_sum[:, br:br + 1]).then_inc(G["exp_ready"], 1)

            def evac_sparse(t):
                act.wait_ge(G["sparseT_ps"], t + 1 + FIRST)
                act.wait_ge(G["in_ps"], t)
                act.activation(sparseT, F1[:, 0:2 * P].rearrange("p (k n) -> p k n", k=KH), ACT.Copy).then_inc(G["sparseT_sb"], 1)

            def gate_tile(t, e, ahead=True):
                if ahead:
                    prepare_rows(t + 1, 1 - e)
                    prepare_acts(t + 1, 1 - e)
                    evac_hs(t + 1, 1 - e)
                exponentials(t, e)
                if ahead:
                    save_logits(t + 1, 1 - e)
                if not (isinstance(t, int) and t == 0):
                    evac_sparse(t - 1)

            act.wait_ge(gate_in, 16)
            act.wait_ge(G["h_ready"], CHUNKS)
            evac_rowsT(0, 0)
            evac_rowsT(1, 1)
            save_sums(0, 0)
            with act.Fori(1, CHUNKS // 2) as i:
                for e in range(2):
                    evac_rowsT(i * 2 + e, e)
                    save_sums(i * 2 + e - 1, 1 - e)
            save_sums(CHUNKS - 1, 1)
            act.preload_act_table_set("gelu_and_others")
            prepare_rows(0, 0)
            evac_hs(0, 0)
            act.wait_ge(G["bn_ready"], 1)
            step.did(activate(0))
            step.settle()
            prepare_acts(0, 0)
            with act.Fori(1, CHUNKS) as c:
                step.enter(c - 1, 1)
                step.did(activate(c))
                step.leave(CHUNKS - 1)
            step.settle()
            save_logits(0, 0)
            act.preload_act_table_set("natural_log_exp_and_others")
            for e in range(2):
                gate_tile(e, e)
            with act.Fori(1, TILES // 2 - 1) as i:
                for e in range(2):
                    gate_tile(i * 2 + e, e)
            for e in range(2):
                gate_tile(TILES - 2 + e, e, e == 0)
            evac_sparse(TILES - 1)

        @block.vector
        def _(dve):
            step = Chain(dve, dve_step)

            def split_biases():
                step.did(dve.memset(bias3[:, :, :], 0.0))
                step.did(dve.tensor_scalar(bias_rows[0:3, :], bias_rows[0:3, :], bias_gates[:, 0:1], None, ALU.mult))
                step.settle()
                for k in range(3):
                    step.did(dve.tensor_copy(bias_piece[k][:, :], bias_rows[:, :]))
                    step.settle()
                    if k < 2:
                        step.did(dve.tensor_tensor(bias_rows[:, :], bias_rows[:, :], bias_piece[k][:, :], ALU.subtract))
                        step.settle()
                dve.sem_inc(pieces_ready, 1)

            def row_stats_of(s, tile0, n, step):
                if not (isinstance(n, int) and n == 0):
                    dve.wait_ge(s["rstd_ready"], n)
                    plain(dve)
                for t in range(CHUNK_TILES):
                    step.did(dve.bn_stats(row_stats[:, t, :], x[:, ds(tile0 + t, 1), :].rearrange("p a d -> p (a d)")))
                step.settle()
                plain(dve)
                for t in range(CHUNK_TILES):
                    ins = dve.bn_aggr(mean_var[:, t, :], row_stats[:, t, :])
                ins.then_inc(s["stats"], 1)

            def normalize(s, tile0, a):
                dve.wait_ge(s["rstd_ready"], a + 1)
                if not (isinstance(a, int) and a == 0):
                    dve.wait_ge(s["hT_ps"], a)
                for t in range(CHUNK_TILES):
                    ins = dve.tensor_scalar(h[:, t, :], x[:, ds(tile0 + t, 1), :].rearrange("p a d -> p (a d)"),
                                            mean_var[:, t, 0:1], rstd[:, t:t + 1], ALU.subtract, ALU.mult)
                ins.then_inc(s["h_ready"], 1)

            def row_max(s, n, j):
                t, m = j // 2, j % 2
                dve.wait_ge(s["max_ps"], n * 8 + (j + 1))
                if j == 0 and not (isinstance(n, int) and n == 0):
                    dve.wait_ge(s["maxT_ps"], n)
                dve.tensor_reduce(max16[:, t, 8 * m:8 * m + 8], mid[j % 2][:, :].rearrange("p (h k) -> p h k", h=8),
                                  AX_X, ALU.max).then_inc(s["max_done"], 1)

            def divide(s, c, m):
                dve.wait_ge(s["inv_ready"], c * 2 + (m + 1))
                if not (isinstance(c, int) and c == 0):
                    dve.wait_ge(s["o_ps"], c * 2)
                dve.tensor_tensor(yT[:, m, :], YB[:, :], inv_den[:, m, :], ALU.mult).then_inc(s["y_ready"], 1)

            def add_to_x(s, c, g):
                dve.wait_ge(s["o_ps"], c * 2 + (g + 1))
                rows = x[:, ds(c * 4 + 2 * g, 2), :].rearrange("p a d -> p (a d)")
                dve.tensor_tensor(rows, rows, mid[g][:, :], ALU.add).then_inc(s["x_new"], 1)

            def key_diagonal(s, b, first):
                if not first:
                    dve.wait_ge(s["s_ps"], b * 16)
                for m in range(KH):
                    dve.tensor_tensor(k_diag[:, m, :, :], kT[:, m, ds(b, 1), :].to_broadcast([P, 8, KEYS]),
                                      head_mask[:, :, :], ALU.mult).then_inc(s["kv_diag"], 1)

            def value_diagonal(s, b, first):
                if not first:
                    dve.wait_ge(s["pv"], b * 16 + 4)
                dve.tensor_tensor(v_diag[:, :, :], v_all[:, ds(b, 1), :].rearrange("p a (h d) -> p (a h) d", h=HEADS),
                                  pair_mask[:, :, :], ALU.mult).then_inc(s["kv_diag"], 1)

            def chunk_step(s, c, e, b, ahead, nxt, before):
                for p in range(PAIRS):
                    if nxt:
                        row_max(s, c + 1, p)
                    if p == 1 and ahead and e == 0 and s is S[1]:
                        dve.wait_ge(mixed, b + 2)
                    if p == 1 and ahead:
                        row_stats_of(s, c * 4 + 8, c + 2, step)
                    if p == 3 and before:
                        route_stats_of(c - 1) if s is S[0] else gate_stats_of(c - 1)
                    if p == 4 and ahead:
                        normalize(s, c * 4 + 8, c + 2)
                    if p == 5:
                        divide(s, c, 0)
                    if p == 6 and before:
                        route_logits_of(c - 1) if s is S[0] else gate_rows_of(c - 1)
                if e == 1 and nxt:
                    key_diagonal(s, b + 1, False)
                divide(s, c, 1)
                if e == 1 and nxt:
                    value_diagonal(s, b + 1, False)
                for g in range(2):
                    add_to_x(s, c, g)

            def route_stats_of(c):
                dve.wait_ge(s0["x_new"], c * 2 + 2 + FIRST)
                dve.wait_ge(scale_ready, c * 2)
                plain(dve)
                for t in range(CHUNK_TILES):
                    step.did(dve.bn_stats(route_stats[:, t, :], x[:, ds(c * 4 + t, 1), :].rearrange("p a d -> p (a d)")))
                step.settle()
                plain(dve)
                for t in range(CHUNK_TILES):
                    ins = dve.bn_aggr(route_mv[:, t, :], route_stats[:, t, :])
                ins.then_inc(route_stats_ready, 1)

            def route_logits_of(c):
                dve.wait_ge(scale_ready, c * 2 + 2)
                for t in range(CHUNK_TILES):
                    step.did(dve.tensor_scalar(normed[:, ds(c * 4 + t, 1), 0:DIM].rearrange("p a d -> p (a d)"),
                                               x[:, ds(c * 4 + t, 1), :].rearrange("p a d -> p (a d)"),
                                               route_mv[:, t, 0:1], row_scale[:, t:t + 1], ALU.subtract, ALU.mult))
                for t in range(CHUNK_TILES):
                    step.did(dve.scalar_tensor_tensor(
                        out=dot_out[:, :], in0=x[:, ds(c * 4 + t, 1), :].rearrange("p a d -> p (a d)"),
                        scalar=route_mv[:, t, 0:1], in1=token_row[:, :], op0=ALU.subtract, op1=ALU.mult,
                        accum_out=raw_dot[:, t:t + 1]))
                    step.settle()
                step.did(dve.tensor_tensor(raw_dot[:, :], raw_dot[:, :], row_scale[:, :], ALU.mult))
                step.settle()
                dve.tensor_tensor(logit[:, ds(c * 4, 4)], raw_dot[:, :], row_norm[:, ds(c * 4, 4)], ALU.mult).then_inc(logit_ready, 1)

            by_batch = lambda ap: ap.rearrange("p (b c) -> p b c", b=BATCH)
            spread = lambda ap: ap.unsqueeze(2).to_broadcast([P, BATCH, TILES // BATCH])

            def cross_max(n):
                dve.wait_ge(cross_ps, n + 1)
                dve.tensor_reduce(col4[:, :], YB[0:BATCH, 0:P], AX_X, ALU.max).then_inc(cross_col, 1)
                dve.wait_ge(cross_col, n + 1)
                dve.tensor_scalar(diag4[:, :], ident[0:BATCH, 0:BATCH], col4[:, 0:1], None, ALU.mult).then_inc(cross_diag, 1)
                dve.wait_ge(cross_out, n + 1)

            def exp_args():
                step.did(dve.tensor_tensor(level[:, :], minus_a[:, :], top_logit[:, :], ALU.min))
                step.settle()
                step.did(dve.tensor_tensor(by_batch(args[:, 0:TILES]), by_batch(logit[:, :]), spread(level[:, :]), ALU.subtract))
                step.did(dve.tensor_tensor(args[:, TILES:], minus_a[:, :], level[:, :], ALU.subtract))
                step.settle()
                dve.tensor_scalar(args[:, :], args[:, :], 1.0 / ROUTE_EPS, 80.0, ALU.mult, ALU.min).then_inc(args_ready, 1)

            def route_iteration(sums):
                dve.wait_ge(sum_ready, sums)
                step.did(dve.tensor_tensor(by_batch(capped[:, :]), by_batch(exps[:, 0:TILES]), spread(DB[:, 0:BATCH]), ALU.min))
                step.settle()
                dve.tensor_reduce(part_sum[:, :], by_batch(capped[:, :]), AX_X, ALU.add).then_inc(part_ready, 1)

            def compare(n, b, e):
                if not (isinstance(n, int) and n == 0):
                    dve.wait_ge(counted, n * 4 + (e - 3))
                dve.tensor_scalar(larger16[e], logit_rows[:, b, :], logit[:, ds(n * 4 + e, 1)], None,
                                  ALU.is_lt).then_inc(compared[1], 1)

            def light_to_x(n, g):
                dve.wait_ge(light_o, n * 2 + (g + 1) + FIRST)
                rows = x[:, ds(n * 4 + 2 * g, 2), :].rearrange("p a d -> p (a d)")
                dve.tensor_tensor(rows, rows, score[g][:, :], ALU.add).then_inc(light_added, 1)

            def route():
                dve.wait_ge(logit_ready, CHUNKS)
                dve.wait_ge(s0["x_new"], 2 * CHUNKS + FIRST)
                dve.tensor_reduce(part_sum[:, :], by_batch(logit[:, :]), AX_X, ALU.max).then_inc(cross_in, 1)
                step.did(dve.memset(minus_a[:, :], 0.0))
                cross_max(0)
                step.did(dve.tensor_copy(top_logit[:, :], YB[:, P:P + BATCH]))
                step.settle()
                exp_args()
                for n, iters in enumerate(ROUTE_BLOCKS):
                    dve.wait_ge(exps_ready, n + 1)
                    dve.tensor_scalar(part_sum[:, :], exps[:, TILES:], ROUTE_K / P, None, ALU.mult).then_inc(part_ready, 1)

                    dve.wait_ge(rows_sb, 2 * n + 2)

                    def route_round(i, first=False):
                        for j in range(CHUNK_ITERS):
                            route_iteration(i * CHUNK_ITERS + (sums_before[n] + 1 + j))
                            if j in (2, 4) and not first:
                                light_to_x(i + (2 * n - 1), j // 2 - 1)
                            if j in (0, 3):
                                compare(i + 2 * n, n, 1 if j == 0 else 3)

                    if n == 0:
                        route_round(0, first=True)
                        route_round(1)
                    else:
                        with dve.Fori(0, 2) as i:
                            step.enter(i, CHUNK_ITERS)
                            route_round(i)
                            step.leave(2)
                    for j in range(2 * CHUNK_ITERS, iters):
                        route_iteration(sums_before[n] + 1 + j)
                    dve.wait_ge(log_ready, n + 1)
                    step.did(dve.tensor_scalar(log_sum[:, :], log_sum[:, :], LOG_SHIFT * math.log(2.0), None, ALU.add))
                    step.settle()
                    step.did(dve.scalar_tensor_tensor(out=minus_a[:, :], in0=log_sum[:, :], scalar=ROUTE_EPS, in1=level[:, :],
                                                      op0=ALU.mult, op1=ALU.add))
                    step.settle()
                    if n + 1 < len(ROUTE_BLOCKS):
                        exp_args()
                    else:
                        for g in range(2):
                            light_to_x(CHUNKS - 1, g)
                step.did(dve.tensor_tensor(by_batch(args[:, 0:TILES]), by_batch(logit[:, :]), spread(minus_a[:, :]), ALU.subtract))
                step.settle()
                step.did(dve.tensor_scalar(args[:, 0:TILES], args[:, 0:TILES], 0.0, 1.0 / ROUTE_EPS, ALU.min, ALU.mult))
                step.settle()
                dve.sem_inc(score_arg, 1)
                key, larger, equal, take = (pick[:, i, :] for i in range(4))
                step.did(dve.tensor_scalar(key, args[:, 0:TILES], LOG_TINY, None, ALU.max))
                dve.wait_ge(counted, TILES)
                step.did(dve.tensor_scalar(take, counts_ps, ROUTED - 0.5, 1.0, ALU.is_gt, ALU.mult))
                step.settle()
                step.did(dve.scalar_tensor_tensor(out=larger, in0=take, scalar=1e4, in1=key, op0=ALU.mult, op1=ALU.add))
                step.settle()
                dve.tensor_reduce(part_sum[:, :], by_batch(larger), AX_X, ALU.min, negate=True).then_inc(cross_in, 1)
                cross_max(1)
                step.did(dve.tensor_scalar(level[:, :], YB[:, P:P + BATCH], -1.0, None, ALU.mult))
                step.settle()
                step.did(dve.tensor_tensor(by_batch(larger), by_batch(key), spread(level[:, :]), ALU.is_gt))
                step.did(dve.tensor_tensor(by_batch(equal), by_batch(key), spread(level[:, :]), ALU.is_equal))
                step.settle()
                step.did(dve.tensor_copy(flag16[:, :], equal))
                step.did(dve.tensor_reduce(part_sum[:, :], by_batch(larger), AX_X, ALU.add))
                step.settle()
                dve.tensor_copy(count16[:, :], part_sum[:, :]).then_inc(flags_ready, 1)
                dve.wait_ge(prefix_ready, 1)
                step.did(dve.tensor_scalar(minus_a[:, :], M1[:, 0:BATCH], -1.0, float(ROUTED), ALU.mult, ALU.add))
                step.settle()
                step.did(dve.tensor_tensor(by_batch(take), by_batch(M0[:, 0:TILES]), spread(minus_a[:, :]), ALU.is_lt))
                step.settle()
                step.did(dve.tensor_tensor(take, take, equal, ALU.mult))
                step.settle()
                step.did(dve.tensor_tensor(take, take, larger, ALU.add))
                step.settle()
                dve.tensor_copy(flag16[:, :], take).then_inc(flags_ready, 1)
                dve.wait_ge(prefix_ready, 2)
                step.did(dve.scalar_tensor_tensor(out=take, in0=M0[:, 0:TILES], scalar=float(ROUTED), in1=take,
                                                  op0=ALU.is_lt, op1=ALU.mult))
                step.did(dve.tensor_tensor(key, M0[:, 0:TILES], slot_base[:, 0, :], ALU.add))
                step.settle()
                step.did(dve.tensor_tensor(key, key, take, ALU.mult))
                step.settle()
                step.did(dve.tensor_tensor(key, key, slot_base[:, 1, :], ALU.add))
                step.settle()
                dve.wait_ge(score_ready, 1)
                step.did(dve.tensor_copy(normed[:, :, DIM], score_of[:, :]))
                step.did(dve.tensor_copy(slot[:, :], key))
                step.settle()
                dve.sem_inc(slot_ready, 1)

            def heavy():
                with dve.Fori(0, BATCH // 2) as i:
                    step.enter(i, 2 * 3)
                    for e in range(2):
                        b = i * 2 + e
                        dve.wait_ge(heavy_T, b + 1)
                        dve.wait_ge(heavy_h, b * 8 + FIRST)
                        dve.tensor_copy(pickedT[:, :, :], F0[:, :].rearrange("p (k n) -> p k n", k=KH)).then_inc(heavy_Tsb, 1)
                        dve.wait_ge(picked_in, b * 16 + 16)
                        dve.wait_ge(heavy_done, b + FIRST)
                        step.did(dve.tensor_scalar(pick_gate[:, :], picked[e][:, :, DIM], -1.0, 1.0, ALU.mult, ALU.add))
                        step.settle()
                        step.did(dve.tensor_tensor(pick_gate[:, :], pick_gate[:, :], picked[e][:, :, DIM], ALU.add))
                        step.settle()
                        step.did(dve.tensor_scalar(pick_gate[:, :], pick_gate[:, :], gates[:, 1:2], None, ALU.mult))
                        step.settle()
                        dve.wait_ge(heavy_o, b + 1 + FIRST)
                        dve.wait_ge(heavy_room, b + 1)
                        for j in range(2):
                            ins = dve.tensor_scalar(heavy_y[e][:, j, :], YB[:, j * DIM:(j + 1) * DIM], pick_gate[:, j:j + 1], None,
                                                    ALU.mult)
                        ins.then_inc(heavy_done, 1)
                    step.leave(BATCH // 2)

            def gate_ffn0():
                dve.wait_ge(ffn0_in, 32)
                for k in range(KH):
                    dve.tensor_scalar(w1l[:, k, :], w1l[:, k, :], ffn0_cols[:, k:k + 1], None, ALU.mult).then_inc(ffn0_ready, 1)
                    dve.tensor_scalar(w1h[:, k, :], w1h[:, k, :], ffn0_cols[:, 2 + k:3 + k], None, ALU.mult).then_inc(ffn0_ready, 1)
                dve.tensor_scalar(w2l[:, :], w2l[:, :], gates[:, 1:2], None, ALU.mult).then_inc(ffn0_ready, 1)

            def gate_stats_of(c):
                dve.wait_ge(S[1]["x_new"], c * 2 + 2 + FIRST)
                dve.wait_ge(G["rstd_ready"], c)
                plain(dve)
                for t in range(CHUNK_TILES):
                    step.did(dve.bn_stats(route_stats[:, t, :], x[:, ds(c * 4 + t, 1), :].rearrange("p a d -> p (a d)")))
                step.settle()
                plain(dve)
                for t in range(CHUNK_TILES):
                    ins = dve.bn_aggr(route_mv[:, t, :], route_stats[:, t, :])
                ins.then_inc(G["stats"], 1)

            def gate_rows_of(c):
                dve.wait_ge(G["rstd_ready"], c + 1)
                for t in range(CHUNK_TILES):
                    step.did(dve.tensor_scalar(normed[:, ds(c * 4 + t, 1), 0:DIM].rearrange("p a d -> p (a d)"),
                                               x[:, ds(c * 4 + t, 1), :].rearrange("p a d -> p (a d)"),
                                               route_mv[:, t, 0:1], row_scale[:, t:t + 1], ALU.subtract, ALU.mult))
                step.settle()
                dve.sem_inc(G["h_ready"], 1)

            def gate_copy(c, e):
                if not isinstance(c, int) or c >= 2:
                    dve.wait_ge(G["hT_ps"], c - 1)
                dve.tensor_copy(rows2[e], normed[:, ds(c * 4, 4), 0:DIM]).then_inc(G["copied"], 1)

            def group_stats(c):
                dve.wait_ge(G["sums_sb"], c + 1 + FIRST)
                plain(dve)
                step.did(dve.bn_stats(bn_parts[:, ds(c * 6, 6)], groups[:, ds(c * CHUNK, CHUNK)]))

            def gate_tile(t, e):
                dve.wait_ge(G["work_ready"], t + 1)
                for r in range(4):
                    for br in range(2):
                        cols = work[e][:, br * DIM:(br + 1) * DIM]
                        if r:
                            dve.wait_ge(top_step, t * 16 + (4 * r + br - 1))
                        dve.max(top8[:, r, br, :], cols).then_inc(top_step, 1)
                    for br in range(2):
                        cols = work[e][:, br * DIM:(br + 1) * DIM]
                        dve.wait_ge(top_step, t * 16 + (4 * r + br + 1))
                        dve.match_replace(cols, top8[:, r, br, :], cols, FOUND).then_inc(top_step, 1)
                        if r == 0 and br == 0:
                            dve.wait_ge(top_step, t * 16 + 2)
                            dve.wait_ge(G["exp_ready"], t * 2)
                            dve.tensor_scalar(minus_top[:, :], top8[:, 0, :, 0], -1.0, None, ALU.mult).then_inc(G["minus_ready"], 1)
                    if r == 1 and t >= 2:
                        add_in(t - 2, e)
                    if r == 2 and t:
                        out_branch(t - 1, 1 - e)
                dve.wait_ge(G["exp_ready"], t * 2 + 2)
                step.did(dve.reciprocal(inv_sum[e][:, :], exp_sum[:, :]))
                dve.wait_ge(top_step, t * 16 + 16)
                step.settle()
                dve.sem_inc(G["top_ready"], 1)

            def out_branch(t, e):
                dve.wait_ge(G["full_ps"], t + 1)
                dve.wait_ge(G["taken_ready"], t + 1)
                dve.wait_ge(G["part_added"], t)
                dve.scalar_tensor_tensor(out=out_part, in0=score[e][:, 0:DIM], scalar=inv_sum[e][:, 0:1], in1=taken[:, 0:DIM],
                                         op0=ALU.mult, op1=ALU.mult).then_inc(G["part_ready"], 1)

            def add_in(t, e):
                dve.wait_ge(G["in_ps"], t + 1)
                dve.wait_ge(G["part_added"], t + 1)
                rows = x[:, ds(t, 1), :].rearrange("p a d -> p (a d)")
                dve.scalar_tensor_tensor(out=rows, in0=out_banks[e][:, 0:DIM], scalar=inv_sum[e][:, 1:2], in1=rows,
                                         op0=ALU.mult, op1=ALU.add).then_inc(G["x_new"], 1)

            def gate_layer():
                gate_copy(0, 0)
                gate_copy(1, 1)
                with dve.Fori(1, CHUNKS // 2) as i:
                    step.enter(i - 1, 2)
                    for e in range(2):
                        gate_copy(i * 2 + e, e)
                        group_stats(i * 2 + e - 2)
                    step.leave(CHUNKS // 2 - 1)
                group_stats(CHUNKS - 2)
                group_stats(CHUNKS - 1)
                step.settle()
                dve.bn_aggr(bn_mv[:, :], bn_parts[:, :]).then_inc(G["bn_done"], 1)
                for t in range(TILES):
                    gate_tile(t, t % 2)
                add_in(TILES - 2, 0)
                out_branch(TILES - 1, 1)
                add_in(TILES - 1, 1)

            def values(s, l):
                for b in range(BATCH):
                    dve.wait_ge(s["v_ps"], b + 1)
                    if l == 0:
                        dve.tensor_copy(v_all[:, b, :], mid[b % 2][:, 0:DIM]).then_inc(s["v_sb"], 1)
                    else:
                        dve.tensor_tensor(v_all[:, b, :], mid[b % 2][:, 0:DIM], v_bias[:, :], ALU.add).then_inc(s["v_sb"], 1)

            s0 = S[0]
            dve.wait_ge(x_in[0], 16)
            for l in range(2):
                s = S[l]
                if l == 1:
                    route()
                    heavy()
                    dve.wait_ge(gate_in, 16)
                    dve.tensor_scalar(gate_w[:, :, :], gate_w[:, :, :], gates[:, 3:4], None, ALU.mult).then_inc(gate_ready, 1)
                    dve.tensor_scalar(bias1[:, :], bias1[:, :], gates[:, 3:4], None, ALU.mult).then_inc(gate_ready, 1)
                    dve.wait_ge(mixed, 1)
                row_stats_of(s, 0, 0, step)
                normalize(s, 0, 0)
                if l == 0:
                    dve.wait_ge(consts_in, 16)
                if l == 0:
                    values(s, l)
                if l == 0:
                    dve.wait_ge(x_in[1], 16)
                row_stats_of(s, 4, 1, step)
                normalize(s, 4, 1)
                if l == 0:
                    dve.wait_ge(bias_in, 16)
                    dve.wait_ge(gates_ready, 2)
                    split_biases()
                dve.wait_ge(attn_w_in[l], 16)
                dve.tensor_scalar(Wo[l][:, :, :], Wo[l][:, :, :], gates[:, 2 * l:2 * l + 1], None, ALU.mult).then_inc(wo_ready, 1)
                dve.wait_ge(s["v_sb"], BATCH)
                dve.wait_ge(s["k_sb"], KH)
                key_diagonal(s, 0, True)
                value_diagonal(s, 0, True)
                for a in range(2):
                    if a == 0:
                        for j in range(8):
                            row_max(s, 0, j)
                if l == 0:
                    dve.wait_ge(x_in[2], 16)
                if l == 0:
                    gate_ffn0()
                    dve.wait_ge(route_in, 48)
                def chunk_pair(b, ahead, first):
                    for e in range(2):
                        chunk_step(s, b * 2 + e, e, b, ahead, ahead or e == 0, before=not (first and e == 0))

                chunk_pair(0, True, True)
                with dve.Fori(1, BATCH - 1) as b:
                    step.enter(b - 1, 8 + (26 if l == 0 else 16))
                    chunk_pair(b, True, False)
                    step.leave(BATCH - 2)
                chunk_pair(BATCH - 1, False, False)
                if l == 0:
                    route_stats_of(CHUNKS - 1)
                    values(S[1], 1)
                    route_logits_of(CHUNKS - 1)
                else:
                    gate_stats_of(CHUNKS - 1)
                    gate_rows_of(CHUNKS - 1)
            gate_layer()

        @block.tensor
        def _(pe):
            def keys_values(s, l):
                for m in range(KH):
                    for k in range(KH):
                        mm = pe.matmul(front[m][:, 0:BATCH * KEYS], Wk[l][:, k, m * P:(m + 1) * P],
                                       ctxT[:, k, :, 0, :], start=(k == 0), stop=(k == KH - 1))
                    mm.then_inc(s["k_ps"], 1)
                for b in range(BATCH):
                    if b >= 2:
                        pe.wait_ge(s["v_sb"], b - 1)
                    elif l == 1:
                        pe.wait_ge(S[0]["x_new"], 2 * CHUNKS + FIRST)
                    for k in range(KH):
                        mm = pe.matmul(mid[b % 2][:, 0:DIM], ctxT[:, k, b, :, :].rearrange("p r n -> p (r n)"), Wv[l][:, k, :],
                                       start=(k == 0), stop=(k == KH - 1))
                    mm.then_inc(s["v_ps"], 1)

            def transpose_h(s, a):
                pe.wait_ge(s["h_ready"], a + 1)
                if not (isinstance(a, int) and a == 0):
                    pe.wait_ge(s["q_sb"], a * 2)
                for k in range(KH):
                    for t in range(CHUNK_TILES):
                        mm = pe.transpose(front[k][:, t * P:(t + 1) * P], h[:, t, k * P:(k + 1) * P], ident[:, :])
                mm.then_inc(s["hT_ps"], 1)

            def project_q(s, l, a, m):
                pe.wait_ge(s["hT_sb"], a * 2 + 2)
                for k in range(KH):
                    mm = pe.matmul(front[m][:, :], Wq[l][:, k, m * P:(m + 1) * P], hT[:, k, :],
                                   start=(k == 0), stop=(k == KH - 1))
                mm.then_inc(s["q_ps"], 1)

            def max_scores(s, l, n, first, b, j):
                t, m = j // 2, j % 2
                pe.wait_ge(s["q16_ready"], n * 2 + (m + 1))
                if j >= 2:
                    pe.wait_ge(s["max_done"], n * 8 + (j - 1))
                masked = l == 0 and first and t == 0
                mm = pe.matmul(mid[j % 2][:, :], q16[:, m, t * P:(t + 1) * P],
                               k16[:, ds(b, 1), m, :, :].rearrange("p a h k -> p (a h k)"), start=True, stop=not masked)
                if masked:
                    mm = pe.matmul(mid[j % 2][:, :], ident16[:, :], causal_rows16[:, :], start=False, stop=True)
                mm.then_inc(s["max_ps"], 1)

            def transpose_max(s, n):
                pe.wait_ge(s["max_done"], n * 8 + 8)
                if not (isinstance(n, int) and n == 0):
                    pe.wait_ge(s["s_exp"], n * 8 + FIRST)
                for t in range(CHUNK_TILES):
                    mm = pe.transpose(maxT_ps[:, t * P:(t + 1) * P], max16[:, t, :], ident16[:, :])
                mm.then_inc(s["maxT_ps"], 1)

            def scores(s, l, c, e, p):
                m = p // 4
                if p == 0:
                    pe.wait_ge(s["maxT_sb"], c + 1)
                if p % 4 == 0:
                    pe.wait_ge(s["q_sb"], c * 2 + (m + 1))
                if not (isinstance(c, int) and c == 0 and p < 2):
                    pe.wait_ge(s["s_exp"], (c * 8 + (p - 1) if p else c * 8) + FIRST)
                out = score[p % 2][:, :]
                pe.matmul(out, k_diag[:, m, 2 * (p % 4):2 * (p % 4) + 2, :].rearrange("p h k -> p (h k)"), qT[e][:, m, :],
                          start=True, stop=False)
                masked = l == 0 and e == 0
                if masked:
                    pe.matmul(score[p % 2][:, 0:KEYS], ident16[:, :], causal_keys16[:, :], start=False, stop=False)
                pe.matmul(out, neg_sel16[:, p, :], maxT16[:, :], start=False, stop=True).then_inc(s["s_ps"], 1)

            def weigh_values(s, c, p):
                m, r = p // 4, 32 * (p % 4)
                pe.wait_ge(s["s_exp"], c * 8 + (p + 1) + FIRST)
                if p % 4 == 0:
                    pe.wait_ge(s["y_ready"], c * 2 + m + FIRST)
                pe.matmul(YB[r:r + 32, :], v_diag[:, 2 * p:2 * p + 2, :].rearrange("p h d -> p (h d)"), probs[:, p % 4, :],
                          start=True, stop=True)
                pe.matmul(DB[r:r + 32, :], pair_mask[:, 0:2, :].rearrange("p h d -> p (h d)"), probs[:, p % 4, :],
                          start=True, stop=True).then_inc(s["pv"], 1)

            def project_out(s, l, c):
                pe.wait_ge(s["y_ready"], c * 2 + 2 + FIRST)
                for g in range(2):
                    for i in range(2):
                        t = 2 * g + i
                        out = mid[g][:, i * DIM:(i + 1) * DIM]
                        for m in range(KH):
                            pe.matmul(out, yT[:, m, t * P:(t + 1) * P], Wo[l][:, m, :], start=(i == 0 and m == 0), stop=False,
                                      skip_group_check=True)
                        mm = pe.matmul(out, ones16[:, :], bias3[:, l, :], start=False, stop=(i == 1),
                                       skip_group_check=True)
                    mm.then_inc(s["o_ps"], 1)

            def chunk_step(s, l, c, e, b, ahead, nxt):
                for p in range(PAIRS):
                    if p == 0 and e == 0:
                        pe.wait_ge(s["kv_diag"], b * 3 + 3)
                    scores(s, l, c, e, p)
                    if nxt:
                        if p < 2 and not (isinstance(c, int) and c == 0):
                            pe.wait_ge(s["x_new"], c * 2 + FIRST)
                        max_scores(s, l, c + 1, e == 1, b + 1 if e == 1 else b, p)
                    if p >= 2:
                        weigh_values(s, c, p - 2)
                    if p == 6 and ahead:
                        transpose_h(s, c + 2)
                for p in range(PAIRS - 2, PAIRS):
                    weigh_values(s, c, p)
                if ahead:
                    project_q(s, l, c + 2, 0)
                if nxt:
                    transpose_max(s, c + 1)
                if ahead:
                    project_q(s, l, c + 2, 1)
                if nxt:
                    pe.wait_ge(s["max_done"], c * 8 + 16)
                elif not (isinstance(c, int) and c == 0):
                    pe.wait_ge(s["x_new"], c * 2 + FIRST)
                project_out(s, l, c)

            def cross_max(n):
                pe.wait_ge(cross_in, n + 1)
                pe.transpose(YB[0:BATCH, 0:P], part_sum[:, :], ident[:, :]).then_inc(cross_ps, 1)
                pe.wait_ge(cross_diag, n + 1)
                pe.matmul(YB[:, P:P + BATCH], ones4[:, :], diag4[:, :], start=True, stop=True).then_inc(cross_out, 1)

            def sum_parts(n):
                pe.wait_ge(part_ready, n)
                pe.matmul(DB[:, 0:BATCH], eighth[:, :], part_sum[:, :], start=True, stop=True).then_inc(sum_ready, 1)

            def light_out(m, t):
                if t == 0:
                    pe.wait_ge(light_g, m + 1)
                    pe.wait_ge(light_added, m * 2)
                out = score[t // 2][:, (t % 2) * DIM:(t % 2 + 1) * DIM]
                pe.matmul(out, light_gT[:, t * P:(t + 1) * P], w2l[:, :], start=(t % 2 == 0), stop=False, skip_group_check=True)
                mm = pe.matmul(out, ones16[:, :], bias3[:, B2_LIGHT, :], start=False, stop=(t % 2 == 1), skip_group_check=True)
                if t % 2 == 1:
                    mm.then_inc(light_o, 1)

            def count_above(b, n, e):
                pe.wait_ge(compared[e % 2], n * 2 + (e // 2 + 1))
                for i in range(8):
                    mm = pe.matmul(counts_ps[:, 8 * b + i:8 * b + i + 1], larger16[e][:, i * P:(i + 1) * P], ones16[:, 0:1],
                                   start=False, stop=False, skip_group_check=True)
                mm.then_inc(counted, 1)

            def light_piece(n, j, b, first):
                if j == 0:
                    pe.wait_ge(copied, n + 1)
                    pe.wait_ge(light_Tsb, n * 2)
                    for k in range(KH):
                        for t in range(CHUNK_TILES):
                            mm = pe.transpose(front[k][:, t * P:(t + 1) * P], h[:, t, k * P:(k + 1) * P], ident[:, :])
                    mm.then_inc(light_T, 1)
                if j < CHUNK_TILES and not first:
                    light_out(n - 1, j)
                if j == 4:
                    pe.wait_ge(light_Tsb, n * 2 + 2)
                    pe.wait_ge(light_g, n)
                if j >= 4:
                    mm = pe.matmul(mid[0][:, :], w1l[:, j - 4, :], hT[:, j - 4, :], start=(j == 4), stop=(j == 5))
                    if j == 5:
                        mm.then_inc(light_h, 1)
                if j in COUNT_SLOTS:
                    count_above(b, n, COUNT_SLOTS.index(j))

            def prefix(n):
                pe.wait_ge(flags_ready, n + 1)
                out, flags = M0[:, 0:TILES].rearrange("p (b c) -> p b c", b=BATCH), flag16[:, :].rearrange("p (b c) -> p b c", b=BATCH)
                mm = pe.matmul(out, before16[:, :], flags, start=True, stop=False, skip_group_check=True)
                for d in range(1, 8):
                    mm = pe.matmul(out[:, :, d:8], ones16[:, :], flags[:, :, 0:8 - d], start=False, stop=(d == 7),
                                   skip_group_check=True)
                if n == 0:
                    mm = pe.matmul(M1[:, 0:BATCH], ones16[:, :], count16[:, :], start=True, stop=True)
                mm.then_inc(prefix_ready, 1)

            def ffn0():
                pe.wait_ge(attn_w_in[1], 16)
                keys_values(S[1], 1)
                cross_max(0)
                pe.wait_ge(logit_ready, CHUNKS)
                for b in range(BATCH):
                    for i in range(2):
                        if b:
                            pe.wait_ge(rows_sb, 2 * b + i - 1)
                        for t in range(4):
                            mm = pe.matmul(score[i][:, t * P:(t + 1) * P],
                                           logit[:, 8 * b + 4 * i + t:8 * b + 4 * i + t + 1].to_broadcast([P, P]),
                                           ident[:, :], start=True, stop=True)
                        mm.then_inc(rows_ps, 1)
                pe.wait_ge(rows_sb, 2 * BATCH)
                pe.wait_ge(ffn0_ready, 5)
                pe.wait_ge(bias_ready, 48)
                pe.matmul(counts_ps, ones16[:, :], zeros16[:, :], start=True, stop=False, skip_group_check=True)

                def route_round(n, i, first=False):
                    for j in range(CHUNK_ITERS):
                        sum_parts(i * CHUNK_ITERS + (sums_before[n] + 2 + j))
                        light_piece(i + 2 * n, j, n, first)

                for n, iters in enumerate(ROUTE_BLOCKS):
                    sum_parts(sums_before[n] + 1)
                    if n == 0:
                        route_round(0, 0, first=True)
                        route_round(0, 1)
                    else:
                        with pe.Fori(0, 2) as i:
                            route_round(n, i)
                    for j in range(2 * CHUNK_ITERS, iters):
                        sum_parts(sums_before[n] + 2 + j)
                        for t in range(2 * (j % 2), 2 * (j % 2) + 2):
                            light_out(CHUNKS - 1, t)
                cross_max(1)
                prefix(0)
                prefix(1)
                with pe.Fori(0, BATCH // 2) as i:
                    for e in range(2):
                        b = i * 2 + e
                        pe.wait_ge(picked_in, b * 16 + 16)
                        pe.wait_ge(heavy_Tsb, b + FIRST)
                        for k in range(KH):
                            for j in range(2):
                                mm = pe.transpose(F0[:, (2 * k + j) * P:(2 * k + j + 1) * P],
                                                  picked[e][:, j, k * P:(k + 1) * P], ident[:, :])
                        mm.then_inc(heavy_T, 1)
                        pe.wait_ge(heavy_Tsb, b + 1 + FIRST)
                        for m in range(HEAVY // P):
                            if m >= 4:
                                pe.wait_ge(heavy_g, b * 8 + (m - 3))
                            for k in range(KH):
                                mm = pe.matmul(heavy_banks[m % 4][:, 0:ROUTED], w1h[:, k, m * P:(m + 1) * P], pickedT[:, k, :],
                                               start=(k == 0), stop=(k == KH - 1))
                            mm.then_inc(heavy_h, 1)
                        pe.wait_ge(heavy_g, b * 8 + 8)
                        pe.wait_ge(heavy_done, b + FIRST)
                        for j in range(2):
                            out = YB[:, j * DIM:(j + 1) * DIM]
                            for m in range(HEAVY // P):
                                pe.matmul(out, heavy_gT[:, m, j * P:(j + 1) * P], w2h[:, m, :], start=(j == 0 and m == 0),
                                          stop=False, skip_group_check=True)
                            mm = pe.matmul(out, ones16[:, :], bias3[:, B2_HEAVY, :], start=False, stop=(j == 1),
                                           skip_group_check=True)
                        mm.then_inc(heavy_o, 1)

            pe.wait_ge(ctx_in, 16)
            pe.wait_ge(consts_in, 16)
            pe.wait_ge(kv_in, 16)
            pe.wait_ge(set_ready, 6)
            for l in range(2):
                s = S[l]
                if l == 1:
                    ffn0()
                if l == 0:
                    keys_values(s, l)
                pe.wait_ge(s["k_sb"], KH)
                for a in range(2):
                    transpose_h(s, a)
                    pe.wait_ge(attn_w_in[l], 16)
                    for m in range(KH):
                        project_q(s, l, a, m)
                    if a == 0:
                        pe.wait_ge(consts16_in, 16)
                        pe.wait_ge(s["k16_ready"], KH)
                        pe.wait_ge(s["v_sb"], BATCH)
                        for j in range(8):
                            max_scores(s, l, 0, True, 0, j)
                        transpose_max(s, 0)
                pe.wait_ge(s["k16_ready"], BATCH * KH)
                pe.wait_ge(wo_ready, l + 1)
                pe.wait_ge(bias_ready, 48)
                with pe.Fori(0, BATCH - 1) as b:
                    for e in range(2):
                        chunk_step(s, l, b * 2 + e, e, b, True, True)
                for e in range(2):
                    chunk_step(s, l, CHUNKS - 2 + e, e, BATCH - 1, False, e == 0)
            pe.wait_ge(gate_in, 16)

            def transpose_rows(c, e):
                pe.wait_ge(G["copied"], c + 1)
                if not isinstance(c, int) or c >= 2:
                    pe.wait_ge(G["hT_sb"], c * 2 - 2)
                for k in range(KH):
                    for t in range(CHUNK_TILES):
                        mm = pe.transpose(rowsT_banks[e][k][:, t * P:(t + 1) * P], rows2[e][:, t, k * P:(k + 1) * P], ident[:, :])
                mm.then_inc(G["hT_ps"], 1)

            def group_sums(c, e):
                pe.wait_ge(G["hT_sb"], c * 2 + 2)
                if not isinstance(c, int) or c >= 2:
                    pe.wait_ge(G["sums_sb"], c - 1 + FIRST)
                for k in range(KH):
                    mm = pe.matmul(mid[e][:, :], conv_bd[:, k, :], rowsT2[e][:, k, :], start=(k == 0), stop=(k == KH - 1))
                mm.then_inc(G["sums_ps"], 1)

            transpose_rows(0, 0)
            transpose_rows(1, 1)
            group_sums(0, 0)
            with pe.Fori(1, CHUNKS // 2) as i:
                for e in range(2):
                    transpose_rows(i * 2 + e, e)
                    group_sums(i * 2 + e - 1, 1 - e)
            group_sums(CHUNKS - 1, 1)
            pe.wait_ge(gate_ready, 2)

            def prepare(t, e):
                pe.wait_ge(G["hs_ready"], t + 1)
                pe.wait_ge(G["hsT_sb"], t)
                for k in range(KH):
                    mm = pe.transpose(F0[:, k * P:(k + 1) * P], hs[e][:, k * P:(k + 1) * P], ident[:, :])
                mm.then_inc(G["hsT_ps"], 1)
                pe.wait_ge(G["acts_ready"], t + 1)
                if not (isinstance(t, int) and t == 0):
                    pe.wait_ge(G["exp_ready"], t * 2 - 2)
                pe.matmul(mid[e][:, :], acts[e], lin_bd[:, :], start=True, stop=False)
                pe.matmul(mid[e][:, :], ones16[:, :], bias3[:, SO_B:SO_B + 2, :].rearrange("p a d -> p (a d)"),
                          start=False, stop=True).then_inc(G["logit_ps"], 1)
                pe.wait_ge(G["hsT_sb"], t + 1)
                if not (isinstance(t, int) and t == 0):
                    pe.wait_ge(G["part_ready"], t - 1 + FIRST)
                for k in range(KH):
                    mm = pe.matmul(score[e][:, 0:DIM], hsT[e][:, k, :], gate_w[:, k, :], start=(k == 0), stop=(k == KH - 1))
                mm.then_inc(G["full_ps"], 1)

            def in_branch(t, e):
                pe.wait_ge(G["sparse_ready"], t + 1)
                pe.wait_ge(G["sparseT_sb"], t)
                for k in range(KH):
                    mm = pe.transpose(F1[:, k * P:(k + 1) * P], sparse[:, k * P:(k + 1) * P], ident[:, :])
                mm.then_inc(G["sparseT_ps"], 1)
                pe.wait_ge(G["sparseT_sb"], t + 1)
                if not (isinstance(t, int) and t == 0):
                    pe.wait_ge(G["x_new"], t - 1 + FIRST)
                for k in range(KH):
                    mm = pe.matmul(out_banks[e][:, 0:DIM], sparseT[:, k, :], gate_w[:, k, :], start=(k == 0), stop=(k == KH - 1))
                mm.then_inc(G["in_ps"], 1)

            def gate_tile(t, e, ahead=True):
                if ahead:
                    prepare(t + 1, 1 - e)
                if not (isinstance(t, int) and t == 0):
                    in_branch(t - 1, 1 - e)

            prepare(0, 0)
            for e in range(2):
                gate_tile(e, e)
            with pe.Fori(1, TILES // 2 - 1) as i:
                for e in range(2):
                    gate_tile(i * 2 + e, e)
            for e in range(2):
                gate_tile(TILES - 2 + e, e, e == 0)
            in_branch(TILES - 1, 1)


def host_arrays(inp):
    import numpy as np
    f = lambda a: np.ascontiguousarray(np.asarray(a))
    bf16_bits = lambda a: (np.ascontiguousarray(a, np.float32).view(np.uint32) >> 16).astype(np.uint16)
    r, col, feature, tile = np.arange(P), np.arange(512), np.arange(DIM), np.arange(TILES)[None, :]
    rows = lambda a: np.asarray(a).reshape(-1, P, np.asarray(a).shape[-1]).transpose(1, 0, 2).reshape(P, -1)
    cols = lambda a: np.asarray(a).reshape(-1, P).T
    pack = lambda *a: np.ascontiguousarray(np.concatenate(a, axis=1))
    d = {"x": f(inp["x"]).reshape(BATCH * TOKENS, DIM)}
    ctx = np.asarray(inp["ctx_1024"]).transpose(2, 0, 1).reshape(KH, P, BATCH, 1, KEYS).transpose(1, 0, 2, 3, 4)
    d["ctxT"] = np.ascontiguousarray(np.repeat(ctx, 2, axis=3)).reshape(P, -1)
    for l in range(2):
        d[f"kvqo{l}"] = pack(*(rows(np.asarray(inp[f"L{l}_xattn_W{w}"]).T) for w in "kvqo"))
    d["gates"] = np.stack([np.asarray(inp["g_xattn"])[0], np.asarray(inp["g_ffn"])[0],
                           np.asarray(inp["g_xattn"])[1], np.asarray(inp["g_ffn"])[1]])
    d["bias_gates"] = d["gates"][[0, 2, 1]].reshape(3, 1)
    d["bias_rows"] = np.stack([np.asarray(inp[n]) for n in (
        "L0_xattn_bo", "L1_xattn_bo", "L0_ffn_b2_light", "L0_ffn_b2_heavy", "L1_ffn_so_lin_b", "L1_ffn_si_lin_b")])
    d["bv1"], d["bias1"], d["token"] = f(inp["L1_xattn_bv"]), f(inp["L1_ffn_bias"]), f(inp["L0_ffn_routing_token"])
    outside = (BATCH * TOKENS + tile * P + r[:, None]).astype(np.float32)
    d["consts"] = pack(
        np.eye(P, dtype=np.float32),
        (r[:, None] // HEAD_DIM == col[None, :] // KEYS).astype(np.float32),
        (r[:, None] // KEYS == (feature[None, :] // HEAD_DIM) % 2).astype(np.float32),
        -outside, outside,
        cols(inp["L1_xattn_bq"]), cols(inp["L1_xattn_bk"]),
        cols(inp["L0_ffn_gamma_light"]), cols(inp["L0_ffn_gamma_heavy"]), cols(inp["L0_ffn_b1_light"]), cols(inp["L0_ffn_b1_heavy"]),
        np.stack([np.concatenate([np.asarray(inp[f"L1_ffn_{br}_{n}"]) for br in ("so", "si")])
                  for n in ("conv_b", "gamma", "beta")], 1))
    pair = np.arange(PAIRS)[None, :, None]
    d["consts16"] = bf16_bits(pack(
        np.eye(P),
        (-1.0 * (r[:, None, None] == 2 * pair + r[None, None, :] // KEYS)).reshape(P, -1),
        np.where(col[None, :] % KEYS > r[:, None], -1e30, 0.0),
        np.where(r[:, None] % KEYS > np.arange(KEYS)[None, :], -1e30, 0.0),
        r[:, None] < r[None, :]))
    d["light_w"] = pack(rows(inp["L0_ffn_w1_light"]), rows(inp["L0_ffn_w2_light"]))
    d["heavy_w"] = pack(rows(inp["L0_ffn_w1_heavy"]), rows(inp["L0_ffn_w2_heavy"]))
    conv, lin = np.zeros((DIM, P), np.float32), np.zeros((P, 2 * DIM), np.float32)
    for i, br in enumerate(("so", "si")):
        conv[feature, i * GROUPS + feature // 4] = np.asarray(inp[f"L1_ffn_{br}_conv_w"]).reshape(-1)
        lin[i * GROUPS:(i + 1) * GROUPS, i * DIM:(i + 1) * DIM] = np.asarray(inp[f"L1_ffn_{br}_lin_w"]).T
    d["gate_all"] = pack(rows(conv), rows(inp["L1_ffn_weight"]), lin)
    return d


def kernel(**inputs):
    import concourse.bacc as bacc
    from concourse.bass_utils import run_bass_kernel_spmd

    nc = bacc.Bacc("TRN2", target_bir_lowering=False, num_devices=1)
    arrays = host_arrays(inputs)
    A = {n: nc.dram_tensor(f"in_{n}", a.shape, mybir.dt.from_np(a.dtype), kind="ExternalInput").ap()
         for n, a in arrays.items()}
    A["out"] = nc.dram_tensor("out", (BATCH * TOKENS, DIM), F32, kind="ExternalOutput").ap()
    build(nc, A)
    r = run_bass_kernel_spmd(nc, [{f"in_{n}": a for n, a in arrays.items()}], core_ids=[0])
    return r.results[0]["out"].reshape(BATCH, TOKENS, DIM)
```

```python
import math
from contextlib import ExitStack

import concourse.bass as bass
from concourse import mybir

F32 = mybir.dt.float32
F32R = mybir.dt.float32r
BF16 = mybir.dt.bfloat16
U32 = mybir.dt.uint32
ALU = mybir.AluOpType
ACT = mybir.ActivationFunctionType
AX_X = mybir.AxisListType.X
ds = bass.ds

P = 128
BATCH, TOKENS, DIM = 4, 1024, 256
KEYS, HEADS, HEAD_DIM = 64, 16, 16
KH = DIM // P
TILES = BATCH * TOKENS // P
CHUNK_TILES = 4
CHUNK = CHUNK_TILES * P
CHUNKS = TILES // CHUNK_TILES
PAIRS = HEADS // 2
SCALE = HEAD_DIM ** -0.5
LN_EPS = 1e-5

LIGHT, HEAVY = 128, 1024
ROUTED = 256
ROUTE_ITERS, ROUTE_K, ROUTE_EPS = 50, 8.0, 0.1
TOPK = 32
FOUND = -1e30
LOG_TINY = -87.33654
LOG_SHIFT = 40
GROUPS = DIM // 4
BN_EPS = 1e-5
FIRST = 1


class Chain:

    def __init__(self, eng, sem):
        self.eng, self.sem, self.base, self.k, self.i, self.per = eng, sem, 0, 0, None, 0

    def did(self, ins):
        ins.then_inc(self.sem, 1)
        self.k += 1
        return ins

    def at(self):
        return self.base + self.k if self.i is None else self.i * self.per + (self.base + self.k)

    def settle(self):
        self.eng.wait_ge(self.sem, self.at())

    def enter(self, i, per):
        self.base, self.k, self.i, self.per = self.base + self.k, 0, i, per

    def leave(self, trips):
        assert self.k == self.per, (self.k, self.per)
        self.base, self.k, self.i = self.base + trips * self.per, 0, None


def build(nc, A):
    with ExitStack() as ctx:
        def sb(name, shape, dt=F32):
            return ctx.enter_context(nc.sbuf_tensor(name, shape, dt))

        def sem(name):
            return ctx.enter_context(nc.semaphore(name))

        x = sb("x", [P, TILES, DIM])
        def parts(name, widths, dt=F32):
            whole, at0, views = sb(name, [P, sum(widths)], dt), 0, []
            for w in widths:
                views.append(whole[:, at0:at0 + w])
                at0 += w
            return whole, views

        consts, (ident, head_mask, pair_mask, slot_base, qkv_bias, ffn0_cols, bn_cols) = parts(
            "consts", [P, 8 * KEYS, DIM, 2 * TILES, 4, 13, 3])
        head_mask = head_mask.rearrange("p (h k) -> p h k", h=8)
        pair_mask = pair_mask.rearrange("p (h d) -> p h d", h=HEADS)
        slot_base = slot_base.rearrange("p (a n) -> p a n", a=2)
        consts16, (ident16, neg_sel16, causal_rows16, causal_keys16, before16) = parts(
            "consts16", [P, PAIRS * P, 512, KEYS, P], BF16)
        neg_sel16 = neg_sel16.rearrange("p (a n) -> p a n", a=PAIRS)
        ctx_all, (ctxT,) = parts("ctx_all", [KH * BATCH * 2 * KEYS])
        ctxT = ctxT.rearrange("p (k b r n) -> p k b r n", k=KH, b=BATCH, r=2)
        kvqo, Wk, Wv, Wq, Wo = [], [], [], [], []
        for l in range(2):
            whole, views = parts(f"kvqo{l}", [KH * DIM] * 4)
            kvqo.append(whole)
            for w, v in zip((Wk, Wv, Wq, Wo), views):
                w.append(v.rearrange("p (k n) -> p k n", k=KH))
        light_w, (w1l, w2l) = parts("light_w", [KH * LIGHT, DIM])
        w1l = w1l.rearrange("p (k n) -> p k n", k=KH)
        heavy_w, (w1h, w2h) = parts("heavy_w", [KH * HEAVY, HEAVY // P * DIM])
        w1h, w2h = w1h.rearrange("p (k n) -> p k n", k=KH), w2h.rearrange("p (m n) -> p m n", m=HEAVY // P)
        gate_all, (conv_bd, gate_w, lin_bd) = parts("gate_all", [KH * P, KH * DIM, 2 * DIM])
        conv_bd, gate_w = (w.rearrange("p (k n) -> p k n", k=KH) for w in (conv_bd, gate_w))
        ones16 = sb("ones16", [P, P], BF16)
        gates = sb("gates", [P, 4])
        v_bias, bias1 = sb("v_bias", [P, DIM]), sb("bias1", [P, DIM])
        BO0, BO1, B2_LIGHT, B2_HEAVY, SO_B, SI_B = range(6)
        bias_gates = sb("bias_gates", [3, 1])
        bias3 = sb("bias3", [P, 6, DIM], BF16)
        arena = sb("arena", [P, 10496])

        def at(first, words, pattern=None, **sizes):
            flat = arena[:, first:first + words]
            return flat.rearrange(pattern, **sizes) if pattern else flat

        DEN, PROBS, YT, H, HT, K16, KT, VALL, Q16, VD = 0, 1024, 3072, 4096, 5120, 6144, 8192, 8704, 9728, 10240
        qT, q_low = ([sb(f"{n}{i}", [P, KH, CHUNK], F32R) for i in range(2)] for n in ("qT", "q_low"))
        inv_den = at(DEN, 1024, "p (m n) -> p m n", m=KH)
        probs = at(PROBS, 2048, "p (a n) -> p a n", a=4)
        yT = at(YT, 1024, "p (m n) -> p m n", m=KH)
        h = at(H, 1024, "p (t d) -> p t d", t=CHUNK_TILES)
        hT = at(HT, 1024, "p (m n) -> p m n", m=KH)
        k16 = at(K16, 2048).bitcast(BF16).rearrange("p (b m h k) -> p b m h k", b=BATCH, m=KH, h=8)
        kT = at(KT, 512, "p (m b k) -> p m b k", m=KH, b=BATCH)
        kT_low = sb("kT_low", [P, KH, BATCH, KEYS])
        v_all = at(VALL, 1024, "p (b d) -> p b d", b=BATCH)
        k_diag, k_diag_low = (sb(n, [P, KH, 8, KEYS], F32R) for n in ("k_diag", "k_diag_low"))
        q16 = at(Q16, 512).bitcast(BF16).rearrange("p (m n) -> p m n", m=KH)
        v_diag = at(VD, 256, "p (h d) -> p h d", h=HEADS)
        heavy_gT = at(PROBS, 2048, "p (m n) -> p m n", m=HEAVY // P)
        light_gT = at(YT, 512)
        bias_rows = at(YT, 256)[0:6, :]
        bias_piece = [at(YT + 256 + 128 * k, 128).bitcast(BF16)[0:6, :] for k in range(3)]
        larger16 = [at(DEN + i * 512, 512).bitcast(BF16) for i in range(4)]
        picked = [at(first, 2 * (DIM + 1), "p (j d) -> p j d", j=2) for first in (YT, HT)]
        pickedT = at(Q16, 512, "p (k n) -> p k n", k=KH)
        heavy_y = [at(DEN + i * 512, 512, "p (j d) -> p j d", j=2) for i in range(2)]
        row_stats = sb("row_stats", [P, CHUNK_TILES, 6])
        mean_var = sb("mean_var", [P, CHUNK_TILES, 2])
        var_eps = sb("var_eps", [P, CHUNK_TILES])
        minus_half = sb("minus_half", [P, CHUNK_TILES])
        rstd = sb("rstd", [P, CHUNK_TILES])
        minus_mean = sb("minus_mean", [P, CHUNK_TILES])
        shift = sb("shift", [P, CHUNK_TILES])
        max16 = sb("max16", [P, CHUNK_TILES, HEADS], BF16)
        maxT16 = sb("maxT16", [P, CHUNK], BF16)
        token_row = sb("token_row", [P, DIM])
        ROW = DIM + 1
        normed = sb("normed", [P, TILES, ROW])
        big = sb("big", [P, BATCH * TOKENS])
        logit_rows = big[:, :].rearrange("p (b n) -> p b n", b=BATCH)
        heavy_rows = [big[:, i * 8 * DIM:(i + 1) * 8 * DIM].rearrange("p (t d) -> p t d", t=8) for i in range(2)]
        route_stats = sb("route_stats", [P, CHUNK_TILES, 6])
        route_mv = sb("route_mv", [P, CHUNK_TILES, 2])
        route_var = sb("route_var", [P, 6, CHUNK_TILES])
        row_scale = sb("row_scale", [P, CHUNK_TILES])
        row_norm = sb("row_norm", [P, TILES])
        raw_dot = sb("raw_dot", [P, CHUNK_TILES])
        dot_out = big[:, 0:DIM]
        logit = sb("logit", [P, TILES])
        level = sb("level", [P, BATCH])
        top_logit = sb("top_logit", [P, BATCH])
        minus_a = sb("minus_a", [P, BATCH])
        log_sum = sb("log_sum", [P, BATCH])
        args = sb("args", [P, TILES + BATCH])
        exps = sb("exps", [P, TILES + BATCH])
        capped = sb("capped", [P, TILES])
        part_sum = sb("part_sum", [P, BATCH])
        eighth = sb("eighth", [P, P])
        diag4 = sb("diag4", [4, BATCH])
        col4 = sb("col4", [4, 1])
        score_of = sb("score_of", [P, TILES])
        pick = at(HT + 512, 4 * TILES, "p (a n) -> p a n", a=4)
        flag16 = sb("flag16", [P, TILES], BF16)
        count16 = sb("count16", [P, BATCH], BF16)
        slot = sb("slot", [P, TILES], U32)
        pick_gate = sb("pick_gate", [P, 2])
        rows_in = [nc.dram_tensor(f"rows_in{b}", (ROUTED, ROW), F32, kind="Internal").ap() for b in range(BATCH)]
        rows_out = [nc.dram_tensor(f"rows_out{b}", (ROUTED, DIM), F32, kind="Internal").ap() for b in range(BATCH)]

        groups = big[:, :]
        bn_parts = sb("bn_parts", [P, CHUNKS * 6])
        bn_mv = sb("bn_mv", [P, 2])
        bn_tmp = sb("bn_tmp", [P, 5])
        rows2 = [at(first, 1024, "p (t d) -> p t d", t=CHUNK_TILES) for first in (H, PROBS)]
        rowsT2 = [at(first, 1024, "p (m n) -> p m n", m=KH) for first in (HT, DEN)]
        hs = [at(i * 256, 256) for i in range(2)]
        hsT = [at(512 + i * 256, 256, "p (k n) -> p k n", k=KH) for i in range(2)]
        acts = [at(1024 + i * 128, 128) for i in range(2)]
        work = [at(1280 + i * 512, 512) for i in range(2)]
        expw = [at(first, 512) for first in (2304, 4096)]
        taken = at(2816, 512)
        out_part = at(3328, 256)
        sparse = at(3584, 256)
        sparseT = at(3840, 256, "p (k n) -> p k n", k=KH)
        in_part = [at(K16 + i * 256, 256) for i in range(2)]
        top8 = at(4608, 64, "p (r b n) -> p r b n", r=4, b=2)
        zeros16 = sb("zeros16", [P, TILES], BF16)
        minus_top = [sb(f"minus_top{i}", [P, 2]) for i in range(2)]
        exp_sum = sb("exp_sum", [P, 2])
        inv_sum = [sb(f"inv_sum{i}", [P, 2]) for i in range(2)]
        bank = [ctx.enter_context(nc.psum_tensor(f"bank{i}", [P, 512], F32)) for i in range(8)]
        F0, F1, M0, M1, S0, S1, YB, DB = bank
        front = [F0, F1]
        mid = [M0, M1]
        score = [S0, S1]
        out_banks = [YB, DB]
        rowsT_banks = [front, score]
        heavy_banks = [M0, M1, S0, S1]
        CHUNK_ITERS = 6
        COUNT_SLOTS = [1, 2, 3, 5]
        ROUTE_BLOCKS = [12, 12, 12, 14]
        assert sum(ROUTE_BLOCKS) == ROUTE_ITERS and len(ROUTE_BLOCKS) == BATCH
        sums_before = [sum(ROUTE_BLOCKS[:n]) + n for n in range(BATCH + 1)]
        counts_ps = M1[:, 0:TILES]
        maxT_ps = S0[0:HEADS, 0:CHUNK // 2].bitcast(BF16)

        x_in = [sem(f"x_in{i}") for i in range(3)]
        keys_in, gates_in, consts_in, consts16_in = (sem(n) for n in ("keys_in", "gates_in", "consts_in", "consts16_in"))
        attn_w_in = [sem(f"attn_w_in{l}") for l in range(2)]
        bias_in = sem("bias_in")
        gates_ready, set_ready, wo_ready = sem("gates_ready"), sem("set_ready"), sem("wo_ready")
        pieces_ready, bias_ready = sem("pieces_ready"), sem("bias_ready")
        dve_step, pool_step, act_step = sem("dve_step"), sem("pool_step"), sem("act_step")
        top_step = sem("top_step")
        out_done, waits_taken = sem("out_done"), sem("waits_taken")
        names = ("k_low q_low k_ps k_sb k16_ready v_ps v_sb stats rstd_ready h_ready hT_ps hT_sb q_ps q_sb q16_ready "
                 "max_ps max_done maxT_ps maxT_sb s_ps s_exp pv inv_ready y_ready o_ps x_new kv_diag").split()
        ffn0_in, route_in = sem("ffn0_in"), sem("route_in")
        ffn0_ready = sem("ffn0_ready")
        route_stats_ready, scale_ready, logit_ready = sem("route_stats_ready"), sem("scale_ready"), sem("logit_ready")
        rows_ps, rows_sb = sem("rows_ps"), sem("rows_sb")
        compared, counted = [sem("compared_pool"), sem("compared_dve")], sem("counted")
        cross_in, cross_ps, cross_diag, cross_out = (sem(n) for n in ("cross_in", "cross_ps", "cross_diag", "cross_out"))
        part_ready, sum_ready, log_ready, args_ready, exps_ready = (sem(n) for n in ("part_ready", "sum_ready", "log_ready", "args_ready", "exps_ready"))
        score_arg, score_ready = sem("score_arg"), sem("score_ready")
        flags_ready, prefix_ready, slot_ready = sem("flags_ready"), sem("prefix_ready"), sem("slot_ready")
        copied, light_T, light_Tsb, light_h, light_g, light_o, light_added = (
            sem(n) for n in ("copied", "light_T", "light_Tsb", "light_h", "light_g", "light_o", "light_added"))
        scattered = [sem(f"scattered{b}") for b in range(BATCH)]
        picked_in, stored = sem("picked_in"), sem("stored")
        gathered = [sem(f"gathered{b}") for b in range(BATCH)]
        heavy_room = sem("heavy_room")
        heavy_T, heavy_Tsb, heavy_h, heavy_g, heavy_o, heavy_done, mixed = (
            sem(n) for n in ("heavy_T", "heavy_Tsb", "heavy_h", "heavy_g", "heavy_o", "heavy_done", "mixed"))
        S = [{n: sem(f"{n}_{l}") for n in names} for l in range(2)]
        gate_in, gate_ready = sem("gate_in"), sem("gate_ready")
        G = {n: sem(f"g_{n}") for n in (
            "stats rstd_ready h_ready copied bias_added hT_ps hT_sb sums_ps sums_sb bn_done bn_ready hs_ready acts_ready hsT_ps hsT_sb "
            "logit_ps full_ps work_ready minus_ready exp_ready top_ready taken_ready part_ready sparse_ready sparseT_ps "
            "sparseT_sb in_ps in_scaled part_added x_new").split()}

        start_at_first = (
            [s[n] for s in S for n in ("s_exp", "x_new", "y_ready")] +
            [G[n] for n in ("in_scaled", "sums_sb")] +
            [heavy_Tsb, heavy_done, heavy_o, light_o])

        block = ctx.enter_context(nc.Block())

        x_dram = A["x"].rearrange("(n p) d -> p n d", p=P)
        out_dram = A["out"].rearrange("(n p) d -> p n d", p=P)

        def halves(w):
            return w.rearrange("(k p) n -> p k n", p=P)

        def plain(eng):
            eng.sem_inc(waits_taken, 1)

        @block.sync
        def _(sp):
            sp.dma_start(x[:, 0:4, :], x_dram[:, 0:4, :]).then_inc(x_in[0], 16)
            sp.dma_start(ctx_all[:, :], A["ctxT"]).then_inc(keys_in, 16)
            HALF = 2 * KH * DIM
            sp.dma_start(kvqo[0][:, 0:HALF], A["kvqo0"][:, 0:HALF]).then_inc(keys_in, 16)
            sp.dma_start(kvqo[0][:, HALF:], A["kvqo0"][:, HALF:]).then_inc(attn_w_in[0], 16)
            sp.dma_start(x[:, 4:8, :], x_dram[:, 4:8, :]).then_inc(x_in[1], 16)
            sp.dma_start(x[:, 8:TILES, :], x_dram[:, 8:TILES, :]).then_inc(x_in[2], 16)
            sp.dma_start(light_w[:, :], A["light_w"]).then_inc(ffn0_in, 16)
            sp.dma_start(heavy_w[:, :], A["heavy_w"]).then_inc(ffn0_in, 16)
            sp.dma_start(kvqo[1][:, :], A["kvqo1"]).then_inc(attn_w_in[1], 16)
            sp.dma_start(gate_all[:, :], A["gate_all"]).then_inc(gate_in, 16)
            sp.wait_ge(pieces_ready, 1)
            for k in range(3):
                sp.dma_start(bias3[k:k + 1, :, :].rearrange("p j d -> p (j d)"), bias_piece[k][:, :]).then_inc(bias_ready, 16)

            def load_picked(b):
                sp.wait_ge(scattered[b], 16 * 8)
                if b >= 2:
                    sp.wait_ge(heavy_T, b - 1)
                    sp.wait_ge(heavy_done, b - 1 + FIRST)
                sp.dma_start(picked[b % 2][:, :, :], rows_in[b].rearrange("(j p) d -> p j d", p=P))\
                  .then_inc(picked_in, 16)
                sp.wait_ge(picked_in, 16 * (b + 1))

            def store_heavy(b):
                sp.wait_ge(heavy_done, b + 1 + FIRST)
                sp.dma_start(rows_out[b].rearrange("(j p) d -> p j d", p=P), heavy_y[b % 2][:, :, :])\
                  .then_inc(stored, 16)
                sp.wait_ge(stored, 16 * (b + 1))
                sp.sem_inc(heavy_room, 1)

            sp.sem_inc(heavy_room, 2)
            load_picked(0)
            load_picked(1)
            for b in range(BATCH):
                store_heavy(b)
                if b + 2 < BATCH:
                    load_picked(b + 2)
            for b in range(BATCH):
                sp.wait_ge(G["x_new"], 8 * (b + 1))
                sp.dma_start(out_dram[:, 8 * b:8 * b + 8, :], x[:, 8 * b:8 * b + 8, :]).then_inc(out_done, 16)
            sp.wait_ge(out_done, 16 * BATCH)

        @block.gpsimd
        def _(pool):
            for first in start_at_first:
                pool.sem_inc(first, FIRST)
            step = Chain(pool, pool_step)
            pool.memset(minus_half[:, :], -0.5).then_inc(set_ready, 1)
            pool.memset(ones16[:, :], 1.0).then_inc(set_ready, 1)
            pool.memset(maxT16[:, :], 0.0).then_inc(set_ready, 1)

            pool.memset(eighth[:, :], 1.0 / ROUTE_K).then_inc(set_ready, 1)
            pool.memset(zeros16[:, :], 0.0).then_inc(set_ready, 1)

            def row_rstd(s, n):
                pool.wait_ge(s["stats"], n)
                if not (isinstance(n, int) and n == 1):
                    pool.wait_ge(s["h_ready"], n - 1)
                plain(pool)
                step.did(pool.tensor_scalar(var_eps[:, :], mean_var[:, :, 1], LN_EPS, None, ALU.add))
                step.did(pool.tensor_scalar(minus_mean[:, :], mean_var[:, :, 0], -1.0, None, ALU.mult))
                step.settle()
                step.did(pool.tensor_tensor(rstd[:, :], var_eps[:, :], minus_half[:, :], ALU.pow))
                step.settle()
                pool.tensor_tensor(shift[:, :], minus_mean[:, :], rstd[:, :], ALU.mult).then_inc(s["rstd_ready"], 1)

            def keys16(s, batches):
                for b in batches:
                    for m in range(KH):
                        pool.wait_ge(s["k_sb"], m + 1)
                        pool.tensor_tensor(k16[:, b, m, :, :], kT[:, m, b, :].unsqueeze(1).to_broadcast([P, 8, KEYS]),
                                           head_mask[:, :, :], ALU.mult).then_inc(s["k16_ready"], 1)

            def row_scales(c):
                pool.wait_ge(route_stats_ready, c + 1)
                plain(pool)
                v = [route_var[:, i, :] for i in range(6)]
                step.did(pool.tensor_scalar(v[0], route_mv[:, :, 1], LN_EPS, None, ALU.add))
                step.settle()
                step.did(pool.tensor_tensor(v[1], v[0], minus_half[:, :], ALU.pow))
                step.settle()
                step.did(pool.tensor_tensor(v[2], v[1], v[1], ALU.mult))
                step.settle()
                step.did(pool.tensor_tensor(v[3], v[2], route_mv[:, :, 1], ALU.mult))
                step.settle()
                plain(pool)
                step.did(pool.tensor_scalar(v[4], v[3], (1e-12 / 16.0) ** 2, None, ALU.max))
                step.settle()
                step.did(pool.tensor_tensor(v[5], v[4], minus_half[:, :], ALU.pow))
                step.settle()
                pool.tensor_tensor(row_scale[:, :], v[5], v[1], ALU.mult).then_inc(scale_ready, 1)
                pool.tensor_tensor(row_norm[:, ds(c * 4, 4)], v[5], v[4], ALU.mult).then_inc(scale_ready, 1)

            def route_rows():
                for k in range(0, TILES, 2):
                    if k % 8 == 0:
                        pool.wait_ge(rows_sb, 2 * (k // 8) + 2)
                    if k >= 4:
                        pool.wait_ge(counted, k - 3)
                    pool.tensor_scalar(larger16[k % 4], logit_rows[:, k // 8, :], logit[:, k:k + 1], None,
                                       ALU.is_lt).then_inc(compared[0], 1)

                def clear(i):
                    step.did(pool.memset(heavy_rows[i][:, :, :], 0.0))
                for n in range(2):
                    pool.wait_ge(compared[n], TILES // 2)
                for i in range(2):
                    clear(i)
                step.settle()
                keys16(S[1], range(BATCH))
                pool.wait_ge(slot_ready, 1)
                for b in range(BATCH):
                    for t in range(8 * b, 8 * b + 8):
                        pool.indirect_dma_start(rows_in[b], bass.IndirectOffsetOnAxis(ap=slot[:, t:t + 1], axis=0),
                                                normed[:, t, :], None, bounds_check=ROUTED - 1,
                                                oob_is_err=False).then_inc(scattered[b], 16)

                def gather(b):
                    pool.wait_ge(stored, 16 * (b + 1))
                    for t in range(8 * b, 8 * b + 8):
                        pool.indirect_dma_start(heavy_rows[b % 2][:, t - 8 * b, :], None, rows_out[b],
                                                bass.IndirectOffsetOnAxis(ap=slot[:, t:t + 1], axis=0),
                                                bounds_check=ROUTED - 1, oob_is_err=False).then_inc(gathered[b], 16)

                pool.wait_ge(light_added, 2 * CHUNKS)
                for b in range(BATCH - 1):
                    gather(b)
                    if b == 1:
                        row_rstd(S[1], 1)
                    if b < 2:
                        pool.wait_ge(mixed, b + 1)
                        clear(b)
                        step.settle()
                row_rstd(S[1], 2)
                gather(BATCH - 1)
                pool.wait_ge(gathered[BATCH - 1], 16 * 8)
                pool.tensor_tensor(x[:, TILES - 8:, :], x[:, TILES - 8:, :], heavy_rows[1][:, :, :], ALU.add).then_inc(mixed, 1)

            def gate_norm():
                pool.wait_ge(G["bn_done"], 1)
                pool.wait_ge(G["bias_added"], CHUNKS)
                c = [bn_tmp[:, i:i + 1] for i in range(5)]
                step.did(pool.tensor_scalar(c[0], bn_mv[:, 1:2], BN_EPS, None, ALU.add))
                step.settle()
                step.did(pool.tensor_tensor(c[1], c[0], minus_half[:, 0:1], ALU.pow))
                step.settle()
                step.did(pool.tensor_tensor(c[2], c[1], bn_cols[:, 1:2], ALU.mult))
                step.settle()
                step.did(pool.tensor_tensor(c[3], c[2], bn_mv[:, 0:1], ALU.mult))
                step.settle()
                pool.tensor_tensor(c[4], bn_cols[:, 2:3], c[3], ALU.subtract).then_inc(G["bn_ready"], 1)

            def add_in(t, e):
                pool.wait_ge(G["in_scaled"], t + 1 + FIRST)
                pool.wait_ge(G["part_added"], t + 1)
                rows = x[:, ds(t, 1), :].rearrange("p a d -> p (a d)")
                pool.tensor_tensor(rows, rows, in_part[e], ALU.add).then_inc(G["x_new"], 1)

            def gate_tile(t, e):
                pool.wait_ge(G["part_ready"], t * 3 + 2)
                pool.wait_ge(G["sparseT_ps"], t)
                pool.tensor_tensor(taken, expw[e], taken, ALU.subtract).then_inc(G["taken_ready"], 1)
                pool.wait_ge(G["taken_ready"], t + 1)
                pool.tensor_tensor(sparse, taken[:, DIM:], normed[:, ds(t, 1), 0:DIM].rearrange("p a d -> p (a d)"), ALU.mult).then_inc(G["sparse_ready"], 1)
                if not isinstance(t, int) or t >= 2:
                    add_in(t - 2, e)
                pool.wait_ge(G["part_ready"], t * 3 + 3)
                rows = x[:, ds(t, 1), :].rearrange("p a d -> p (a d)")
                step.did(pool.tensor_tensor(out_part, out_part, taken[:, 0:DIM], ALU.mult))
                step.settle()
                pool.tensor_tensor(rows, rows, out_part, ALU.add).then_inc(G["part_added"], 1)

            def gate_scales(c):
                pool.wait_ge(G["stats"], c + 1)
                plain(pool)
                step.did(pool.tensor_scalar(route_var[:, 0, :], route_mv[:, :, 1], LN_EPS, None, ALU.add))
                step.settle()
                pool.tensor_tensor(row_scale[:, :], route_var[:, 0, :], minus_half[:, :], ALU.pow).then_inc(G["rstd_ready"], 1)
                pool.wait_ge(G["h_ready"], c + 1)
                pool.wait_ge(gate_ready, 2)
                rows = x[:, ds(c * 4, 4), :]
                pool.tensor_tensor(rows, rows, bias1[:, :].unsqueeze(1).to_broadcast([P, CHUNK_TILES, DIM]),
                                   ALU.add).then_inc(G["bias_added"], 1)

            pool.wait_ge(set_ready, 1)
            pool.wait_ge(consts_in, 16)
            for l in range(2):
                s = S[l]
                if l == 0:
                    row_rstd(s, 1)
                    keys16(s, range(1))
                    row_rstd(s, 2)
                    keys16(s, range(1, BATCH))
                row_rstd(s, 3)
                with pool.Fori(1, CHUNKS - 2) as c:
                    step.enter(c - 1, 3 + (6 if l == 0 else 1))
                    row_rstd(s, c + 3)
                    scales = row_scales if l == 0 else gate_scales
                    scales(c - 1)
                    step.leave(CHUNKS - 3)
                for c in range(CHUNKS - 3, CHUNKS):
                    scales(c)
                if l == 0:
                    route_rows()
            gate_norm()
            for e in range(2):
                gate_tile(e, e)
            with pool.Fori(1, TILES // 2) as i:
                step.enter(i - 1, 2)
                for e in range(2):
                    gate_tile(i * 2 + e, e)
                step.leave(TILES // 2 - 1)
            for e in range(2):
                add_in(TILES - 2 + e, e)

        @block.scalar
        def _(act):
            act.dma_start(consts[:, :], A["consts"]).then_inc(consts_in, 16)
            act.dma_start(consts16[:, :], A["consts16"].bitcast(BF16)).then_inc(consts16_in, 16)
            act.dma_start(gates[:, :], A["gates"].partition_broadcast(P)).then_inc(gates_in, 16)
            act.dma_start(bias_gates[:, :], A["bias_gates"]).then_inc(gates_in, 16)
            act.dma_start(bias_rows[:, :], A["bias_rows"]).then_inc(bias_in, 16)
            act.dma_start(token_row[:, :], A["token"].partition_broadcast(P)).then_inc(route_in, 16)
            act.dma_start(v_bias[:, :], A["bv1"].partition_broadcast(P)).then_inc(route_in, 16)
            act.dma_start(bias1[:, :], A["bias1"].partition_broadcast(P)).then_inc(route_in, 16)
            act.wait_ge(gates_in, 32)
            act.activation(gates[:, :], gates[:, :], ACT.Tanh).then_inc(gates_ready, 1)
            act.activation(bias_gates[:, :], bias_gates[:, :], ACT.Tanh).then_inc(gates_ready, 1)

            def keys(s, l):
                for m in range(KH):
                    act.wait_ge(s["k_ps"], m + 1)
                    src = front[m][:, 0:BATCH * KEYS].rearrange("p (b n) -> p b n", b=BATCH)
                    if l == 0:
                        act.activation(kT[:, m, :, :].bitcast(F32R), src, ACT.Copy).then_inc(s["k_sb"], 1)
                    else:
                        act.activation(kT[:, m, :, :].bitcast(F32R), src, ACT.Identity, bias=qkv_bias[:, 2 + m:3 + m]).then_inc(s["k_sb"], 1)

            def normalize(s, tile0, a):
                act.wait_ge(s["rstd_ready"], a + 1)
                if not (isinstance(a, int) and a == 0):
                    act.wait_ge(s["hT_ps"], a)
                for t in range(CHUNK_TILES):
                    ins = act.activation(h[:, t, :], x[:, ds(tile0 + t, 1), :].rearrange("p a d -> p (a d)"), ACT.Identity,
                                         bias=shift[:, t:t + 1], scale=rstd[:, t:t + 1])
                ins.then_inc(s["h_ready"], 1)

            def evac_hT(s, a):
                act.wait_ge(s["hT_ps"], a + 1)
                if not (isinstance(a, int) and a == 0):
                    act.wait_ge(s["q_ps"], a * 2)
                for k in range(KH):
                    act.activation(hT[:, k, :], front[k][:, :], ACT.Copy).then_inc(s["hT_sb"], 1)

            def evac_q(s, l, a, e, m):
                act.wait_ge(s["q_ps"], a * 2 + (m + 1))
                if not isinstance(a, int) or a >= 2:
                    act.wait_ge(s["s_ps"], a * 8 - 8)
                if not (isinstance(a, int) and a == 0):
                    act.wait_ge(s["max_ps"], a * 8)
                for q, ready in ((q16, "q16_ready"), (qT[e], "q_sb")):
                    if l == 0:
                        act.activation(q[:, m, :], front[m][:, :], ACT.Copy).then_inc(s[ready], 1)
                    else:
                        act.activation(q[:, m, :], front[m][:, :], ACT.Identity, bias=qkv_bias[:, m:m + 1]).then_inc(s[ready], 1)

            def evac_maxT(s, n):
                act.wait_ge(s["maxT_ps"], n + 1)
                if not (isinstance(n, int) and n == 0):
                    act.wait_ge(s["s_ps"], n * 8)
                act.activation(maxT16[0:HEADS, :], maxT_ps, ACT.Copy).then_inc(s["maxT_sb"], 1)

            def exp(s, c, p):
                act.wait_ge(s["s_ps"], c * 8 + (p + 1))
                act.wait_ge(s["pv"], c * 8 + (p + 1))
                act.activation(probs[:, p % 4, :], score[p % 2][:, :], ACT.Exp, scale=SCALE).then_inc(s["s_exp"], 1)

            def inverse(s, step, c, m):
                act.wait_ge(s["pv"], c * 8 + (4 * m + 4 + 4))
                act.wait_ge(s["y_ready"], c * 2 + m + FIRST)
                step.did(act.activation(inv_den[:, m, :], DB[:, :], ACT.Ln))
                step.settle()
                act.activation(inv_den[:, m, :], inv_den[:, m, :], ACT.Exp, scale=-1.0).then_inc(s["inv_ready"], 1)

            def chunk_step(s, l, step, c, e, ahead, nxt):
                for p in range(PAIRS):
                    exp(s, c, p)
                    if p == 3 and ahead:
                        normalize(s, c * 4 + 8, c + 2)
                    if p == 4:
                        inverse(s, step, c, 0)
                    if p == 6 and ahead:
                        evac_hT(s, c + 2)
                inverse(s, step, c, 1)
                if ahead:
                    evac_q(s, l, c + 2, e, 0)
                if nxt:
                    evac_maxT(s, c + 1)
                if ahead:
                    evac_q(s, l, c + 2, e, 1)

            def ffn0():
                keys(S[1], 1)
                def save_rows(b):
                    for i in range(2):
                        act.wait_ge(rows_ps, 2 * b + i + 1)
                        act.activation(logit_rows[:, b, i * 512:(i + 1) * 512], score[i][:, :], ACT.Copy).then_inc(rows_sb, 1)

                save_rows(0)
                act.wait_ge(args_ready, 1)
                act.activation(exps[:, :], args[:, :], ACT.Exp).then_inc(exps_ready, 1)

                def copy_rows(n):
                    act.activation(h[:, :, :], normed[:, ds(n * 4, 4), 0:DIM], ACT.Copy).then_inc(copied, 1)

                def light_chunk(n, more):
                    act.wait_ge(light_T, n + 1)
                    for k in range(KH):
                        act.activation(hT[:, k, :], front[k][:, :], ACT.Copy).then_inc(light_Tsb, 1)
                    if more:
                        copy_rows(n + 1)
                    act.wait_ge(light_h, n + 1)
                    act.wait_ge(light_o, n * 2 + FIRST)
                    act.activation(light_gT, mid[0][:, :], ACT.Gelu, bias=ffn0_cols[:, 4:5]).then_inc(light_g, 1)

                def relevel(n):
                    act.wait_ge(sum_ready, n)
                    act.activation(log_sum[:, :], DB[:, 0:BATCH], ACT.Ln, scale=2.0 ** -LOG_SHIFT).then_inc(log_ready, 1)

                copy_rows(0)
                for n in range(len(ROUTE_BLOCKS)):
                    act.preload_act_table_set("gelu_and_others")
                    if n + 1 < len(ROUTE_BLOCKS):
                        with act.Fori(0, 2) as i:
                            light_chunk(i + 2 * n, True)
                    else:
                        light_chunk(CHUNKS - 2, True)
                        light_chunk(CHUNKS - 1, False)
                    act.preload_act_table_set("natural_log_exp_and_others")
                    relevel(sums_before[n + 1])
                    if n + 1 < len(ROUTE_BLOCKS):
                        save_rows(n + 1)
                        act.wait_ge(args_ready, n + 2)
                        act.activation(exps[:, :], args[:, :], ACT.Exp).then_inc(exps_ready, 1)
                act.wait_ge(score_arg, 1)
                act.activation(score_of[:, :], args[:, 0:TILES], ACT.Exp).then_inc(score_ready, 1)
                def heavy(b):
                    for m in range(HEAVY // P):
                        act.wait_ge(heavy_h, b * 8 + (m + 1))
                        if m == 0:
                            act.wait_ge(heavy_o, b + FIRST)
                        act.activation(heavy_gT[:, m, :], heavy_banks[m % 4][:, 0:ROUTED], ACT.Gelu,
                                       bias=ffn0_cols[:, 5 + m:6 + m]).then_inc(heavy_g, 1)

                with act.Fori(0, BATCH - 1) as b:
                    heavy(b)
                normalize(S[1], 0, 0)
                heavy(BATCH - 1)

            step = Chain(act, act_step)
            for l in range(2):
                s = S[l]
                if l == 1:
                    ffn0()
                act.sem_inc(s["pv"], 4)
                act.preload_act_table_set("natural_log_exp_and_others")
                if l == 0:
                    normalize(s, 0, 0)
                    keys(s, l)
                if l == 1:
                    act.wait_ge(heavy_done, BATCH + FIRST)
                evac_hT(s, 0)
                for m in range(KH):
                    evac_q(s, l, 0, 0, m)
                normalize(s, 4, 1)
                evac_hT(s, 1)
                for m in range(KH):
                    evac_q(s, l, 1, 1, m)
                evac_maxT(s, 0)
                with act.Fori(0, BATCH - 1) as b:
                    step.enter(b, 4)
                    for e in range(2):
                        chunk_step(s, l, step, b * 2 + e, e, True, True)
                    step.leave(BATCH - 1)
                for e in range(2):
                    chunk_step(s, l, step, CHUNKS - 2 + e, e, False, e == 0)
            def evac_rowsT(c, e):
                act.wait_ge(G["hT_ps"], c + 1)
                if not isinstance(c, int) or c >= 2:
                    act.wait_ge(G["sums_ps"], c - 1)
                for k in range(KH):
                    act.activation(rowsT2[e][:, k, :], rowsT_banks[e][k][:, :], ACT.Copy).then_inc(G["hT_sb"], 1)

            def save_sums(c, e):
                act.wait_ge(G["sums_ps"], c + 1)
                act.activation(groups[:, ds(c * CHUNK, CHUNK)], mid[e][:, :], ACT.Identity,
                               bias=bn_cols[:, 0:1]).then_inc(G["sums_sb"], 1)

            def activate(c):
                return act.activation(groups[:, ds(c * CHUNK, CHUNK)], groups[:, ds(c * CHUNK, CHUNK)], ACT.Gelu,
                                      bias=bn_tmp[:, 4:5], scale=bn_tmp[:, 2:3])

            def prepare_rows(t, e):
                act.wait_ge(G["hsT_ps"], t)
                act.activation(hs[e], normed[:, ds(t, 1), 0:DIM].rearrange("p a d -> p (a d)"), ACT.Copy).then_inc(G["hs_ready"], 1)

            def prepare_acts(t, e):
                act.wait_ge(G["logit_ps"], t)
                act.activation(acts[e], groups[:, ds(t * P, P)], ACT.Copy).then_inc(G["acts_ready"], 1)

            def evac_hs(t, e):
                act.wait_ge(G["hsT_ps"], t + 1)
                act.wait_ge(G["full_ps"], t)
                act.activation(hsT[e], F0[:, 0:2 * P].rearrange("p (k n) -> p k n", k=KH), ACT.Copy).then_inc(G["hsT_sb"], 1)

            def save_logits(t, e):
                act.wait_ge(G["logit_ps"], t + 1)
                if not (isinstance(t, int) and t == 0):
                    act.wait_ge(G["taken_ready"], t - 1)
                act.activation(work[e], mid[e][:, :], ACT.Copy).then_inc(G["work_ready"], 1)

            def exponentials(t, e):
                act.wait_ge(G["minus_ready"], t + 1)
                for br in range(2):
                    act.activation(expw[e][:, br * DIM:(br + 1) * DIM], mid[e][:, br * DIM:(br + 1) * DIM], ACT.Exp,
                                   bias=minus_top[e][:, br:br + 1], accum_out=exp_sum[:, br:br + 1]).then_inc(G["exp_ready"], 1)

            def evac_sparse(t):
                act.wait_ge(G["sparseT_ps"], t + 1)
                act.wait_ge(G["in_ps"], t)
                act.activation(sparseT, F1[:, 0:2 * P].rearrange("p (k n) -> p k n", k=KH), ACT.Copy).then_inc(G["sparseT_sb"], 1)

            def rest(t, e):
                act.wait_ge(G["top_ready"], t + 1)
                act.wait_ge(G["part_added"], t)
                for br in range(2):
                    act.activation(taken[:, br * DIM:(br + 1) * DIM], work[e][:, br * DIM:(br + 1) * DIM], ACT.Exp,
                                   bias=minus_top[e][:, br:br + 1]).then_inc(G["part_ready"], 1)

            def scale_out(t, e):
                act.wait_ge(G["full_ps"], t + 1)
                act.activation(out_part, score[e][:, 0:DIM], ACT.Copy, scale=inv_sum[e][:, 0:1]).then_inc(G["part_ready"], 1)

            def scale_in(t, e):
                act.wait_ge(G["in_ps"], t + 1)
                act.wait_ge(G["top_ready"], t + 1)
                act.wait_ge(G["part_added"], t + 1)
                act.activation(in_part[e], out_banks[e][:, 0:DIM], ACT.Copy, scale=inv_sum[e][:, 1:2]).then_inc(G["in_scaled"], 1)

            def gate_tile(t, e, ahead=True):
                if ahead:
                    prepare_rows(t + 1, 1 - e)
                    prepare_acts(t + 1, 1 - e)
                    evac_hs(t + 1, 1 - e)
                if not (isinstance(t, int) and t == 0):
                    rest(t - 1, 1 - e)
                    scale_out(t - 1, 1 - e)
                exponentials(t, e)
                if not isinstance(t, int) or t >= 2:
                    scale_in(t - 2, e)
                if ahead:
                    save_logits(t + 1, 1 - e)
                if not (isinstance(t, int) and t == 0):
                    evac_sparse(t - 1)

            act.wait_ge(gate_in, 16)
            act.wait_ge(G["h_ready"], CHUNKS)
            evac_rowsT(0, 0)
            evac_rowsT(1, 1)
            save_sums(0, 0)
            with act.Fori(1, CHUNKS // 2) as i:
                for e in range(2):
                    evac_rowsT(i * 2 + e, e)
                    save_sums(i * 2 + e - 1, 1 - e)
            save_sums(CHUNKS - 1, 1)
            act.preload_act_table_set("gelu_and_others")
            prepare_rows(0, 0)
            evac_hs(0, 0)
            act.wait_ge(G["bn_ready"], 1)
            step.did(activate(0))
            step.settle()
            prepare_acts(0, 0)
            with act.Fori(1, CHUNKS) as c:
                step.enter(c - 1, 1)
                step.did(activate(c))
                step.leave(CHUNKS - 1)
            step.settle()
            save_logits(0, 0)
            act.preload_act_table_set("natural_log_exp_and_others")
            for e in range(2):
                gate_tile(e, e)
            with act.Fori(1, TILES // 2 - 1) as i:
                for e in range(2):
                    gate_tile(i * 2 + e, e)
            for e in range(2):
                gate_tile(TILES - 2 + e, e, e == 0)
            rest(TILES - 1, 1)
            scale_out(TILES - 1, 1)
            evac_sparse(TILES - 1)
            for e in range(2):
                scale_in(TILES - 2 + e, e)

        @block.vector
        def _(dve):
            step = Chain(dve, dve_step)

            def split_biases():
                step.did(dve.memset(bias3[:, :, :], 0.0))
                step.did(dve.tensor_scalar(bias_rows[0:3, :], bias_rows[0:3, :], bias_gates[:, 0:1], None, ALU.mult))
                step.settle()
                for k in range(3):
                    step.did(dve.tensor_copy(bias_piece[k][:, :], bias_rows[:, :]))
                    step.settle()
                    if k < 2:
                        step.did(dve.tensor_tensor(bias_rows[:, :], bias_rows[:, :], bias_piece[k][:, :], ALU.subtract))
                        step.settle()
                dve.sem_inc(pieces_ready, 1)

            def row_stats_of(s, tile0, n, step):
                if not (isinstance(n, int) and n == 0):
                    dve.wait_ge(s["rstd_ready"], n)
                    plain(dve)
                for t in range(CHUNK_TILES):
                    step.did(dve.bn_stats(row_stats[:, t, :], x[:, ds(tile0 + t, 1), :].rearrange("p a d -> p (a d)")))
                step.settle()
                plain(dve)
                for t in range(CHUNK_TILES):
                    ins = dve.bn_aggr(mean_var[:, t, :], row_stats[:, t, :])
                ins.then_inc(s["stats"], 1)

            def row_max(s, n, j):
                t, m = j // 2, j % 2
                dve.wait_ge(s["max_ps"], n * 8 + (j + 1))
                if j == 0 and not (isinstance(n, int) and n == 0):
                    dve.wait_ge(s["maxT_ps"], n)
                dve.tensor_reduce(max16[:, t, 8 * m:8 * m + 8], mid[j % 2][:, :].rearrange("p (h k) -> p h k", h=8),
                                  AX_X, ALU.max).then_inc(s["max_done"], 1)

            def divide(s, c, m):
                dve.wait_ge(s["inv_ready"], c * 2 + (m + 1))
                if not (isinstance(c, int) and c == 0):
                    dve.wait_ge(s["o_ps"], c * 2)
                else:
                    dve.wait_ge(bias_ready, 48)
                dve.tensor_tensor(yT[:, m, :], YB[:, :], inv_den[:, m, :], ALU.mult).then_inc(s["y_ready"], 1)

            def add_to_x(s, c, g):
                dve.wait_ge(s["o_ps"], c * 2 + (g + 1))
                rows = x[:, ds(c * 4 + 2 * g, 2), :].rearrange("p a d -> p (a d)")
                dve.tensor_tensor(rows, rows, mid[g][:, :], ALU.add).then_inc(s["x_new"], 1)

            def low_part(out, total, high, bias):
                if bias is None:
                    return dve.tensor_tensor(out, total, high, ALU.subtract)
                return dve.scalar_tensor_tensor(out=out, in0=total, scalar=bias, in1=high, op0=ALU.add, op1=ALU.subtract)

            def keys_low(s, l):
                for m in range(KH):
                    dve.wait_ge(s["k_sb"], m + 1)
                    low_part(kT_low[:, m, :, :], front[m][:, 0:BATCH * KEYS].rearrange("p (b n) -> p b n", b=BATCH), kT[:, m, :, :],
                             qkv_bias[:, 2 + m:3 + m] if l else None).then_inc(s["k_low"], 1)

            def queries_low(s, l, a, e, m):
                dve.wait_ge(s["q_sb"], a * 2 + (m + 1))
                if not isinstance(a, int) or a >= 2:
                    dve.wait_ge(s["s_ps"], a * 8 - 8)
                low_part(q_low[e][:, m, :], front[m][:, :], qT[e][:, m, :].bitcast(F32), qkv_bias[:, m:m + 1] if l else None)\
                    .then_inc(s["q_low"], 1)

            def key_diagonal(s, b, first, out, part):
                if not first:
                    dve.wait_ge(s["s_ps"], b * 16)
                for m in range(KH):
                    dve.tensor_tensor(out[:, m, :, :], part[:, m, ds(b, 1), :].to_broadcast([P, 8, KEYS]),
                                      head_mask[:, :, :], ALU.mult).then_inc(s["kv_diag"], 1)

            def value_diagonal(s, b, first):
                if not first:
                    dve.wait_ge(s["pv"], b * 16 + 4)
                dve.tensor_tensor(v_diag[:, :, :], v_all[:, ds(b, 1), :].rearrange("p a (h d) -> p (a h) d", h=HEADS),
                                  pair_mask[:, :, :], ALU.mult).then_inc(s["kv_diag"], 1)

            def chunk_step(s, l, c, e, b, ahead, nxt, before):
                for p in range(PAIRS):
                    if nxt:
                        row_max(s, c + 1, p)
                    if p == 0 and ahead and e == 0 and s is S[1]:
                        dve.wait_ge(mixed, b + 2)
                    if p == 0 and ahead:
                        row_stats_of(s, c * 4 + 8, c + 2, step)
                    if p == 2 and before:
                        route_stats_of(c - 1) if s is S[0] else gate_stats_of(c - 1)
                    if p == 5:
                        divide(s, c, 0)
                    if p == 6 and before:
                        route_logits_of(c - 1) if s is S[0] else gate_rows_of(c - 1)
                if e == 1 and nxt:
                    key_diagonal(s, b + 1, False, k_diag, kT)
                divide(s, c, 1)
                if ahead:
                    queries_low(s, l, c + 2, e, 0)
                if e == 1 and nxt:
                    key_diagonal(s, b + 1, False, k_diag_low, kT_low)
                    value_diagonal(s, b + 1, False)
                if ahead:
                    queries_low(s, l, c + 2, e, 1)
                for g in range(2):
                    add_to_x(s, c, g)

            def route_stats_of(c):
                dve.wait_ge(s0["x_new"], c * 2 + 2 + FIRST)
                dve.wait_ge(scale_ready, c * 2)
                plain(dve)
                for t in range(CHUNK_TILES):
                    step.did(dve.bn_stats(route_stats[:, t, :], x[:, ds(c * 4 + t, 1), :].rearrange("p a d -> p (a d)")))
                step.settle()
                plain(dve)
                for t in range(CHUNK_TILES):
                    ins = dve.bn_aggr(route_mv[:, t, :], route_stats[:, t, :])
                ins.then_inc(route_stats_ready, 1)

            def route_logits_of(c):
                dve.wait_ge(scale_ready, c * 2 + 2)
                for t in range(CHUNK_TILES):
                    step.did(dve.tensor_scalar(normed[:, ds(c * 4 + t, 1), 0:DIM].rearrange("p a d -> p (a d)"),
                                               x[:, ds(c * 4 + t, 1), :].rearrange("p a d -> p (a d)"),
                                               route_mv[:, t, 0:1], row_scale[:, t:t + 1], ALU.subtract, ALU.mult))
                for t in range(CHUNK_TILES):
                    step.did(dve.scalar_tensor_tensor(
                        out=dot_out[:, :], in0=x[:, ds(c * 4 + t, 1), :].rearrange("p a d -> p (a d)"),
                        scalar=route_mv[:, t, 0:1], in1=token_row[:, :], op0=ALU.subtract, op1=ALU.mult,
                        accum_out=raw_dot[:, t:t + 1]))
                    step.settle()
                step.did(dve.tensor_tensor(raw_dot[:, :], raw_dot[:, :], row_scale[:, :], ALU.mult))
                step.settle()
                dve.tensor_tensor(logit[:, ds(c * 4, 4)], raw_dot[:, :], row_norm[:, ds(c * 4, 4)], ALU.mult).then_inc(logit_ready, 1)

            by_batch = lambda ap: ap.rearrange("p (b c) -> p b c", b=BATCH)
            spread = lambda ap: ap.unsqueeze(2).to_broadcast([P, BATCH, TILES // BATCH])

            def cross_max(n):
                dve.wait_ge(cross_ps, n + 1)
                step.did(dve.tensor_reduce(col4[:, :], YB[0:BATCH, 0:P], AX_X, ALU.max))
                step.settle()
                dve.tensor_scalar(diag4[:, :], ident[0:BATCH, 0:BATCH], col4[:, 0:1], ROUTE_K, ALU.mult, ALU.mult).then_inc(cross_diag, 1)
                dve.wait_ge(cross_out, n + 1)

            def exp_args():
                step.did(dve.tensor_tensor(level[:, :], minus_a[:, :], top_logit[:, :], ALU.min))
                step.settle()
                step.did(dve.tensor_tensor(by_batch(args[:, 0:TILES]), by_batch(logit[:, :]), spread(level[:, :]), ALU.subtract))
                step.did(dve.tensor_tensor(args[:, TILES:], minus_a[:, :], level[:, :], ALU.subtract))
                step.settle()
                dve.tensor_scalar(args[:, :], args[:, :], 1.0 / ROUTE_EPS, 80.0, ALU.mult, ALU.min).then_inc(args_ready, 1)

            def route_iteration(sums):
                dve.wait_ge(sum_ready, sums)
                step.did(dve.tensor_tensor(by_batch(capped[:, :]), by_batch(exps[:, 0:TILES]), spread(DB[:, 0:BATCH]), ALU.min))
                step.settle()
                dve.tensor_reduce(part_sum[:, :], by_batch(capped[:, :]), AX_X, ALU.add).then_inc(part_ready, 1)

            def compare(n, b, e):
                if not (isinstance(n, int) and n == 0):
                    dve.wait_ge(counted, n * 4 + (e - 3))
                dve.tensor_scalar(larger16[e], logit_rows[:, b, :], logit[:, ds(n * 4 + e, 1)], None,
                                  ALU.is_lt).then_inc(compared[1], 1)

            def light_to_x(n, g):
                dve.wait_ge(light_o, n * 2 + (g + 1) + FIRST)
                rows = x[:, ds(n * 4 + 2 * g, 2), :].rearrange("p a d -> p (a d)")
                dve.tensor_tensor(rows, rows, score[g][:, :], ALU.add).then_inc(light_added, 1)

            def route():
                dve.wait_ge(logit_ready, CHUNKS)
                dve.wait_ge(s0["x_new"], 2 * CHUNKS + FIRST)
                dve.tensor_reduce(part_sum[:, :], by_batch(logit[:, :]), AX_X, ALU.max).then_inc(cross_in, 1)
                step.did(dve.memset(minus_a[:, :], 0.0))
                cross_max(0)
                step.did(dve.tensor_copy(top_logit[:, :], YB[:, P:P + BATCH]))
                step.settle()
                exp_args()
                for n, iters in enumerate(ROUTE_BLOCKS):
                    dve.wait_ge(exps_ready, n + 1)
                    dve.tensor_scalar(part_sum[:, :], exps[:, TILES:], ROUTE_K / P, None, ALU.mult).then_inc(part_ready, 1)

                    dve.wait_ge(rows_sb, 2 * n + 2)

                    def route_round(i, first=False):
                        for j in range(CHUNK_ITERS):
                            route_iteration(i * CHUNK_ITERS + (sums_before[n] + 1 + j))
                            if j in (2, 4) and not first:
                                light_to_x(i + (2 * n - 1), j // 2 - 1)
                            if j in (0, 3):
                                compare(i + 2 * n, n, 1 if j == 0 else 3)

                    if n == 0:
                        route_round(0, first=True)
                        route_round(1)
                    else:
                        with dve.Fori(0, 2) as i:
                            step.enter(i, CHUNK_ITERS)
                            route_round(i)
                            step.leave(2)
                    for j in range(2 * CHUNK_ITERS, iters):
                        route_iteration(sums_before[n] + 1 + j)
                    dve.wait_ge(log_ready, n + 1)
                    step.did(dve.tensor_scalar(log_sum[:, :], log_sum[:, :], LOG_SHIFT * math.log(2.0), None, ALU.add))
                    step.settle()
                    step.did(dve.scalar_tensor_tensor(out=minus_a[:, :], in0=log_sum[:, :], scalar=ROUTE_EPS, in1=level[:, :],
                                                      op0=ALU.mult, op1=ALU.add))
                    step.settle()
                    if n + 1 < len(ROUTE_BLOCKS):
                        exp_args()
                    else:
                        for g in range(2):
                            light_to_x(CHUNKS - 1, g)
                step.did(dve.tensor_tensor(by_batch(args[:, 0:TILES]), by_batch(logit[:, :]), spread(minus_a[:, :]), ALU.subtract))
                step.settle()
                step.did(dve.tensor_scalar(args[:, 0:TILES], args[:, 0:TILES], 0.0, 1.0 / ROUTE_EPS, ALU.min, ALU.mult))
                step.settle()
                dve.sem_inc(score_arg, 1)
                key, larger, equal, take = (pick[:, i, :] for i in range(4))
                step.did(dve.tensor_scalar(key, args[:, 0:TILES], LOG_TINY, None, ALU.max))
                dve.wait_ge(counted, TILES)
                step.did(dve.tensor_scalar(take, counts_ps, ROUTED - 0.5, 1.0, ALU.is_gt, ALU.mult))
                step.settle()
                step.did(dve.scalar_tensor_tensor(out=larger, in0=take, scalar=1e4, in1=key, op0=ALU.mult, op1=ALU.add))
                step.settle()
                dve.tensor_reduce(part_sum[:, :], by_batch(larger), AX_X, ALU.min, negate=True).then_inc(cross_in, 1)
                cross_max(1)
                step.did(dve.tensor_scalar(level[:, :], YB[:, P:P + BATCH], -1.0, None, ALU.mult))
                step.settle()
                step.did(dve.tensor_tensor(by_batch(larger), by_batch(key), spread(level[:, :]), ALU.is_gt))
                step.did(dve.tensor_tensor(by_batch(equal), by_batch(key), spread(level[:, :]), ALU.is_equal))
                step.settle()
                step.did(dve.tensor_copy(flag16[:, :], equal))
                step.did(dve.tensor_reduce(part_sum[:, :], by_batch(larger), AX_X, ALU.add))
                step.settle()
                dve.tensor_copy(count16[:, :], part_sum[:, :]).then_inc(flags_ready, 1)
                dve.wait_ge(prefix_ready, 1)
                step.did(dve.tensor_scalar(minus_a[:, :], M1[:, 0:BATCH], -1.0, float(ROUTED), ALU.mult, ALU.add))
                step.settle()
                step.did(dve.tensor_tensor(by_batch(take), by_batch(M0[:, 0:TILES]), spread(minus_a[:, :]), ALU.is_lt))
                step.settle()
                step.did(dve.tensor_tensor(take, take, equal, ALU.mult))
                step.settle()
                step.did(dve.tensor_tensor(take, take, larger, ALU.add))
                step.settle()
                dve.tensor_copy(flag16[:, :], take).then_inc(flags_ready, 1)
                dve.wait_ge(prefix_ready, 2)
                step.did(dve.scalar_tensor_tensor(out=take, in0=M0[:, 0:TILES], scalar=float(ROUTED), in1=take,
                                                  op0=ALU.is_lt, op1=ALU.mult))
                step.did(dve.tensor_tensor(key, M0[:, 0:TILES], slot_base[:, 0, :], ALU.add))
                step.settle()
                step.did(dve.tensor_tensor(key, key, take, ALU.mult))
                step.settle()
                step.did(dve.tensor_tensor(key, key, slot_base[:, 1, :], ALU.add))
                step.settle()
                dve.wait_ge(score_ready, 1)
                step.did(dve.tensor_copy(normed[:, :, DIM], score_of[:, :]))
                step.did(dve.tensor_copy(slot[:, :], key))
                step.settle()
                dve.sem_inc(slot_ready, 1)

            def add_heavy(b):
                dve.wait_ge(light_added, 2 * CHUNKS)
                dve.wait_ge(gathered[b], 16 * 8)
                dve.tensor_tensor(x[:, 8 * b:8 * b + 8, :], x[:, 8 * b:8 * b + 8, :], heavy_rows[b % 2][:, :, :],
                                  ALU.add).then_inc(mixed, 1)

            def heavy(b, e):
                dve.wait_ge(heavy_T, b + 1)
                dve.wait_ge(heavy_h, b * 8)
                dve.tensor_copy(pickedT[:, :, :], F0[:, :].rearrange("p (k n) -> p k n", k=KH)).then_inc(heavy_Tsb, 1)
                dve.wait_ge(picked_in, b * 16 + 16)
                dve.wait_ge(heavy_done, b + FIRST)
                step.did(dve.tensor_scalar(pick_gate[:, :], picked[e][:, :, DIM], -1.0, 1.0, ALU.mult, ALU.add))
                step.settle()
                step.did(dve.tensor_tensor(pick_gate[:, :], pick_gate[:, :], picked[e][:, :, DIM], ALU.add))
                step.settle()
                step.did(dve.tensor_scalar(pick_gate[:, :], pick_gate[:, :], gates[:, 1:2], None, ALU.mult))
                step.settle()
                if b == 2:
                    dve.wait_ge(mixed, 1)
                    row_stats_of(S[1], 0, 0, step)
                if b:
                    add_heavy(b - 1)
                dve.wait_ge(heavy_o, b + 1 + FIRST)
                dve.wait_ge(heavy_room, b + 1)
                for j in range(2):
                    ins = dve.tensor_scalar(heavy_y[e][:, j, :], YB[:, j * DIM:(j + 1) * DIM], pick_gate[:, j:j + 1], None,
                                            ALU.mult)
                ins.then_inc(heavy_done, 1)

            def gate_ffn0():
                dve.wait_ge(ffn0_in, 32)
                for k in range(KH):
                    dve.tensor_scalar(w1l[:, k, :], w1l[:, k, :], ffn0_cols[:, k:k + 1], None, ALU.mult).then_inc(ffn0_ready, 1)
                    dve.tensor_scalar(w1h[:, k, :], w1h[:, k, :], ffn0_cols[:, 2 + k:3 + k], None, ALU.mult).then_inc(ffn0_ready, 1)
                dve.tensor_scalar(w2l[:, :], w2l[:, :], gates[:, 1:2], None, ALU.mult).then_inc(ffn0_ready, 1)

            def gate_stats_of(c):
                dve.wait_ge(S[1]["x_new"], c * 2 + 2 + FIRST)
                dve.wait_ge(G["rstd_ready"], c)
                plain(dve)
                for t in range(CHUNK_TILES):
                    step.did(dve.bn_stats(route_stats[:, t, :], x[:, ds(c * 4 + t, 1), :].rearrange("p a d -> p (a d)")))
                step.settle()
                plain(dve)
                for t in range(CHUNK_TILES):
                    ins = dve.bn_aggr(route_mv[:, t, :], route_stats[:, t, :])
                ins.then_inc(G["stats"], 1)

            def gate_rows_of(c):
                dve.wait_ge(G["rstd_ready"], c + 1)
                for t in range(CHUNK_TILES):
                    step.did(dve.tensor_scalar(normed[:, ds(c * 4 + t, 1), 0:DIM].rearrange("p a d -> p (a d)"),
                                               x[:, ds(c * 4 + t, 1), :].rearrange("p a d -> p (a d)"),
                                               route_mv[:, t, 0:1], row_scale[:, t:t + 1], ALU.subtract, ALU.mult))
                step.settle()
                dve.sem_inc(G["h_ready"], 1)

            def gate_copy(c, e):
                if not isinstance(c, int) or c >= 2:
                    dve.wait_ge(G["hT_ps"], c - 1)
                dve.tensor_copy(rows2[e], normed[:, ds(c * 4, 4), 0:DIM]).then_inc(G["copied"], 1)

            def group_stats(c):
                dve.wait_ge(G["sums_sb"], c + 1 + FIRST)
                plain(dve)
                step.did(dve.bn_stats(bn_parts[:, ds(c * 6, 6)], groups[:, ds(c * CHUNK, CHUNK)]))

            def gate_tile(t, e):
                dve.wait_ge(G["work_ready"], t + 1)
                for r in range(4):
                    for br in range(2):
                        cols = work[e][:, br * DIM:(br + 1) * DIM]
                        if r:
                            dve.wait_ge(top_step, t * 16 + (4 * r + br - 1))
                        dve.max(top8[:, r, br, :], cols).then_inc(top_step, 1)
                    for br in range(2):
                        cols = work[e][:, br * DIM:(br + 1) * DIM]
                        dve.wait_ge(top_step, t * 16 + (4 * r + br + 1))
                        dve.match_replace(cols, top8[:, r, br, :], cols, FOUND).then_inc(top_step, 1)
                        if r == 0 and br == 0:
                            dve.wait_ge(top_step, t * 16 + 2)
                            if t >= 2:
                                dve.wait_ge(G["part_ready"], t * 3 - 3)
                            dve.tensor_scalar(minus_top[e][:, :], top8[:, 0, :, 0], -1.0, None, ALU.mult).then_inc(G["minus_ready"], 1)
                dve.wait_ge(G["exp_ready"], t * 2 + 2)
                if t >= 2:
                    dve.wait_ge(G["in_scaled"], t - 1 + FIRST)
                step.did(dve.reciprocal(inv_sum[e][:, :], exp_sum[:, :]))
                dve.wait_ge(top_step, t * 16 + 16)
                step.settle()
                dve.sem_inc(G["top_ready"], 1)

            def gate_layer():
                gate_copy(0, 0)
                gate_copy(1, 1)
                with dve.Fori(1, CHUNKS // 2) as i:
                    step.enter(i - 1, 2)
                    for e in range(2):
                        gate_copy(i * 2 + e, e)
                        group_stats(i * 2 + e - 2)
                    step.leave(CHUNKS // 2 - 1)
                group_stats(CHUNKS - 2)
                group_stats(CHUNKS - 1)
                step.settle()
                dve.bn_aggr(bn_mv[:, :], bn_parts[:, :]).then_inc(G["bn_done"], 1)
                for t in range(TILES):
                    gate_tile(t, t % 2)

            def values(s, l):
                keys_low(s, l)
                for b in range(BATCH):
                    dve.wait_ge(s["v_ps"], b + 1)
                    if l == 0:
                        dve.tensor_copy(v_all[:, b, :], mid[b % 2][:, 0:DIM]).then_inc(s["v_sb"], 1)
                    else:
                        dve.tensor_tensor(v_all[:, b, :], mid[b % 2][:, 0:DIM], v_bias[:, :], ALU.add).then_inc(s["v_sb"], 1)

            s0 = S[0]
            dve.wait_ge(x_in[0], 16)
            for l in range(2):
                s = S[l]
                if l == 1:
                    route()
                    for b in range(BATCH - 1):
                        heavy(b, b % 2)
                    dve.wait_ge(gate_in, 16)
                    dve.tensor_scalar(gate_w[:, :, :], gate_w[:, :, :], gates[:, 3:4], None, ALU.mult).then_inc(gate_ready, 1)
                    dve.tensor_scalar(bias1[:, :], bias1[:, :], gates[:, 3:4], None, ALU.mult).then_inc(gate_ready, 1)
                    heavy(BATCH - 1, 1)
                if l == 0:
                    row_stats_of(s, 0, 0, step)
                    dve.wait_ge(consts_in, 16)
                if l == 0:
                    values(s, l)
                if l == 0:
                    dve.wait_ge(x_in[1], 16)
                row_stats_of(s, 4, 1, step)
                for m in range(KH):
                    queries_low(s, l, 0, 0, m)
                for j in range(8):
                    row_max(s, 0, j)
                dve.wait_ge(s["v_sb"], BATCH)
                dve.wait_ge(s["k_low"], KH)
                key_diagonal(s, 0, True, k_diag, kT)
                key_diagonal(s, 0, True, k_diag_low, kT_low)
                for m in range(KH):
                    queries_low(s, l, 1, 1, m)
                value_diagonal(s, 0, True)
                if l == 0:
                    dve.wait_ge(bias_in, 16)
                    dve.wait_ge(gates_ready, 2)
                    split_biases()
                dve.wait_ge(attn_w_in[l], 16)
                dve.tensor_scalar(Wo[l][:, :, :], Wo[l][:, :, :], gates[:, 2 * l:2 * l + 1], None, ALU.mult).then_inc(wo_ready, 1)
                if l == 0:
                    dve.wait_ge(x_in[2], 16)
                    dve.wait_ge(route_in, 48)
                def chunk_pair(b, ahead, first):
                    for e in range(2):
                        chunk_step(s, l, b * 2 + e, e, b, ahead, ahead or e == 0, before=not (first and e == 0))

                chunk_pair(0, True, True)
                if l == 0:
                    gate_ffn0()
                with dve.Fori(1, BATCH - 1) as b:
                    step.enter(b - 1, 8 + (26 if l == 0 else 16))
                    chunk_pair(b, True, False)
                    step.leave(BATCH - 2)
                chunk_pair(BATCH - 1, False, False)
                if l == 0:
                    route_stats_of(CHUNKS - 1)
                    values(S[1], 1)
                    route_logits_of(CHUNKS - 1)
                else:
                    gate_stats_of(CHUNKS - 1)
                    gate_rows_of(CHUNKS - 1)
            gate_layer()

        @block.tensor
        def _(pe):
            def keys_values(s, l):
                for m in range(KH):
                    for k in range(KH):
                        mm = pe.matmul(front[m][:, 0:BATCH * KEYS], Wk[l][:, k, m * P:(m + 1) * P],
                                       ctxT[:, k, :, 0, :], start=(k == 0), stop=(k == KH - 1))
                    mm.then_inc(s["k_ps"], 1)
                for b in range(BATCH):
                    if b >= 2:
                        pe.wait_ge(s["v_sb"], b - 1)
                    elif l == 1:
                        pe.wait_ge(S[0]["x_new"], 2 * CHUNKS + FIRST)
                    for k in range(KH):
                        mm = pe.matmul(mid[b % 2][:, 0:DIM], ctxT[:, k, b, :, :].rearrange("p r n -> p (r n)"), Wv[l][:, k, :],
                                       start=(k == 0), stop=(k == KH - 1))
                    mm.then_inc(s["v_ps"], 1)

            def transpose_h(s, a):
                pe.wait_ge(s["h_ready"], a + 1)
                if not (isinstance(a, int) and a == 0):
                    pe.wait_ge(s["q_sb"], a * 2)
                    pe.wait_ge(s["q_low"], a * 2)
                for k in range(KH):
                    for t in range(CHUNK_TILES):
                        mm = pe.transpose(front[k][:, t * P:(t + 1) * P], h[:, t, k * P:(k + 1) * P], ident[:, :])
                mm.then_inc(s["hT_ps"], 1)

            def project_q(s, l, a, m):
                pe.wait_ge(s["hT_sb"], a * 2 + 2)
                for k in range(KH):
                    mm = pe.matmul(front[m][:, :], Wq[l][:, k, m * P:(m + 1) * P], hT[:, k, :],
                                   start=(k == 0), stop=(k == KH - 1))
                mm.then_inc(s["q_ps"], 1)

            def max_scores(s, l, n, first, b, j):
                t, m = j // 2, j % 2
                pe.wait_ge(s["q16_ready"], n * 2 + (m + 1))
                if j >= 2:
                    pe.wait_ge(s["max_done"], n * 8 + (j - 1))
                masked = l == 0 and first and t == 0
                mm = pe.matmul(mid[j % 2][:, :], q16[:, m, t * P:(t + 1) * P],
                               k16[:, ds(b, 1), m, :, :].rearrange("p a h k -> p (a h k)"), start=True, stop=not masked)
                if masked:
                    mm = pe.matmul(mid[j % 2][:, :], ident16[:, :], causal_rows16[:, :], start=False, stop=True)
                mm.then_inc(s["max_ps"], 1)

            def transpose_max(s, n):
                pe.wait_ge(s["max_done"], n * 8 + 8)
                if not (isinstance(n, int) and n == 0):
                    pe.wait_ge(s["s_exp"], n * 8 + FIRST)
                for t in range(CHUNK_TILES):
                    mm = pe.transpose(maxT_ps[:, t * P:(t + 1) * P], max16[:, t, :], ident16[:, :])
                mm.then_inc(s["maxT_ps"], 1)

            def scores(s, l, c, e, p):
                m = p // 4
                if p == 0:
                    pe.wait_ge(s["maxT_sb"], c + 1)
                if p % 4 == 0:
                    pe.wait_ge(s["q_low"], c * 2 + (m + 1))
                if not (isinstance(c, int) and c == 0 and p < 2):
                    pe.wait_ge(s["s_exp"], (c * 8 + (p - 1) if p else c * 8) + FIRST)
                out = score[p % 2][:, :]
                for keys, queries in ((k_diag, qT[e]), (k_diag_low, qT[e]), (k_diag, q_low[e])):
                    pe.matmul(out, keys[:, m, 2 * (p % 4):2 * (p % 4) + 2, :].rearrange("p h k -> p (h k)"),
                              queries[:, m, :], start=(keys is k_diag and queries is qT[e]), stop=False)
                masked = l == 0 and e == 0
                if masked:
                    pe.matmul(score[p % 2][:, 0:KEYS], ident16[:, :], causal_keys16[:, :], start=False, stop=False)
                pe.matmul(out, neg_sel16[:, p, :], maxT16[:, :], start=False, stop=True).then_inc(s["s_ps"], 1)

            def weigh_values(s, c, p):
                m, r = p // 4, 32 * (p % 4)
                pe.wait_ge(s["s_exp"], c * 8 + (p + 1) + FIRST)
                if p % 4 == 0:
                    pe.wait_ge(s["y_ready"], c * 2 + m + FIRST)
                pe.matmul(YB[r:r + 32, :], v_diag[:, 2 * p:2 * p + 2, :].rearrange("p h d -> p (h d)"), probs[:, p % 4, :],
                          start=True, stop=True)
                pe.matmul(DB[r:r + 32, :], pair_mask[:, 0:2, :].rearrange("p h d -> p (h d)"), probs[:, p % 4, :],
                          start=True, stop=True).then_inc(s["pv"], 1)

            def project_out(s, l, c):
                pe.wait_ge(wo_ready, l + 1)
                pe.wait_ge(bias_ready, 48)
                pe.wait_ge(s["y_ready"], c * 2 + 2 + FIRST)
                for g in range(2):
                    for i in range(2):
                        t = 2 * g + i
                        out = mid[g][:, i * DIM:(i + 1) * DIM]
                        for m in range(KH):
                            pe.matmul(out, yT[:, m, t * P:(t + 1) * P], Wo[l][:, m, :], start=(i == 0 and m == 0), stop=False,
                                      skip_group_check=True)
                        mm = pe.matmul(out, ones16[:, :], bias3[:, l, :], start=False, stop=(i == 1),
                                       skip_group_check=True)
                    mm.then_inc(s["o_ps"], 1)

            def chunk_step(s, l, c, e, b, ahead, nxt):
                for p in range(PAIRS):
                    if p == 0 and e == 0:
                        pe.wait_ge(s["kv_diag"], b * 5 + 5)
                        pe.wait_ge(s["k16_ready"], BATCH * KH)
                    if p == 5:
                        weigh_values(s, c, 3)
                    scores(s, l, c, e, p)
                    if nxt:
                        if p < 2 and not (isinstance(c, int) and c == 0):
                            pe.wait_ge(s["x_new"], c * 2 + FIRST)
                        max_scores(s, l, c + 1, e == 1, b + 1 if e == 1 else b, p)
                    if p == 6 and ahead:
                        transpose_h(s, c + 2)
                    if p >= 2 and p != 5:
                        weigh_values(s, c, p - 2)
                for p in range(PAIRS - 2, PAIRS):
                    weigh_values(s, c, p)
                if ahead:
                    project_q(s, l, c + 2, 0)
                if nxt:
                    transpose_max(s, c + 1)
                if ahead:
                    project_q(s, l, c + 2, 1)
                if nxt:
                    pe.wait_ge(s["max_done"], c * 8 + 16)
                elif not (isinstance(c, int) and c == 0):
                    pe.wait_ge(s["x_new"], c * 2 + FIRST)
                project_out(s, l, c)

            def cross_max(n):
                pe.wait_ge(cross_in, n + 1)
                pe.transpose(YB[0:BATCH, 0:P], part_sum[:, :], ident[:, :]).then_inc(cross_ps, 1)
                pe.wait_ge(cross_diag, n + 1)
                pe.matmul(YB[:, P:P + BATCH], eighth[0:4, :], diag4[:, :], start=True, stop=True).then_inc(cross_out, 1)

            def sum_parts(n):
                pe.wait_ge(part_ready, n)
                pe.matmul(DB[:, 0:BATCH], eighth[:, :], part_sum[:, :], start=True, stop=True).then_inc(sum_ready, 1)

            def light_out(m, t):
                if t == 0:
                    pe.wait_ge(light_g, m + 1)
                    pe.wait_ge(light_added, m * 2)
                out = score[t // 2][:, (t % 2) * DIM:(t % 2 + 1) * DIM]
                pe.matmul(out, light_gT[:, t * P:(t + 1) * P], w2l[:, :], start=(t % 2 == 0), stop=False, skip_group_check=True)
                mm = pe.matmul(out, ones16[:, :], bias3[:, B2_LIGHT, :], start=False, stop=(t % 2 == 1), skip_group_check=True)
                if t % 2 == 1:
                    mm.then_inc(light_o, 1)

            def count_above(b, n, e):
                pe.wait_ge(compared[e % 2], n * 2 + (e // 2 + 1))
                for i in range(8):
                    mm = pe.matmul(counts_ps[:, 8 * b + i:8 * b + i + 1], larger16[e][:, i * P:(i + 1) * P], ones16[:, 0:1],
                                   start=False, stop=False, skip_group_check=True)
                mm.then_inc(counted, 1)

            def light_piece(n, j, b, first):
                if j == 0:
                    pe.wait_ge(copied, n + 1)
                    pe.wait_ge(light_Tsb, n * 2)
                    for k in range(KH):
                        for t in range(CHUNK_TILES):
                            mm = pe.transpose(front[k][:, t * P:(t + 1) * P], h[:, t, k * P:(k + 1) * P], ident[:, :])
                    mm.then_inc(light_T, 1)
                if j < CHUNK_TILES and not first:
                    light_out(n - 1, j)
                if j == 4:
                    pe.wait_ge(light_Tsb, n * 2 + 2)
                    pe.wait_ge(light_g, n)
                if j >= 4:
                    mm = pe.matmul(mid[0][:, :], w1l[:, j - 4, :], hT[:, j - 4, :], start=(j == 4), stop=(j == 5))
                    if j == 5:
                        mm.then_inc(light_h, 1)
                if j in COUNT_SLOTS:
                    count_above(b, n, COUNT_SLOTS.index(j))

            def prefix(n):
                pe.wait_ge(flags_ready, n + 1)
                out, flags = M0[:, 0:TILES].rearrange("p (b c) -> p b c", b=BATCH), flag16[:, :].rearrange("p (b c) -> p b c", b=BATCH)
                mm = pe.matmul(out, before16[:, :], flags, start=True, stop=False, skip_group_check=True)
                for d in range(1, 8):
                    mm = pe.matmul(out[:, :, d:8], ones16[:, :], flags[:, :, 0:8 - d], start=False, stop=(d == 7),
                                   skip_group_check=True)
                if n == 0:
                    mm = pe.matmul(M1[:, 0:BATCH], ones16[:, :], count16[:, :], start=True, stop=True)
                mm.then_inc(prefix_ready, 1)

            def ffn0():
                pe.wait_ge(attn_w_in[1], 16)
                keys_values(S[1], 1)
                cross_max(0)
                pe.wait_ge(logit_ready, CHUNKS)

                def spread_logits(b):
                    if b:
                        pe.wait_ge(light_added, 4 * b - 2)
                    for i in range(2):
                        for t in range(4):
                            mm = pe.matmul(score[i][:, t * P:(t + 1) * P],
                                           logit[:, 8 * b + 4 * i + t:8 * b + 4 * i + t + 1].to_broadcast([P, P]),
                                           ident[:, :], start=True, stop=True)
                        mm.then_inc(rows_ps, 1)

                spread_logits(0)
                pe.wait_ge(ffn0_ready, 5)
                pe.wait_ge(bias_ready, 48)
                pe.matmul(counts_ps, ones16[:, :], zeros16[:, :], start=True, stop=False, skip_group_check=True)

                def route_round(n, i, first=False):
                    for j in range(CHUNK_ITERS):
                        sum_parts(i * CHUNK_ITERS + (sums_before[n] + 2 + j))
                        light_piece(i + 2 * n, j, n, first)

                for n, iters in enumerate(ROUTE_BLOCKS):
                    sum_parts(sums_before[n] + 1)
                    pe.wait_ge(rows_sb, 2 * n + 2)
                    if n == 0:
                        route_round(0, 0, first=True)
                        route_round(0, 1)
                    else:
                        with pe.Fori(0, 2) as i:
                            route_round(n, i)
                    for j in range(2 * CHUNK_ITERS, iters):
                        sum_parts(sums_before[n] + 2 + j)
                        for t in range(2 * (j % 2), 2 * (j % 2) + 2):
                            light_out(CHUNKS - 1, t)
                    if n + 1 < BATCH:
                        spread_logits(n + 1)
                cross_max(1)
                prefix(0)
                prefix(1)
                with pe.Fori(0, BATCH // 2) as i:
                    for e in range(2):
                        b = i * 2 + e
                        pe.wait_ge(picked_in, b * 16 + 16)
                        pe.wait_ge(heavy_Tsb, b + FIRST)
                        for k in range(KH):
                            for j in range(2):
                                mm = pe.transpose(F0[:, (2 * k + j) * P:(2 * k + j + 1) * P],
                                                  picked[e][:, j, k * P:(k + 1) * P], ident[:, :])
                        mm.then_inc(heavy_T, 1)
                        pe.wait_ge(heavy_Tsb, b + 1 + FIRST)
                        for m in range(HEAVY // P):
                            if m >= 4:
                                pe.wait_ge(heavy_g, b * 8 + (m - 3))
                            for k in range(KH):
                                mm = pe.matmul(heavy_banks[m % 4][:, 0:ROUTED], w1h[:, k, m * P:(m + 1) * P], pickedT[:, k, :],
                                               start=(k == 0), stop=(k == KH - 1))
                            mm.then_inc(heavy_h, 1)
                        pe.wait_ge(heavy_g, b * 8 + 8)
                        pe.wait_ge(heavy_done, b + FIRST)
                        for j in range(2):
                            out = YB[:, j * DIM:(j + 1) * DIM]
                            for m in range(HEAVY // P):
                                pe.matmul(out, heavy_gT[:, m, j * P:(j + 1) * P], w2h[:, m, :], start=(j == 0 and m == 0),
                                          stop=False, skip_group_check=True)
                            mm = pe.matmul(out, ones16[:, :], bias3[:, B2_HEAVY, :], start=False, stop=(j == 1),
                                           skip_group_check=True)
                        mm.then_inc(heavy_o, 1)

            pe.wait_ge(keys_in, 32)
            pe.wait_ge(consts_in, 16)
            pe.wait_ge(set_ready, 5)
            for l in range(2):
                s = S[l]
                if l == 1:
                    ffn0()
                if l == 0:
                    keys_values(s, l)
                pe.wait_ge(s["k_low"], KH)
                transpose_h(s, 0)
                pe.wait_ge(attn_w_in[l], 16)
                for m in range(KH):
                    project_q(s, l, 0, m)
                transpose_h(s, 1)
                pe.wait_ge(consts16_in, 16)
                pe.wait_ge(s["k16_ready"], KH)
                pe.wait_ge(s["v_sb"], BATCH)
                for j in range(8):
                    max_scores(s, l, 0, True, 0, j)
                for m in range(KH):
                    project_q(s, l, 1, m)
                transpose_max(s, 0)
                with pe.Fori(0, BATCH - 1) as b:
                    for e in range(2):
                        chunk_step(s, l, b * 2 + e, e, b, True, True)
                for e in range(2):
                    chunk_step(s, l, CHUNKS - 2 + e, e, BATCH - 1, False, e == 0)
            pe.wait_ge(gate_in, 16)

            def transpose_rows(c, e):
                pe.wait_ge(G["copied"], c + 1)
                if not isinstance(c, int) or c >= 2:
                    pe.wait_ge(G["hT_sb"], c * 2 - 2)
                for k in range(KH):
                    for t in range(CHUNK_TILES):
                        mm = pe.transpose(rowsT_banks[e][k][:, t * P:(t + 1) * P], rows2[e][:, t, k * P:(k + 1) * P], ident[:, :])
                mm.then_inc(G["hT_ps"], 1)

            def group_sums(c, e):
                pe.wait_ge(G["hT_sb"], c * 2 + 2)
                if not isinstance(c, int) or c >= 2:
                    pe.wait_ge(G["sums_sb"], c - 1 + FIRST)
                for k in range(KH):
                    mm = pe.matmul(mid[e][:, :], conv_bd[:, k, :], rowsT2[e][:, k, :], start=(k == 0), stop=(k == KH - 1))
                mm.then_inc(G["sums_ps"], 1)

            transpose_rows(0, 0)
            transpose_rows(1, 1)
            group_sums(0, 0)
            with pe.Fori(1, CHUNKS // 2) as i:
                for e in range(2):
                    transpose_rows(i * 2 + e, e)
                    group_sums(i * 2 + e - 1, 1 - e)
            group_sums(CHUNKS - 1, 1)
            pe.wait_ge(gate_ready, 2)

            def prepare(t, e):
                pe.wait_ge(G["hs_ready"], t + 1)
                pe.wait_ge(G["hsT_sb"], t)
                for k in range(KH):
                    mm = pe.transpose(F0[:, k * P:(k + 1) * P], hs[e][:, k * P:(k + 1) * P], ident[:, :])
                mm.then_inc(G["hsT_ps"], 1)
                pe.wait_ge(G["acts_ready"], t + 1)
                if not (isinstance(t, int) and t == 0):
                    pe.wait_ge(G["exp_ready"], t * 2 - 2)
                pe.matmul(mid[e][:, :], acts[e], lin_bd[:, :], start=True, stop=False)
                pe.matmul(mid[e][:, :], ones16[:, :], bias3[:, SO_B:SO_B + 2, :].rearrange("p a d -> p (a d)"),
                          start=False, stop=True).then_inc(G["logit_ps"], 1)
                pe.wait_ge(G["hsT_sb"], t + 1)
                if not (isinstance(t, int) and t == 0):
                    pe.wait_ge(G["part_ready"], t * 3 - 3)
                for k in range(KH):
                    mm = pe.matmul(score[e][:, 0:DIM], hsT[e][:, k, :], gate_w[:, k, :], start=(k == 0), stop=(k == KH - 1))
                mm.then_inc(G["full_ps"], 1)

            def in_branch(t, e):
                pe.wait_ge(G["sparse_ready"], t + 1)
                pe.wait_ge(G["sparseT_sb"], t)
                for k in range(KH):
                    mm = pe.transpose(F1[:, k * P:(k + 1) * P], sparse[:, k * P:(k + 1) * P], ident[:, :])
                mm.then_inc(G["sparseT_ps"], 1)
                pe.wait_ge(G["sparseT_sb"], t + 1)
                if not (isinstance(t, int) and t == 0):
                    pe.wait_ge(G["in_scaled"], t - 1 + FIRST)
                for k in range(KH):
                    mm = pe.matmul(out_banks[e][:, 0:DIM], sparseT[:, k, :], gate_w[:, k, :], start=(k == 0), stop=(k == KH - 1))
                mm.then_inc(G["in_ps"], 1)

            def gate_tile(t, e, ahead=True):
                if ahead:
                    prepare(t + 1, 1 - e)
                if not (isinstance(t, int) and t == 0):
                    in_branch(t - 1, 1 - e)

            prepare(0, 0)
            for e in range(2):
                gate_tile(e, e)
            with pe.Fori(1, TILES // 2 - 1) as i:
                for e in range(2):
                    gate_tile(i * 2 + e, e)
            for e in range(2):
                gate_tile(TILES - 2 + e, e, e == 0)
            in_branch(TILES - 1, 1)


def host_arrays(inp):
    import numpy as np
    f = lambda a: np.ascontiguousarray(np.asarray(a))
    bf16_bits = lambda a: (np.ascontiguousarray(a, np.float32).view(np.uint32) >> 16).astype(np.uint16)
    r, col, feature, tile = np.arange(P), np.arange(512), np.arange(DIM), np.arange(TILES)[None, :]
    rows = lambda a: np.asarray(a).reshape(-1, P, np.asarray(a).shape[-1]).transpose(1, 0, 2).reshape(P, -1)
    cols = lambda a: np.asarray(a).reshape(-1, P).T
    pack = lambda *a: np.ascontiguousarray(np.concatenate(a, axis=1))
    d = {"x": f(inp["x"]).reshape(BATCH * TOKENS, DIM)}
    ctx = np.asarray(inp["ctx_1024"]).transpose(2, 0, 1).reshape(KH, P, BATCH, 1, KEYS).transpose(1, 0, 2, 3, 4)
    d["ctxT"] = np.ascontiguousarray(np.repeat(ctx, 2, axis=3)).reshape(P, -1)
    for l in range(2):
        d[f"kvqo{l}"] = pack(*(rows(np.asarray(inp[f"L{l}_xattn_W{w}"]).T) for w in "kvqo"))
    d["gates"] = np.stack([np.asarray(inp["g_xattn"])[0], np.asarray(inp["g_ffn"])[0],
                           np.asarray(inp["g_xattn"])[1], np.asarray(inp["g_ffn"])[1]])
    d["bias_gates"] = d["gates"][[0, 2, 1]].reshape(3, 1)
    d["bias_rows"] = np.stack([np.asarray(inp[n]) for n in (
        "L0_xattn_bo", "L1_xattn_bo", "L0_ffn_b2_light", "L0_ffn_b2_heavy", "L1_ffn_so_lin_b", "L1_ffn_si_lin_b")])
    d["bv1"], d["bias1"], d["token"] = f(inp["L1_xattn_bv"]), f(inp["L1_ffn_bias"]), f(inp["L0_ffn_routing_token"])
    outside = (BATCH * TOKENS + tile * P + r[:, None]).astype(np.float32)
    d["consts"] = pack(
        np.eye(P, dtype=np.float32),
        (r[:, None] // HEAD_DIM == col[None, :] // KEYS).astype(np.float32),
        (r[:, None] // KEYS == (feature[None, :] // HEAD_DIM) % 2).astype(np.float32),
        -outside, outside,
        cols(inp["L1_xattn_bq"]), cols(inp["L1_xattn_bk"]),
        cols(inp["L0_ffn_gamma_light"]), cols(inp["L0_ffn_gamma_heavy"]), cols(inp["L0_ffn_b1_light"]), cols(inp["L0_ffn_b1_heavy"]),
        np.stack([np.concatenate([np.asarray(inp[f"L1_ffn_{br}_{n}"]) for br in ("so", "si")])
                  for n in ("conv_b", "gamma", "beta")], 1))
    pair = np.arange(PAIRS)[None, :, None]
    d["consts16"] = bf16_bits(pack(
        np.eye(P),
        (-1.0 * (r[:, None, None] == 2 * pair + r[None, None, :] // KEYS)).reshape(P, -1),
        np.where(col[None, :] % KEYS > r[:, None], -1e30, 0.0),
        np.where(r[:, None] % KEYS > np.arange(KEYS)[None, :], -1e30, 0.0),
        r[:, None] < r[None, :]))
    d["light_w"] = pack(rows(inp["L0_ffn_w1_light"]), rows(inp["L0_ffn_w2_light"]))
    d["heavy_w"] = pack(rows(inp["L0_ffn_w1_heavy"]), rows(inp["L0_ffn_w2_heavy"]))
    conv, lin = np.zeros((DIM, P), np.float32), np.zeros((P, 2 * DIM), np.float32)
    for i, br in enumerate(("so", "si")):
        conv[feature, i * GROUPS + feature // 4] = np.asarray(inp[f"L1_ffn_{br}_conv_w"]).reshape(-1)
        lin[i * GROUPS:(i + 1) * GROUPS, i * DIM:(i + 1) * DIM] = np.asarray(inp[f"L1_ffn_{br}_lin_w"]).T
    d["gate_all"] = pack(rows(conv), rows(inp["L1_ffn_weight"]), lin)
    return d


def kernel(**inputs):
    import concourse.bacc as bacc
    from concourse.bass_utils import run_bass_kernel_spmd

    nc = bacc.Bacc("TRN2", target_bir_lowering=False, num_devices=1)
    arrays = host_arrays(inputs)
    A = {n: nc.dram_tensor(f"in_{n}", a.shape, mybir.dt.from_np(a.dtype), kind="ExternalInput").ap()
         for n, a in arrays.items()}
    A["out"] = nc.dram_tensor("out", (BATCH * TOKENS, DIM), F32, kind="ExternalOutput").ap()
    build(nc, A)
    r = run_bass_kernel_spmd(nc, [{f"in_{n}": a for n, a in arrays.items()}], core_ids=[0])
    return r.results[0]["out"].reshape(BATCH, TOKENS, DIM)
```
